# Optimizing a Trainium2 kernel written in Bass

```python
import numpy as np
import jax
import jax.numpy as jnp

def _softmax(x, axis=-1):
    return jax.nn.softmax(x, axis=axis)

def _gelu(x):
    return jax.nn.gelu(x, approximate=True)

def _silu(x):
    return jax.nn.silu(x)

def _sigmoid(x):
    return jax.nn.sigmoid(x)

def _layernorm(x, axis=-1, eps=1e-05):
    m = jnp.mean(x, axis=axis, keepdims=True)
    v = jnp.var(x, axis=axis, keepdims=True)
    return (x - m) / jnp.sqrt(v + eps)

def _scatter_add(tgt, idx, src, axis=0):
    return tgt.at[idx].add(src)

def _segment_sum(src, seg, n):
    return jax.ops.segment_sum(src, seg, n)
kernel_name = 'mk_gps_d2_gnn_r32_2c89e6'

def setup_inputs(seed: int=0):
    np.random.seed(seed)
    _w = jnp.asarray

    def _rec_inputs():
        import jax
        import jax.numpy as jnp
        _gk = jax.random.key(seed)
        x = -0.0002117 + 1 * jax.random.normal(jax.random.fold_in(_gk, 1), (3125, 256), jnp.float32)
        _s = jax.random.randint(jax.random.fold_in(_gk, 2), (25000,), 0, 3125, jnp.int32)
        _d = jax.random.randint(jax.random.fold_in(_gk, 3), (25000,), 0, 3125, jnp.int32)
        _loop = jnp.arange(3125, dtype=jnp.int32)
        src = jnp.concatenate([_s, _d, _loop])
        dst = jnp.concatenate([_d, _s, _loop])
        _o = jnp.argsort(dst, stable=True)
        src = src[_o]
        dst = dst[_o]
        edge_type_64 = jax.random.randint(jax.random.fold_in(_gk, 13), (53125,), 0, 64, jnp.int32)
        edge_weight = jax.random.uniform(jax.random.fold_in(_gk, 14), (53125,), jnp.float32, 0.0, 1)
        return (x, src, dst, edge_type_64, edge_weight)
    x, src, dst, edge_type_64, edge_weight = _rec_inputs()

    def _L0_gnn_setup():
        import jax, jax.numpy as jnp
        import numpy as np
        N_NODES = 3125
        N_EDGES = 100000
        IN_FEATS = 256
        OUT_FEATS = 256
        key = jax.random.key(seed)
        k1, k2, k3, k4, k5, k6 = jax.random.split(key, 6)
        features = jax.random.normal(k1, (N_NODES, IN_FEATS), dtype=jnp.float32)
        edge_src = jax.random.randint(k2, (N_EDGES,), 0, N_NODES, dtype=jnp.int64)
        edge_dst = jnp.sort(jax.random.randint(k3, (N_EDGES,), 0, N_NODES, dtype=jnp.int64))
        edge_weight = jax.random.uniform(k4, (N_EDGES,), dtype=jnp.float32)
        bound = 1.0 / np.sqrt(IN_FEATS)
        W = jax.random.uniform(k5, (OUT_FEATS, IN_FEATS), dtype=jnp.float32, minval=-bound, maxval=bound)
        b = jax.random.uniform(k6, (OUT_FEATS,), dtype=jnp.float32, minval=-bound, maxval=bound)
        return {'features': features, 'edge_src': edge_src, 'edge_dst': edge_dst, 'edge_weight': edge_weight, 'W': W, 'b': b}
    _L0_gnn_all = _L0_gnn_setup()
    _L0_gnn_in = {k: v for k, v in _L0_gnn_all.items() if k in ('W', 'b')}
    del _L0_gnn_all

    def _L0_mix_setup():
        import math
        import jax, jax.numpy as jnp
        import numpy as np
        EPS_DIV = 1e-07
        EPS_NORM = 1e-12

        def _l2_normalize(x, axis):
            n = jnp.sqrt(jnp.sum(x * x, axis=axis, keepdims=True))
            return x / jnp.maximum(n, EPS_NORM)
        key = jax.random.key(seed)
        ks = jax.random.split(key, 5)
        b, N, C = (8, 128, 256)
        x = jax.random.normal(ks[0], (b, N, C), dtype=jnp.float32)
        W_qkv = jax.random.normal(ks[1], (C, 3 * C), dtype=jnp.float32) * (1.0 / math.sqrt(C))
        b_qkv = jax.random.normal(ks[2], (3 * C,), dtype=jnp.float32) * 0.02
        W_out = jax.random.normal(ks[3], (C, C), dtype=jnp.float32) * (1.0 / math.sqrt(C))
        b_out = jax.random.normal(ks[4], (C,), dtype=jnp.float32) * 0.02
        return {'x': x, 'W_qkv': W_qkv, 'b_qkv': b_qkv, 'W_out': W_out, 'b_out': b_out}
    _L0_mix_all = _L0_mix_setup()
    _L0_mix_in = {k: v for k, v in _L0_mix_all.items() if k in ('W_qkv', 'b_qkv', 'W_out', 'b_out')}
    del _L0_mix_all

    def _L0_ffn_setup():
        import jax, jax.numpy as jnp
        import numpy as np
        B, K, D = (512, 16, 256)
        E = 32
        H = int(D * 0.25)
        key = jax.random.key(seed)
        ks = jax.random.split(key, 7)
        d_rs = D ** (-0.5)
        h_rs = H ** (-0.5)
        x = jax.random.normal(ks[0], (B, K, D), dtype=jnp.float32)
        router_w = jax.random.uniform(ks[1], (E, D), jnp.float32, -d_rs, d_rs)
        router_b = jax.random.uniform(ks[2], (E,), jnp.float32, -d_rs, d_rs)
        W1 = jax.random.uniform(ks[3], (E, D, H), jnp.float32, -h_rs, h_rs)
        b1 = jax.random.uniform(ks[4], (E, H), jnp.float32, -h_rs, h_rs)
        W2 = jax.random.uniform(ks[5], (E, H, D), jnp.float32, -d_rs, d_rs)
        b2 = jax.random.uniform(ks[6], (E, D), jnp.float32, -d_rs, d_rs)
        return {'x': x, 'router_w': router_w, 'router_b': router_b, 'W1': W1, 'b1': b1, 'W2': W2, 'b2': b2}
    _L0_ffn_all = _L0_ffn_setup()
    _L0_ffn_in = {k: v for k, v in _L0_ffn_all.items() if k in ('router_w', 'router_b', 'W1', 'b1', 'W2', 'b2')}
    del _L0_ffn_all

    def _L1_gnn_setup():
        import jax, jax.numpy as jnp
        import numpy as np
        N_NODES = 50000
        N_EDGES = 15625
        IN_DIM = 256
        HID = 64
        HEADS = 4
        N_REL = 64
        key = jax.random.key(seed)
        ks = jax.random.split(key, 16)
        s = 0.02
        return {'node_features': jax.random.normal(ks[0], (N_NODES, IN_DIM), jnp.float32), 'edge_index': jax.random.randint(ks[1], (2, N_EDGES), 0, N_NODES, jnp.int32), 'edge_relations': jax.random.randint(ks[2], (N_EDGES,), 0, N_REL, jnp.int32), 'query_emb': jax.random.normal(ks[3], (IN_DIM,), jnp.float32), 'Wq': jax.random.normal(ks[4], (IN_DIM, HID * HEADS), jnp.float32) * s, 'bq': jnp.zeros((HID * HEADS,), jnp.float32), 'Wk': jax.random.normal(ks[5], (IN_DIM, HID * HEADS), jnp.float32) * s, 'bk': jnp.zeros((HID * HEADS,), jnp.float32), 'Wv': jax.random.normal(ks[6], (IN_DIM, HID * HEADS), jnp.float32) * s, 'bv': jnp.zeros((HID * HEADS,), jnp.float32), 'rel_w': jax.random.normal(ks[7], (N_REL, HID), jnp.float32) * s, 'Wo': jax.random.normal(ks[8], (HID * HEADS, IN_DIM), jnp.float32) * s, 'bo': jnp.zeros((IN_DIM,), jnp.float32), 'gamma': jnp.ones((IN_DIM,), jnp.float32), 'beta': jnp.zeros((IN_DIM,), jnp.float32)}
    _L1_gnn_all = _L1_gnn_setup()
    _L1_gnn_in = {k: v for k, v in _L1_gnn_all.items() if k in ('query_emb', 'Wq', 'bq', 'Wk', 'bk', 'Wv', 'bv', 'rel_w', 'Wo', 'bo', 'gamma', 'beta')}
    del _L1_gnn_all

    def _L1_mix_setup():
        import jax, jax.numpy as jnp
        import numpy as np
        HEADS = 4
        DIM_HEAD = 32
        key = jax.random.key(seed)
        k1, k2, k3 = jax.random.split(key, 3)
        B, L, D = (16, 256, 256)
        hidden = HEADS * DIM_HEAD
        x = jax.random.normal(k1, (B, L, D), dtype=jnp.float32)
        W_qkv = jax.random.normal(k2, (D, 3 * hidden), dtype=jnp.float32) * D ** (-0.5)
        W_out = jax.random.normal(k3, (hidden, D), dtype=jnp.float32) * hidden ** (-0.5)
        b_out = jnp.zeros((D,), dtype=jnp.float32)
        return {'x': x, 'W_qkv': W_qkv, 'W_out': W_out, 'b_out': b_out}
    _L1_mix_all = _L1_mix_setup()
    _L1_mix_in = {k: v for k, v in _L1_mix_all.items() if k in ('W_qkv', 'W_out', 'b_out')}
    del _L1_mix_all

    def _L1_ffn_setup():
        import jax, jax.numpy as jnp
        import numpy as np
        B, N, D = (16, 128, 256)
        NUM_EXPERTS, TOP_K, HEADS = (4, 2, 4)
        N_EDGES = 32768
        LN_EPS = 1e-05

        def _layernorm(x, g, b):
            mu = x.mean(-1, keepdims=True)
            var = ((x - mu) ** 2).mean(-1, keepdims=True)
            return (x - mu) * jax.lax.rsqrt(var + LN_EPS) * g + b

        def _forward(x, edge_index, W_gat, att_src, att_dst, b_gat, ln_gamma, ln_beta, W1, b1, W2, b2):
            Bc, Nc, Dc = x.shape
            M = Bc * Nc
            x_flat = x.reshape(M, Dc)
            h = (x_flat @ W_gat).reshape(M, HEADS, NUM_EXPERTS)
            loops = jnp.arange(M, dtype=edge_index.dtype)
            src = jnp.concatenate([edge_index[0], loops])
            dst = jnp.concatenate([edge_index[1], loops])
            a_src = (h * att_src).sum(-1)
            a_dst = (h * att_dst).sum(-1)
            e = jax.nn.leaky_relu(a_src[src] + a_dst[dst], negative_slope=0.2)
            e_max = jax.ops.segment_max(e, dst, num_segments=M)
            ee = jnp.exp(e - e_max[dst])
            denom = jax.ops.segment_sum(ee, dst, num_segments=M)
            alpha = ee / (denom[dst] + 1e-16)
            msg = h[src] * alpha[:, :, None]
            agg = jax.ops.segment_sum(msg, dst, num_segments=M).reshape(M, HEADS * NUM_EXPERTS) + b_gat
            scores = _layernorm(agg, ln_gamma, ln_beta).reshape(M, HEADS, NUM_EXPERTS).mean(1)
            scores = scores.reshape(Bc, Nc, NUM_EXPERTS)
            topk_s, topk_i = jax.lax.top_k(scores, TOP_K)
            w = jax.nn.softmax(topk_s, axis=-1)
            out = jnp.zeros_like(x)
            for ei in range(NUM_EXPERTS):
                g = jnp.where(topk_i == ei, w, 0.0).sum(-1)
                hh = jax.nn.gelu(x @ W1[ei] + b1[ei], approximate=False)
                out = out + g[..., None] * (hh @ W2[ei] + b2[ei])
            return out
        key = jax.random.key(seed)
        ks = jax.random.split(key, 8)
        s = 0.05
        return {'x': jax.random.normal(ks[0], (B, N, D), jnp.float32), 'W_gat': jax.random.normal(ks[1], (D, HEADS * NUM_EXPERTS), jnp.float32) * s, 'att_src': jax.random.normal(ks[2], (HEADS, NUM_EXPERTS), jnp.float32) * s, 'att_dst': jax.random.normal(ks[3], (HEADS, NUM_EXPERTS), jnp.float32) * s, 'b_gat': jnp.zeros((HEADS * NUM_EXPERTS,), jnp.float32), 'ln_gamma': jnp.ones((HEADS * NUM_EXPERTS,), jnp.float32), 'ln_beta': jnp.zeros((HEADS * NUM_EXPERTS,), jnp.float32), 'W1': jax.random.normal(ks[4], (NUM_EXPERTS, D, 2 * D), jnp.float32) * s, 'b1': jnp.zeros((NUM_EXPERTS, 2 * D), jnp.float32), 'W2': jax.random.normal(ks[5], (NUM_EXPERTS, 2 * D, D), jnp.float32) * s, 'b2': jnp.zeros((NUM_EXPERTS, D), jnp.float32), 'edge_index': jax.random.randint(ks[6], (2, N_EDGES), 0, B * N, jnp.int32)}
    _L1_ffn_all = _L1_ffn_setup()
    _L1_ffn_in = {k: v for k, v in _L1_ffn_all.items() if k in ('W_gat', 'att_src', 'att_dst', 'b_gat', 'ln_gamma', 'ln_beta', 'W1', 'b1', 'W2', 'b2', 'edge_index')}
    del _L1_ffn_all
    return {'x': x, 'src': src, 'dst': dst, 'edge_type_64': edge_type_64, 'edge_weight': edge_weight, 'L0_gnn_W': _L0_gnn_in['W'], 'L0_gnn_b': _L0_gnn_in['b'], 'L0_mix_W_qkv': _L0_mix_in['W_qkv'], 'L0_mix_b_qkv': _L0_mix_in['b_qkv'], 'L0_mix_W_out': _L0_mix_in['W_out'], 'L0_mix_b_out': _L0_mix_in['b_out'], 'L0_ffn_router_w': _L0_ffn_in['router_w'], 'L0_ffn_router_b': _L0_ffn_in['router_b'], 'L0_ffn_W1': _L0_ffn_in['W1'], 'L0_ffn_b1': _L0_ffn_in['b1'], 'L0_ffn_W2': _L0_ffn_in['W2'], 'L0_ffn_b2': _L0_ffn_in['b2'], 'L1_gnn_query_emb': _L1_gnn_in['query_emb'], 'L1_gnn_Wq': _L1_gnn_in['Wq'], 'L1_gnn_bq': _L1_gnn_in['bq'], 'L1_gnn_Wk': _L1_gnn_in['Wk'], 'L1_gnn_bk': _L1_gnn_in['bk'], 'L1_gnn_Wv': _L1_gnn_in['Wv'], 'L1_gnn_bv': _L1_gnn_in['bv'], 'L1_gnn_rel_w': _L1_gnn_in['rel_w'], 'L1_gnn_Wo': _L1_gnn_in['Wo'], 'L1_gnn_bo': _L1_gnn_in['bo'], 'L1_gnn_gamma': _L1_gnn_in['gamma'], 'L1_gnn_beta': _L1_gnn_in['beta'], 'L1_mix_W_qkv': _L1_mix_in['W_qkv'], 'L1_mix_W_out': _L1_mix_in['W_out'], 'L1_mix_b_out': _L1_mix_in['b_out'], 'L1_ffn_W_gat': _L1_ffn_in['W_gat'], 'L1_ffn_att_src': _L1_ffn_in['att_src'], 'L1_ffn_att_dst': _L1_ffn_in['att_dst'], 'L1_ffn_b_gat': _L1_ffn_in['b_gat'], 'L1_ffn_ln_gamma': _L1_ffn_in['ln_gamma'], 'L1_ffn_ln_beta': _L1_ffn_in['ln_beta'], 'L1_ffn_W1': _L1_ffn_in['W1'], 'L1_ffn_b1': _L1_ffn_in['b1'], 'L1_ffn_W2': _L1_ffn_in['W2'], 'L1_ffn_b2': _L1_ffn_in['b2'], 'L1_ffn_edge_index': _L1_ffn_in['edge_index']}

def reference(x, src, dst, edge_type_64, edge_weight, L0_gnn_W, L0_gnn_b, L0_mix_W_qkv, L0_mix_b_qkv, L0_mix_W_out, L0_mix_b_out, L0_ffn_router_w, L0_ffn_router_b, L0_ffn_W1, L0_ffn_b1, L0_ffn_W2, L0_ffn_b2, L1_gnn_query_emb, L1_gnn_Wq, L1_gnn_bq, L1_gnn_Wk, L1_gnn_bk, L1_gnn_Wv, L1_gnn_bv, L1_gnn_rel_w, L1_gnn_Wo, L1_gnn_bo, L1_gnn_gamma, L1_gnn_beta, L1_mix_W_qkv, L1_mix_W_out, L1_mix_b_out, L1_ffn_W_gat, L1_ffn_att_src, L1_ffn_att_dst, L1_ffn_b_gat, L1_ffn_ln_gamma, L1_ffn_ln_beta, L1_ffn_W1, L1_ffn_b1, L1_ffn_W2, L1_ffn_b2, L1_ffn_edge_index):
    import jax
    import jax.numpy as jnp

    def _L0_gnn_ref(features, edge_src, edge_dst, edge_weight, W, b):
        import jax, jax.numpy as jnp
        import numpy as np
        N_NODES = 3125
        N_EDGES = 100000
        IN_FEATS = 256
        OUT_FEATS = 256
        msgs = features[edge_src] * edge_weight[:, None]
        agg = jax.ops.segment_sum(msgs, edge_dst, num_segments=N_NODES, indices_are_sorted=True)
        return jnp.einsum('ni,oi->no', agg, W) + b

    def _L0_mix_ref(x, W_qkv, b_qkv, W_out, b_out):
        import math
        import jax, jax.numpy as jnp
        import numpy as np
        EPS_DIV = 1e-07
        EPS_NORM = 1e-12

        def _l2_normalize(x, axis):
            n = jnp.sqrt(jnp.sum(x * x, axis=axis, keepdims=True))
            return x / jnp.maximum(n, EPS_NORM)
        b, N, C = x.shape
        qkv = x @ W_qkv + b_qkv
        q, k, v = jnp.split(qkv, 3, axis=2)
        q = q - jnp.mean(q, axis=2, keepdims=True)
        k = k - jnp.mean(k, axis=2, keepdims=True)
        q2 = q * q
        k2 = k * k
        q2s = jnp.sum(q2, axis=2, keepdims=True)
        k2s = jnp.sum(k2, axis=2, keepdims=True)
        k2 = _l2_normalize(k2 / (k2s + EPS_DIV), axis=-2)
        q2 = _l2_normalize(q2 / (q2s + EPS_DIV), axis=-1)
        kv = jnp.einsum('bnc,bnd->bcd', k2, v)
        t2 = jnp.einsum('bnc,bcd->bnd', q2, kv) / math.sqrt(N)
        attn = v + t2
        return attn @ W_out + b_out

    def _L0_ffn_ref(x, router_w, router_b, W1, b1, W2, b2):
        import jax, jax.numpy as jnp
        import numpy as np
        B, K, D = (512, 16, 256)
        E = 32
        H = int(D * 0.25)
        xf = x.reshape(-1, D)
        logits = xf @ router_w.T + router_b
        idx = jnp.argmax(logits, axis=-1)
        w1t = jnp.take(W1, idx, axis=0)
        h = jnp.einsum('nd,ndh->nh', xf, w1t) + jnp.take(b1, idx, axis=0)
        h = jax.nn.relu(h)
        w2t = jnp.take(W2, idx, axis=0)
        out = jnp.einsum('nh,nhd->nd', h, w2t) + jnp.take(b2, idx, axis=0)
        out = jax.nn.relu(out)
        return out.reshape(x.shape)

    def _L1_gnn_ref(node_features, edge_index, edge_relations, query_emb, Wq, bq, Wk, bk, Wv, bv, rel_w, Wo, bo, gamma, beta):
        import jax, jax.numpy as jnp
        import numpy as np
        N_NODES = 50000
        N_EDGES = 15625
        IN_DIM = 256
        HID = 64
        HEADS = 4
        N_REL = 64
        N = node_features.shape[0]
        D = rel_w.shape[1]
        H = Wq.shape[1] // D
        enh = node_features + 0.1 * query_emb[None, :]
        Q = (enh @ Wq + bq).reshape(N, H, D)
        K = (enh @ Wk + bk).reshape(N, H, D)
        V = (enh @ Wv + bv).reshape(N, H, D)
        src, dst = (edge_index[0], edge_index[1])
        rel = rel_w[edge_relations]
        mod_k = K[src] + 0.2 * rel[:, None, :]
        scores = jnp.einsum('ehd,ehd->eh', Q[dst], mod_k) / D ** 0.5
        seg_max = jax.ops.segment_max(scores, dst, num_segments=N)
        ex = jnp.exp(scores - seg_max[dst])
        denom = jax.ops.segment_sum(ex, dst, num_segments=N)
        w = ex / denom[dst]
        agg = jax.ops.segment_sum(w[:, :, None] * V[src], dst, num_segments=N)
        deg = jax.ops.segment_sum(jnp.ones((src.shape[0],), jnp.float32), dst, num_segments=N)
        msgs = jnp.where(deg[:, None, None] > 0, agg, V)
        out = msgs.reshape(N, H * D) @ Wo + bo
        x = out + node_features
        mu = jnp.mean(x, axis=-1, keepdims=True)
        var = jnp.var(x, axis=-1, keepdims=True)
        return (x - mu) / jnp.sqrt(var + 1e-05) * gamma + beta

    def _L1_mix_ref(x, W_qkv, W_out, b_out):
        import jax, jax.numpy as jnp
        import numpy as np
        HEADS = 4
        DIM_HEAD = 32
        B, L, D = x.shape
        scale = DIM_HEAD ** (-0.5)
        qkv = jnp.einsum('bld,df->blf', x, W_qkv)
        qkv = qkv.reshape(B, L, 3, HEADS, DIM_HEAD)
        q = jnp.transpose(qkv[:, :, 0], (0, 2, 1, 3)) * scale
        k = jax.nn.softmax(jnp.transpose(qkv[:, :, 1], (0, 2, 1, 3)), axis=2)
        v = jnp.transpose(qkv[:, :, 2], (0, 2, 1, 3))
        context = jnp.einsum('bhld,bhle->bhde', k, v)
        out = jnp.einsum('bhde,bhld->bhle', context, q)
        out = jnp.transpose(out, (0, 2, 1, 3)).reshape(B, L, HEADS * DIM_HEAD)
        return jnp.einsum('blf,fd->bld', out, W_out) + b_out

    def _L1_ffn_ref(x, W_gat, att_src, att_dst, b_gat, ln_gamma, ln_beta, W1, b1, W2, b2, edge_index):
        import jax, jax.numpy as jnp
        import numpy as np
        B, N, D = (16, 128, 256)
        NUM_EXPERTS, TOP_K, HEADS = (4, 2, 4)
        N_EDGES = 32768
        LN_EPS = 1e-05

        def _layernorm(x, g, b):
            mu = x.mean(-1, keepdims=True)
            var = ((x - mu) ** 2).mean(-1, keepdims=True)
            return (x - mu) * jax.lax.rsqrt(var + LN_EPS) * g + b

        def _forward(x, edge_index, W_gat, att_src, att_dst, b_gat, ln_gamma, ln_beta, W1, b1, W2, b2):
            Bc, Nc, Dc = x.shape
            M = Bc * Nc
            x_flat = x.reshape(M, Dc)
            h = (x_flat @ W_gat).reshape(M, HEADS, NUM_EXPERTS)
            loops = jnp.arange(M, dtype=edge_index.dtype)
            src = jnp.concatenate([edge_index[0], loops])
            dst = jnp.concatenate([edge_index[1], loops])
            a_src = (h * att_src).sum(-1)
            a_dst = (h * att_dst).sum(-1)
            e = jax.nn.leaky_relu(a_src[src] + a_dst[dst], negative_slope=0.2)
            e_max = jax.ops.segment_max(e, dst, num_segments=M)
            ee = jnp.exp(e - e_max[dst])
            denom = jax.ops.segment_sum(ee, dst, num_segments=M)
            alpha = ee / (denom[dst] + 1e-16)
            msg = h[src] * alpha[:, :, None]
            agg = jax.ops.segment_sum(msg, dst, num_segments=M).reshape(M, HEADS * NUM_EXPERTS) + b_gat
            scores = _layernorm(agg, ln_gamma, ln_beta).reshape(M, HEADS, NUM_EXPERTS).mean(1)
            scores = scores.reshape(Bc, Nc, NUM_EXPERTS)
            topk_s, topk_i = jax.lax.top_k(scores, TOP_K)
            w = jax.nn.softmax(topk_s, axis=-1)
            out = jnp.zeros_like(x)
            for ei in range(NUM_EXPERTS):
                g = jnp.where(topk_i == ei, w, 0.0).sum(-1)
                hh = jax.nn.gelu(x @ W1[ei] + b1[ei], approximate=False)
                out = out + g[..., None] * (hh @ W2[ei] + b2[ei])
            return out
        return _forward(x, edge_index, W_gat, att_src, att_dst, b_gat, ln_gamma, ln_beta, W1, b1, W2, b2)
    edge_index = jnp.stack([src, dst])
    xn = _layernorm(x, axis=-1)
    x = x + _L0_gnn_ref(xn, src, dst, edge_weight, L0_gnn_W, L0_gnn_b) + _L0_mix_ref(xn[None], L0_mix_W_qkv, L0_mix_b_qkv, L0_mix_W_out, L0_mix_b_out)[0]
    x = x + _L0_ffn_ref(_layernorm(x, axis=-1)[None], L0_ffn_router_w, L0_ffn_router_b, L0_ffn_W1, L0_ffn_b1, L0_ffn_W2, L0_ffn_b2)[0]
    xn = _layernorm(x, axis=-1)
    x = x + _L1_gnn_ref(xn, edge_index, edge_type_64, L1_gnn_query_emb, L1_gnn_Wq, L1_gnn_bq, L1_gnn_Wk, L1_gnn_bk, L1_gnn_Wv, L1_gnn_bv, L1_gnn_rel_w, L1_gnn_Wo, L1_gnn_bo, L1_gnn_gamma, L1_gnn_beta) + _L1_mix_ref(xn[None], L1_mix_W_qkv, L1_mix_W_out, L1_mix_b_out)[0]
    x = x + _L1_ffn_ref(_layernorm(x, axis=-1)[None], L1_ffn_W_gat, L1_ffn_att_src, L1_ffn_att_dst, L1_ffn_b_gat, L1_ffn_ln_gamma, L1_ffn_ln_beta, L1_ffn_W1, L1_ffn_b1, L1_ffn_W2, L1_ffn_b2, L1_ffn_edge_index)[0]
    return x

_drawn_inputs = setup_inputs


def setup_inputs(seed=0):
    import zlib

    import numpy as np

    out = dict(_drawn_inputs(seed))
    spreads = {'L1_gnn_bq': (0.0, 0.8),
     'L1_gnn_bk': (0.0, 2.0),
     'L1_gnn_bv': (0.0, 0.44),
     'L1_gnn_bo': (0.0, 0.269),
     'L1_gnn_gamma': (1.0, 0.2),
     'L1_gnn_beta': (0.0, 0.1),
     'L1_mix_b_out': (0.0, 0.1),
     'L1_ffn_b_gat': (0.0, 0.1),
     'L1_ffn_ln_gamma': (1.0, 0.2),
     'L1_ffn_ln_beta': (0.0, 0.273),
     'L1_ffn_b1': (0.0, 0.425),
     'L1_ffn_b2': (0.0, 0.323)}
    factors = {'L0_mix_b_out': 3.37,
     'L0_ffn_b1': 8.0,
     'L0_ffn_b2': 3.934,
     'L1_gnn_query_emb': 8.0,
     'L1_gnn_Wq': 8.0,
     'L1_gnn_Wk': 8.0,
     'L1_gnn_Wv': 4.19,
     'L1_gnn_rel_w': 41.391,
     'L1_gnn_Wo': 2.987,
     'L1_ffn_att_src': 4.125,
     'L1_ffn_att_dst': 6.142}
    for name, (base, spread) in spreads.items():
        noise = np.random.default_rng([zlib.crc32(name.encode()), seed]).standard_normal(out[name].shape)
        drawn = base * np.exp(spread * noise) if base else spread * noise
        out[name] = jnp.asarray(drawn.astype(out[name].dtype))
    for name, factor in factors.items():
        out[name] = (out[name] * factor).astype(out[name].dtype)
    return out
```

```python
from contextlib import ExitStack

import concourse.bass as bass
from concourse import mybir

F32 = mybir.dt.float32
BF16 = mybir.dt.bfloat16
I32 = mybir.dt.int32
U32 = mybir.dt.uint32
ALU = mybir.AluOpType
ACT = mybir.ActivationFunctionType
AX = mybir.AxisListType

D = 256
KC = D // 128
P = 125
N = 3125
NT = N // P
U = 5
E = 53125
T = E // P
G = 5
RING = 5
STEP = G * RING
ITERS = T // STEP
BIG = 1.0e30
EPS = 1e-5
NH = 4
HD = D // NH
NX = 32
HX = 64
NC0 = NX * HX // 128
LO = 128
HI = 25
GE = 32768
GT = GE // 128
GN = GE + N
GC = 288
GP = P * GC
GB = 16
NX1 = 4
HX1 = 512


def linker(eng, sem, base=0):
    count = [0]

    def link(ins):
        count[0] += 1
        ins.then_inc(sem, 1)
        eng.wait_ge(sem, base + count[0])

    return link


GATHER_SEMAPHORES = (
    [f"w0_got{g}" for g in range(RING)] + [f"w1_got{g}" for g in range(RING)] +
    [f"s1_got{g}" for g in range(RING)] + ["g0_fetched", "g1_fetched", "g1_dens_in", "so_sent0", "so_sent1",
                                           "so_loops_sent", "a1_got0", "a1_got1", "a1_fetched"])


class Scope:

    def __init__(self, nc, stack, tag):
        self.nc, self.stack, self.tag = nc, stack, tag

    def sb(self, name, shape, dt=F32):
        return self.stack.enter_context(self.nc.sbuf_tensor(f"{self.tag}_{name}", shape, dt))

    def ps(self, name, shape=(128, 512), dt=F32):
        return self.stack.enter_context(self.nc.psum_tensor(f"{self.tag}_p_{name}", list(shape), dt))

    def sem(self, name):
        return self.stack.enter_context(self.nc.semaphore(f"{self.tag}_{name}"))


def clear_semaphores(nc, io, S):
    with nc.Block() as block:

        @block.sync
        def _(sp):
            sp.sem_clear(range(S.first_semaphore, 256))


def load_and_count(nc, io, S):
    with ExitStack() as stack:
        c = Scope(nc, stack, "load")
        iota_lo = c.sb("iota_lo", [128, LO])
        iota_hi = c.sb("iota_hi", [128, HI])
        dst_lo = c.sb("dst_lo", [P, T], I32)
        dst_hi = c.sb("dst_hi", [P, T], I32)
        hot_lo = c.sb("hot_lo", [P, RING, G, LO], BF16)
        hot_hi = c.sb("hot_hi", [P, RING, G, HI], BF16)
        tri = c.sb("tri", [128, 128])
        deg = c.sb("deg", [128, HI])
        total = c.sb("total", [128, HI])
        upto = c.sb("upto", [128, HI])
        one_hi = c.sb("one_hi", [128, HI])
        last = c.sb("last", [128, HI])
        none = c.sb("none", [128, HI])
        last_i = c.sb("last_i", [128, HI], I32)
        first = c.sb("first", [P, 4], I32)
        firstf = c.sb("firstf", [P, 4])
        raw = c.sb("raw", [P, T], I32)
        p_deg = c.ps("deg")
        p_sum = c.ps("sum")
        loaded, made, ready, counted, freed = [c.sem(x) for x in ("loaded", "made", "ready", "counted", "freed")]
        dve, summed, stored, fetched, filled = [c.sem(x) for x in ("dve", "summed", "stored", "fetched", "filled")]
        hot_made = c.sem("hot_made")
        with nc.Block() as block:

            @block.sync
            def _(sp):
                sp.dma_start(S.dst[:, :], io["dst"].rearrange("(p t) -> p t", p=P)).then_inc(loaded, 16)
                sp.dma_start(S.src[:, :], io["src"].rearrange("(p t) -> p t", p=P)).then_inc(loaded, 16)
                sp.dma_start(raw[:, :], io["edge_type_64"].rearrange("(p t) -> p t", p=P)).then_inc(loaded, 16)
                sp.dma_start(S.w[:, :], io["edge_weight"].rearrange("(p t) -> p t", p=P)).then_inc(loaded, 16)
                sp.dma_start(S.x[:, :, :], io["x"].rearrange("(t p) d -> p t d", p=P)).then_inc(loaded, 16)
                sp.wait_ge(filled, 1)
                d2 = io["dst"].rearrange("(p t) -> p t", p=P)
                sp.dma_start(first[0:P - 1, 0:1], d2[1:P, 0:1]).then_inc(loaded, 16)
                sp.dma_start(first[1:P, 1:2], d2[0:P - 1, T - 1:T]).then_inc(loaded, 16)
                sp.wait_ge(stored, 1)
                sp.dma_start(io["last"].rearrange("(h l) -> l h", l=LO), last_i[:, :]).then_inc(fetched, 16)
                sp.wait_ge(fetched, 16)
                sp.dma_start(S.last[:, :], io["last"][0:N].rearrange("(t p) -> p t", p=P)).then_inc(fetched, 16)
                sp.wait_ge(fetched, 32)

            @block.gpsimd
            def _(pool):
                pool.iota(iota_lo[:, :], [[1, LO]], base=0, channel_multiplier=0,
                          allow_small_or_imprecise_dtypes=True).then_inc(made, 1)
                pool.iota(iota_hi[:, :], [[1, HI]], base=0, channel_multiplier=0,
                          allow_small_or_imprecise_dtypes=True).then_inc(made, 1)
                pool.iota(S.nodes[:, :], [[1, N]], base=0, channel_multiplier=0,
                          allow_small_or_imprecise_dtypes=True).then_inc(made, 1)
                pool.iota(S.row[:, :], [[0, 1]], base=0, channel_multiplier=1,
                          allow_small_or_imprecise_dtypes=True).then_inc(made, 1)
                pool.memset(S.ones[:, :], 1.0).then_inc(made, 1)
                pool.memset(S.ident[:, :], 0.0).then_inc(made, 1)
                pool.wait_ge(made, 6)
                pool.affine_select(out=S.ident[:, :], in_=S.ident[:, :], compare_op=ALU.not_equal, fill=1.0, base=0,
                                   pattern=[[-1, 128]], channel_multiplier=1).then_inc(made, 1)
                pool.affine_select(out=tri[:, :], in_=S.ones[:, :], compare_op=ALU.is_ge, fill=0.0, base=0,
                                   pattern=[[1, 128]], channel_multiplier=-1).then_inc(made, 1)
                pool.affine_select(out=S.below[:, :], in_=S.ones[:, :], compare_op=ALU.is_gt, fill=0.0, base=0,
                                   pattern=[[-1, 128]], channel_multiplier=1).then_inc(made, 1)

            @block.vector
            def _(v):
                link = linker(v, dve)
                link(v.memset(first[:, :], -1))
                v.sem_inc(filled, 1)
                v.memset(p_deg[:, 0:HI], 0.0)
                v.memset(one_hi[:, :], 1.0)
                v.memset(none[:, :], 3.0e7)
                v.wait_ge(loaded, 7 * 16)
                link(v.tensor_copy(S.typ[:, :], raw[:, :]))
                link(v.tensor_copy(S.dstf[:, :], S.dst[:, :]))
                link(v.tensor_copy(firstf[:, :], first[:, :]))
                link(v.memset(S.keep[:, :], 1.0))
                link(v.tensor_tensor(S.keep[:, 1:T], S.dstf[:, 1:T], S.dstf[:, 0:T - 1], ALU.is_equal))
                link(v.tensor_tensor(S.joins[:, 0:1], firstf[:, 1:2], S.dstf[:, 0:1], ALU.is_equal))
                link(v.tensor_tensor(S.joins[:, 1:2], firstf[:, 0:1], S.dstf[:, T - 1:T], ALU.is_equal))
                link(v.tensor_tensor(S.joins[:, 2:3], S.dstf[:, 0:1], S.dstf[:, T - 1:T], ALU.is_equal))
                link(v.scalar_tensor_tensor(S.goes_on[:, :], S.dstf[:, T - 1:T], 1.0, S.joins[:, 1:2],
                                            ALU.add, ALU.mult))
                link(v.tensor_scalar(S.goes_on[:, :], S.goes_on[:, :], 1.0, None, ALU.subtract))
                link(v.tensor_scalar(dst_lo[:, :], S.dst[:, :], LO - 1, None, ALU.bitwise_and))
                link(v.tensor_scalar(dst_hi[:, :], S.dst[:, :], 7, None, ALU.logical_shift_right))
                v.wait_ge(made, 9)
                v.sem_inc(freed, RING)
                with v.Fori(0, T - STEP + 1, STEP) as t0:
                    for g in range(RING):
                        t = t0 + g * G
                        v.wait_ge(freed, t0 // G + g + 1)
                        v.tensor_tensor(hot_lo[:, g, :, :],
                                        dst_lo[:, bass.ds(t, G)].unsqueeze(2).to_broadcast([P, G, LO]),
                                        iota_lo[0:P, :].unsqueeze(1).to_broadcast([P, G, LO]),
                                        ALU.is_equal).then_inc(hot_made, 1)
                        v.tensor_tensor(hot_hi[:, g, :, :],
                                        dst_hi[:, bass.ds(t, G)].unsqueeze(2).to_broadcast([P, G, HI]),
                                        iota_hi[0:P, :].unsqueeze(1).to_broadcast([P, G, HI]),
                                        ALU.is_equal).then_inc(hot_made, 1)
                v.wait_ge(counted, 1)
                link(v.tensor_copy(deg[:, :], p_deg[:, 0:HI]))
                v.sem_inc(ready, 1)
                v.wait_ge(summed, 1)
                link(v.tensor_copy(total[:, :], p_sum[:, 0:HI]))
                link(v.tensor_tensor_scan(upto[:, :], one_hi[:, :], total[:, :], 0.0, ALU.mult, ALU.add))
                link(v.tensor_tensor(upto[:, :], upto[:, :], total[:, :], ALU.subtract))
                link(v.tensor_tensor(upto[:, :], upto[:, :], p_sum[:, 64:64 + HI], ALU.add))
                link(v.tensor_scalar(last[:, :], deg[:, :], 0.0, None, ALU.is_equal))
                link(v.scalar_tensor_tensor(last[:, :], last[:, :], 3.0e7, upto[:, :], ALU.mult, ALU.add))
                link(v.tensor_scalar(last[:, :], last[:, :], 1.0, None, ALU.subtract))
                link(v.tensor_copy(last_i[:, :], last[:, :]))
                v.sem_inc(stored, 1)

            @block.tensor
            def _(pe):
                pe.wait_ge(dve, 1)
                with pe.Fori(0, T - STEP + 1, STEP) as t0:
                    for g in range(RING):
                        pe.wait_ge(hot_made, 2 * (t0 // G) + 2 * g + 2)
                        for j in range(G):
                            mm = pe.matmul(p_deg[:, 0:HI], hot_lo[:, g, j, :], hot_hi[:, g, j, :],
                                           start=False, stop=True, skip_group_check=True)
                        mm.then_inc(freed, 1)
                pe.wait_ge(freed, T // G + RING)
                pe.sem_inc(counted, 1)
                pe.wait_ge(ready, 1)
                pe.wait_ge(made, 9)
                pe.matmul(p_sum[:, 0:HI], S.ones[:, :], deg[:, :], start=True, stop=True)
                pe.matmul(p_sum[:, 64:64 + HI], tri[:, :], deg[:, :], start=True, stop=True).then_inc(summed, 1)


MV_STEPS = 8


def mean_and_var(link, stats, v, mean, var, diff, scale=1.0, eps=EPS):
    me, qe, mo, qo = [stats[:, :, i] for i in (1, 2, 4, 5)]
    link(v.tensor_tensor(mean, me, mo, ALU.add))
    link(v.tensor_scalar(mean, mean, 0.5, None, ALU.mult))
    link(v.tensor_tensor(diff, me, mo, ALU.subtract))
    link(v.scalar_tensor_tensor(diff, diff, 0.25, diff, ALU.mult, ALU.mult))
    link(v.tensor_tensor(var, qe, qo, ALU.add))
    link(v.tensor_scalar(var, var, 1.0 / D, None, ALU.mult))
    link(v.tensor_tensor(var, var, diff, ALU.add))
    link(v.tensor_scalar(var, var, scale, eps, ALU.mult, ALU.add))


def normalize(nc, tag, S, xn, xnT):
    with ExitStack() as stack:
        c = Scope(nc, stack, tag)
        stats = c.sb("stats", [P, NT, 6])
        mean = c.sb("mean", [P, NT])
        diff = c.sb("diff", [P, NT])
        var = c.sb("var", [P, NT])
        std = c.sb("std", [P, NT])
        rstd = c.sb("rstd", [P, NT])
        tile = c.sb("tile", [P, U, D])
        p_t = [c.ps(f"t{u}") for u in range(U)]
        counted, spread, rooted, normed, turned, copied = [
            c.sem(x) for x in ("counted", "spread", "rooted", "normed", "turned", "copied")]
        with nc.Block() as block:

            @block.vector
            def _(v):
                with v.Fori(0, NT) as t:
                    v.bn_stats(stats[:, bass.ds(t, 1), :].rearrange("p a b -> p (a b)"),
                               S.x[:, bass.ds(t, 1), :].rearrange("p a b -> p (a b)")).then_inc(counted, 1)
                v.wait_ge(counted, NT)
                mean_and_var(linker(v, spread), stats, v, mean[:, :], var[:, :], diff[:, :])
                v.wait_ge(rooted, 1)
                v.reciprocal(rstd[:, :], std[:, :]).then_inc(spread, 1)
                v.wait_ge(spread, MV_STEPS + 1)
                with v.Fori(0, NT - U + 1, U) as t0:
                    for u in range(U):
                        t = t0 + u
                        v.wait_ge(turned, t + 1)
                        v.tensor_scalar(tile[:, u, :], S.x[:, bass.ds(t, 1), :].rearrange("p a b -> p (a b)"),
                                        mean[:, bass.ds(t, 1)], rstd[:, bass.ds(t, 1)],
                                        ALU.subtract, ALU.mult).then_inc(normed, 1)
                        if xn is not None:
                            v.tensor_scalar(xn[:, bass.ds(t, 1), :].rearrange("p a b -> p (a b)"),
                                            S.x[:, bass.ds(t, 1), :].rearrange("p a b -> p (a b)"),
                                            mean[:, bass.ds(t, 1)], rstd[:, bass.ds(t, 1)],
                                            ALU.subtract, ALU.mult)

            @block.tensor
            def _(pe):
                pe.sem_inc(turned, U)
                with pe.Fori(0, NT - U + 1, U) as t0:
                    for u in range(U):
                        pe.wait_ge(normed, t0 + u + 1)
                        pe.wait_ge(copied, t0 + u + 1)
                        for k in range(KC):
                            mm = pe.transpose(p_t[u][:, k * P:(k + 1) * P], tile[:, u, k * 128:(k + 1) * 128],
                                              S.ident[0:P, 0:P])
                        mm.then_inc(turned, 1)

            @block.scalar
            def _(a):
                a.wait_ge(spread, MV_STEPS)
                a.activation(std[:, :], var[:, :], ACT.Sqrt).then_inc(rooted, 1)
                a.sem_inc(copied, U)
                with a.Fori(0, NT - U + 1, U) as t0:
                    for u in range(U):
                        a.wait_ge(turned, t0 + u + 1 + U)
                        a.activation(xnT[:, :, bass.ds((t0 + u) * P, P)],
                                     p_t[u][:, 0:KC * P].rearrange("q (k p) -> q k p", k=KC),
                                     ACT.Copy).then_inc(copied, 1)


class Walk:

    def __init__(self, c, S, tag):
        self.idx = c.sb("w_idx", [P, RING, G], I32)
        self.rows = c.sb("w_rows", [P, RING, G, D])
        self.sums = c.sb("w_sums", [P, RING, G, D])
        self.end = self.sums[:, RING - 1, G - 1, :]
        self.indexed, self.asked, self.walked, self.free = [
            c.sem(x) for x in ("w_indexed", "w_asked", "w_walked", "w_free")]
        self.got = [S.gathers[f"{tag}_got{g}"] for g in range(RING)]
        self.sent = [c.sem(f"w_sent{g}") for g in range(RING)]

    def gather(self, pool, table, src):
        with pool.Fori(0, T - STEP + 1, STEP) as t0:
            for g in range(RING):
                pool.wait_ge(self.free, t0 // G + g + 1)
                pool.tensor_copy(self.idx[:, g, :], src[:, bass.ds(t0 + g * G, G)]).then_inc(self.indexed, 1)
                pool.wait_ge(self.indexed, t0 // G + g + 1)
                pool.sem_inc(self.asked, 1)
                for j in range(G):
                    pool.indirect_dma_start(
                        out=self.rows[:, g, j, :], out_offset=None, in_=table,
                        in_offset=bass.IndirectOffsetOnAxis(ap=self.idx[:, g, j:j + 1], axis=0),
                    ).then_inc(self.got[g], 16)

    def walk(self, v, keep, weights, heads):
        link = linker(v, self.walked)
        link(v.memset(self.end, 0.0))
        v.sem_inc(self.free, RING)
        with v.Fori(0, T - STEP + 1, STEP) as t0:
            link = linker(v, self.walked, (t0 // STEP) * (RING * (G + 1)) + 1)
            for g in range(RING):
                v.wait_ge(self.got[g], (t0 // STEP) * (16 * G) + 16 * G)
                rows = self.rows[:, g, :, :]
                scale = weights[:, :, bass.ds(t0 + g * G, G)].rearrange("p h t -> p t h")
                link(v.tensor_tensor(rows.rearrange("p t (h d) -> p t h d", h=heads),
                                     rows.rearrange("p t (h d) -> p t h d", h=heads),
                                     scale.unsqueeze(3).to_broadcast([P, G, heads, D // heads]), ALU.mult))
                v.wait_ge(self.sent[g], (t0 // STEP) * 16 + 16)
                before = self.sums[:, (g - 1) % RING, G - 1, :]
                for j in range(G):
                    link(v.scalar_tensor_tensor(self.sums[:, g, j, :], before, keep[:, bass.ds(t0 + g * G + j, 1)],
                                                self.rows[:, g, j, :], ALU.mult, ALU.add))
                    before = self.sums[:, g, j, :]
                v.sem_inc(self.free, 1)

    def send(self, sp, sums):
        for g in range(RING):
            sp.sem_inc(self.sent[g], 16)
        view = sums.rearrange("(p t) d -> p t d", p=P)
        with sp.Fori(0, T - STEP + 1, STEP) as t0:
            for g in range(RING):
                sp.wait_ge(self.free, t0 // G + g + 1 + RING)
                sp.dma_start(view[:, bass.ds(t0 + g * G, G), :], self.sums[:, g, :, :]).then_inc(self.sent[g], 16)
        for g in range(RING):
            sp.wait_ge(self.sent[g], 16 * (ITERS + 1))


def collect(nc, c, io, S, walk, agg, fetched, before_fetch):
    carry = c.sb("carry", [P, N])
    p_c = [c.ps(f"carry{i}") for i in range(4)]
    ready, carried, added = [c.sem(x) for x in ("c_ready", "c_carried", "c_added")]
    with nc.Block() as block:

        @block.gpsimd
        def _(pool):
            before_fetch(pool)
            for t in range(NT):
                pool.indirect_dma_start(
                    out=agg[:, t, :], out_offset=None, in_=io["sums"],
                    in_offset=bass.IndirectOffsetOnAxis(ap=S.last[:, t:t + 1], axis=0),
                    bounds_check=E - 1, oob_is_err=False).then_inc(fetched, 16)

        @block.vector
        def _(v):
            v.tensor_scalar(carry[:, :], S.nodes[:, :], S.goes_on[:, 0:1], None, ALU.is_equal).then_inc(ready, 1)
            v.wait_ge(fetched, 16 * NT)
            for t in range(NT):
                v.wait_ge(carried, t + 1)
                v.tensor_tensor(agg[:, t, :], agg[:, t, :], p_c[t % 4][0:P, 0:D], ALU.add).then_inc(added, 1)
            v.wait_ge(added, NT)

        @block.tensor
        def _(pe):
            pe.wait_ge(ready, 1)
            for t in range(NT):
                if t >= 4:
                    pe.wait_ge(added, t - 3)
                pe.matmul(p_c[t % 4][0:P, 0:D], carry[:, t * P:(t + 1) * P], walk.end,
                          start=True, stop=True).then_inc(carried, 1)


def layer0_graph(nc, io, S):
    with ExitStack() as stack:
        c = Scope(nc, stack, "g0")
        kvT = c.sb("kvT", [128, KC, D])
        knorm = c.sb("knorm", [128, KC])
        q2T_stack = stack.enter_context(ExitStack())
        c2 = Scope(nc, q2T_stack, "m0")
        q2T = c2.sb("q2T", [128, KC, N])
        project0(nc, io, S, kvT, knorm, q2T)
        walk = Walk(c, S, "w0")
        mix0(nc, io, S, kvT, knorm, q2T, walk)
        agg = c.sb("agg", [P, NT, D])

        def clear(pool):
            pool.memset(agg[:, :, :], 0.0).then_inc(cleared, 1)
            pool.wait_ge(cleared, 1)

        cleared = c.sem("cleared")
        with ExitStack() as s3:
            collect(nc, Scope(nc, s3, "g0c"), io, S, walk, agg, S.gathers["g0_fetched"], clear)
        with nc.Block() as block:
            @block.vector
            def _(v):
                v.tensor_tensor(S.x[:, :, :], S.x[:, :, :], agg[:, :, :], ALU.add)


def project0(nc, io, S, kvT, knorm, q2T):
    W4 = 4 * D
    with ExitStack() as stack:
        c = Scope(nc, stack, "p0")
        w = c.sb("w", [128, KC, W4])
        bias = c.sb("bias", [1, W4])
        xT = c.sb("xT", [128, U, KC, P])
        qk = c.sb("qk", [P, U, 2 * D])
        vy = c.sb("vy", [P, U, 2 * D])
        sq = c.sb("sq", [P, U, 2 * D])
        ksq = c.sb("ksq", [P, U, D])
        junk = c.sb("junk", [P, D])
        stats = c.sb("stats", [P, 2 * U, 6])
        mean, diff, var, r, root, f = [c.sb(x, [P, 2 * U]) for x in ("mean", "diff", "var", "r", "root", "f")]
        ss = c.sb("ss", [P, U])
        p_qk = [c.ps(f"qk{i}") for i in range(2)]
        p_vy = [c.ps(f"vy{i}") for i in range(2)]
        p_t = [c.ps(f"t{i}") for i in range(2)]
        p_kv = c.ps("kv")
        p_ss = c.ps("ss")
        names = ("loaded", "cleared", "staged", "multiplied", "evacuated", "table_out", "dve", "centred",
                 "squared", "sum_ready", "rooted", "scaled", "turned", "copied", "pooled", "group")
        (loaded, cleared, staged, multiplied, evacuated, table_out, dve, centred, squared, sum_ready, rooted,
         scaled, turned, copied, pooled, group) = [c.sem(x) for x in names]
        with nc.Block() as block:

            @block.sync
            def _(sp):
                sp.dma_start(w[:, :, 0:3 * D], io["L0_mix_W_qkv"].rearrange("(k p) n -> p k n", p=128)).then_inc(loaded, 16)
                sp.dma_start(w[:, :, 3 * D:W4], io["L0_gnn_W"].rearrange("(k p) n -> p k n", p=128)).then_inc(loaded, 16)
                sp.wait_ge(cleared, 1)
                sp.dma_start(bias[0:1, 0:3 * D], io["L0_mix_b_qkv"].rearrange("(a n) -> a n", a=1)).then_inc(loaded, 16)
                sp.sem_inc(table_out, 16)
                table = io["table"].rearrange("(t p) d -> p t d", p=P)
                with sp.Fori(0, NT - U + 1, U) as t0:
                    sp.wait_ge(evacuated, t0 + U + 2)
                    sp.dma_start(table[:, bass.ds(t0, U), :], vy[:, :, D:2 * D]).then_inc(table_out, 16)
                sp.wait_ge(table_out, 16 * (NT // U + 1))

            @block.gpsimd
            def _(pool):
                pool.memset(bias[:, :], 0.0).then_inc(cleared, 1)
                with pool.Fori(0, NT - U + 1, U) as t0:
                    for u in range(U):
                        pool.wait_ge(multiplied, t0 + u + 1)
                        pool.tensor_copy(xT[:, u, :, :], S.xnT[:, :, bass.ds((t0 + u) * P, P)]).then_inc(staged, 1)

            @block.tensor
            def _(pe):
                pe.wait_ge(loaded, 3 * 16)
                pe.wait_ge(dve, 2)
                pe.sem_inc(multiplied, U)
                pe.sem_inc(group, 1)
                with pe.Fori(0, NT - U + 1, U) as t0:
                    for u in range(U):
                        pe.wait_ge(staged, t0 + u + 1)
                        pe.wait_ge(evacuated, t0 + u + (2 if u == 0 else 1))
                        for o, (p_o, lo) in enumerate(((p_qk, 0), (p_vy, 2 * D))):
                            for k in range(KC):
                                pe.matmul(p_o[u % 2][0:P, :], xT[:, u, k, :], w[:, k, lo:lo + 2 * D],
                                          start=(k == 0), stop=False)
                            mm = pe.matmul(p_o[u % 2][0:P, :], S.ones[0:1, 0:P], bias[0:1, lo:lo + 2 * D],
                                           start=False, stop=True)
                        mm.then_inc(multiplied, 1)
                    pe.wait_ge(scaled, t0 // U + 1)
                    for u in range(U):
                        pe.wait_ge(copied, t0 + u + (2 if u == 0 else 1))
                        for k in range(KC):
                            mm = pe.transpose(p_t[u % 2][:, k * P:(k + 1) * P], sq[:, u, k * 128:(k + 1) * 128],
                                              S.ident[0:P, 0:P])
                        mm.then_inc(turned, 1)
                        for k in range(KC):
                            pe.matmul(p_kv[:, k * D:(k + 1) * D], vy[:, u, k * 128:(k + 1) * 128],
                                      sq[:, u, D:2 * D], start=False, stop=True, skip_group_check=True)
                            mm = pe.matmul(p_ss[:, k:k + 1], ksq[:, u, k * 128:(k + 1) * 128], S.ones[0:P, 0:1],
                                           start=False, stop=True, skip_group_check=True)
                    mm.then_inc(group, 1)

            @block.scalar
            def _(a):
                a.sem_inc(evacuated, 2)
                a.sem_inc(copied, 2)
                with a.Fori(0, NT - U + 1, U) as t0:
                    a.wait_ge(group, t0 // U + 1)
                    a.wait_ge(table_out, 16 * (t0 // U) + 16)
                    for u in range(U):
                        a.wait_ge(multiplied, t0 + u + 1 + U)
                        a.activation(qk[:, u, :], p_qk[u % 2][0:P, :], ACT.Copy)
                        a.activation(vy[:, u, :], p_vy[u % 2][0:P, :], ACT.Copy).then_inc(evacuated, 1)
                    a.wait_ge(centred, t0 // U + 1)
                    for j in range(2 * U):
                        half = qk[:, j // 2, (j % 2) * D:(j % 2 + 1) * D]
                        a.activation(sq[:, j // 2, (j % 2) * D:(j % 2 + 1) * D], half, ACT.Square,
                                     bias=mean[:, j:j + 1]).then_inc(squared, 1)
                    a.wait_ge(sum_ready, t0 // U + 1)
                    a.activation(root[:, 0:U], ss[:, :], ACT.Sqrt).then_inc(rooted, 1)
                    for u in range(U):
                        a.wait_ge(turned, t0 + u + 1)
                        a.activation(q2T[:, :, bass.ds((t0 + u) * P, P)],
                                     p_t[u % 2][:, 0:KC * P].rearrange("q (k p) -> q k p", k=KC),
                                     ACT.Copy).then_inc(copied, 1)

            @block.vector
            def _(v):
                link = linker(v, dve)
                link(v.memset(p_kv[:, :], 0.0))
                link(v.memset(p_ss[:, :], 0.0))
                per = 2 * U + MV_STEPS + 2 + U + 4 + 2 * U + 1
                with v.Fori(0, NT - U + 1, U) as t0:
                    base = (t0 // U) * per + 2
                    link = linker(v, dve, base)
                    v.wait_ge(evacuated, t0 + U + 2)
                    for j in range(2 * U):
                        link(v.bn_stats(stats[:, j, :], qk[:, j // 2, (j % 2) * D:(j % 2 + 1) * D]))
                    mean_and_var(link, stats, v, mean[:, :], var[:, :], diff[:, :], float(D), 1e-7)
                    link(v.tensor_scalar(mean[:, :], mean[:, :], -1.0, None, ALU.mult))
                    link(v.reciprocal(r[:, :], var[:, :]))
                    v.sem_inc(centred, 1)
                    v.wait_ge(squared, (t0 // U) * (2 * U) + 2 * U)
                    for u in range(U):
                        link(v.tensor_tensor_reduce(junk[:, :], sq[:, u, 0:D], sq[:, u, 0:D], 1.0, 0.0,
                                                    ALU.mult, ALU.add, ss[:, u:u + 1]))
                    v.sem_inc(sum_ready, 1)
                    v.wait_ge(rooted, t0 // U + 1)
                    rq = r[:, 0:2 * U:2]
                    link(v.tensor_tensor(f[:, 0:U], root[:, 0:U], rq, ALU.mult))
                    link(v.tensor_scalar(f[:, 0:U], f[:, 0:U], 1e-12, None, ALU.max))
                    link(v.reciprocal(f[:, 0:U], f[:, 0:U]))
                    link(v.tensor_tensor(f[:, 0:U], f[:, 0:U], rq, ALU.mult))
                    for u in range(U):
                        link(v.tensor_scalar(sq[:, u, 0:D], sq[:, u, 0:D], f[:, u:u + 1], None, ALU.mult))
                        link(v.tensor_scalar(sq[:, u, D:2 * D], sq[:, u, D:2 * D], r[:, 2 * u + 1:2 * u + 2], None,
                                             ALU.mult))
                    link(v.tensor_tensor(ksq[:, :, :], sq[:, :, D:2 * D], sq[:, :, D:2 * D], ALU.mult))
                    v.sem_inc(scaled, 1)
                v.wait_ge(group, NT // U + 1)
                v.tensor_copy(kvT[:, :, :], p_kv[:, :].rearrange("p (k n) -> p k n", k=KC))
                v.tensor_copy(knorm[:, :], p_ss[:, 0:KC])


def mix0(nc, io, S, kvT, knorm, q2T, walk):
    with ExitStack() as stack:
        c = Scope(nc, stack, "x0")
        wout = c.sb("wout", [128, KC, D])
        wvT = c.sb("wvT", [128, KC, D])
        bv = c.sb("bv", [128, KC])
        rows = c.sb("rows", [1, 3, D])
        root = c.sb("root", [128, KC])
        kvw = c.sb("kvw", [128, KC, D])
        wvw = c.sb("wvw", [128, KC, D])
        xq = c.sb("xq", [128, 2, 2 * KC, P])
        p_a, p_b, p_r = c.ps("a"), c.ps("b"), c.ps("r")
        p_o = [c.ps(f"o{i}") for i in range(4)]
        names = ("loaded", "small", "rooted", "dve", "staged", "multiplied", "added")
        loaded, small, rooted, dve, staged, multiplied, added = [c.sem(x) for x in names]
        with nc.Block() as block:

            @block.sync
            def _(sp):
                sp.dma_start(wout[:, :, :], io["L0_mix_W_out"].rearrange("(k p) n -> p k n", p=128)).then_inc(loaded, 16)
                sp.dma_start(wvT[:, :, :], io["L0_mix_W_v_T"].rearrange("(k p) n -> p k n", p=128)).then_inc(loaded, 16)
                sp.dma_start(bv[:, :], io["L0_mix_b_qkv"][2 * D:3 * D].rearrange("(k p) -> p k", p=128)).then_inc(loaded, 16)
                sp.dma_start(rows[0:1, 0, :], io["L0_mix_b_out"].rearrange("(a n) -> a n", a=1)).then_inc(loaded, 16)
                sp.dma_start(rows[0:1, 1, :], io["L0_gnn_b"].rearrange("(a n) -> a n", a=1)).then_inc(loaded, 16)
                walk.send(sp, io["sums"])

            @block.gpsimd
            def _(pool):
                walk.gather(pool, io["table"], S.src)

            @block.tensor
            def _(pe):
                pe.wait_ge(loaded, 5 * 16)
                for m in range(KC):
                    for k in range(KC):
                        pe.matmul(p_a[:, m * D:(m + 1) * D], kvT[:, k, m * 128:(m + 1) * 128], wout[:, k, :],
                                  start=(k == 0), stop=(k == KC - 1))
                    for k in range(KC):
                        pe.matmul(p_b[:, m * D:(m + 1) * D], wvT[:, k, m * 128:(m + 1) * 128], wout[:, k, :],
                                  start=(k == 0), stop=(k == KC - 1))
                for k in range(KC):
                    mm = pe.matmul(p_r[0:1, 0:D], bv[:, k:k + 1], wout[:, k, :], start=(k == 0), stop=(k == KC - 1))
                mm.then_inc(small, 1)
                pe.wait_ge(dve, 8)
                for t in range(NT):
                    pe.wait_ge(staged, t + 1)
                    if t >= 4:
                        pe.wait_ge(added, t - 3)
                    o = p_o[t % 4][0:P, 0:D]
                    for k in range(KC):
                        pe.matmul(o, xq[:, t % 2, k, :], wvw[:, k, :], start=(k == 0), stop=False)
                        pe.matmul(o, xq[:, t % 2, KC + k, :], kvw[:, k, :], start=False, stop=False)
                    pe.matmul(o, S.ones[0:1, 0:P], rows[0:1, 2, :], start=False, stop=True).then_inc(multiplied, 1)

            @block.scalar
            def _(a):
                a.activation(root[:, :], knorm[:, :], ACT.Sqrt).then_inc(rooted, 1)
                for t in range(NT):
                    if t >= 2:
                        a.wait_ge(multiplied, t - 1)
                    a.activation(xq[:, t % 2, 0:KC, :], S.xnT[:, :, t * P:(t + 1) * P], ACT.Copy)
                    a.activation(xq[:, t % 2, KC:2 * KC, :], q2T[:, :, t * P:(t + 1) * P],
                                 ACT.Copy).then_inc(staged, 1)

            @block.vector
            def _(v):
                link = linker(v, dve)
                v.wait_ge(rooted, 1)
                link(v.tensor_scalar(root[:, :], root[:, :], 1e-12, None, ALU.max))
                link(v.reciprocal(root[:, :], root[:, :]))
                link(v.tensor_scalar(root[:, :], root[:, :], float(N) ** -0.5, None, ALU.mult))
                v.wait_ge(small, 1)
                for k in range(KC):
                    link(v.tensor_scalar(kvw[:, k, :], p_a[:, k * D:(k + 1) * D], root[:, k:k + 1], None, ALU.mult))
                link(v.tensor_copy(wvw[:, :, :], p_b[:, :].rearrange("p (k n) -> p k n", k=KC)))
                link(v.tensor_tensor(rows[0:1, 2, :], rows[0:1, 0, :], rows[0:1, 1, :], ALU.add))
                link(v.tensor_tensor(rows[0:1, 2, :], rows[0:1, 2, :], p_r[0:1, 0:D], ALU.add))
                for t in range(NT):
                    v.wait_ge(multiplied, t + 1)
                    v.tensor_tensor(S.x[:, t, :], S.x[:, t, :], p_o[t % 4][0:P, 0:D], ALU.add).then_inc(added, 1)
                walk.walk(v, S.keep, S.w[:, :].unsqueeze(1), 1)


def layer0_experts(nc, io, S):
    with ExitStack() as stack:
        c = Scope(nc, stack, "e0")
        hot = c.sb("hot", [P, NT, NX])
        hotT = c.sb("hotT", [NX, N])
        off = c.sb("off", [NX, N], BF16)
        route0(nc, io, S, hot, hotT, off)
        experts0(nc, io, S, hotT, off)


def route0(nc, io, S, hot, hotT, off):
    with ExitStack() as stack:
        c = Scope(nc, stack, "r0")
        rw = c.sb("rw", [128, KC, NX])
        rb = c.sb("rb", [1, NX])
        logits = c.sb("logits", [P, NT, NX])
        order = c.sb("order", [P, NX])
        top = c.sb("top", [P, NT])
        half = 512 // NX
        p_l = [c.ps(f"l{i}") for i in range(2)]
        p_t = [c.ps(f"t{i}") for i in range(2)]
        loaded, made, routed, dve, turned, copied = [
            c.sem(x) for x in ("loaded", "made", "routed", "dve", "turned", "copied")]
        with nc.Block() as block:

            @block.sync
            def _(sp):
                sp.dma_start(rw[:, :, :], io["L0_ffn_router_w"].rearrange("(k p) n -> p k n", p=128)).then_inc(loaded, 16)
                sp.dma_start(rb[:, :], io["L0_ffn_router_b"].rearrange("(a n) -> a n", a=1)).then_inc(loaded, 16)

            @block.gpsimd
            def _(pool):
                pool.iota(order[:, :], [[-1, NX]], base=NX, channel_multiplier=0,
                          allow_small_or_imprecise_dtypes=True).then_inc(made, 1)

            @block.tensor
            def _(pe):
                pe.wait_ge(loaded, 32)
                for t in range(NT):
                    o = p_l[t // half][0:P, (t % half) * NX:(t % half + 1) * NX]
                    for k in range(KC):
                        pe.matmul(o, S.xnT[:, k, t * P:(t + 1) * P], rw[:, k, :], start=(k == 0), stop=False)
                    mm = pe.matmul(o, S.ones[0:1, 0:P], rb[0:1, :], start=False, stop=True)
                mm.then_inc(routed, 1)
                pe.wait_ge(dve, 7)
                for t in range(NT):
                    if t >= 2:
                        pe.wait_ge(copied, t - 1)
                    pe.transpose(p_t[t % 2][0:NX, 0:P], hot[:, t, :], S.ident[0:P, 0:P]).then_inc(turned, 1)

            @block.scalar
            def _(a):
                for t in range(NT):
                    a.wait_ge(turned, t + 1)
                    a.activation(hotT[:, t * P:(t + 1) * P], p_t[t % 2][0:NX, 0:P], ACT.Copy).then_inc(copied, 1)

            @block.vector
            def _(v):
                link = linker(v, dve)
                v.wait_ge(routed, 1)
                v.wait_ge(made, 1)
                link(v.tensor_copy(logits[:, 0:half, :], p_l[0][0:P, 0:half * NX].rearrange("p (t e) -> p t e", e=NX)))
                link(v.tensor_copy(logits[:, half:NT, :],
                                   p_l[1][0:P, 0:(NT - half) * NX].rearrange("p (t e) -> p t e", e=NX)))
                ranked = order[:, :].unsqueeze(1).to_broadcast([P, NT, NX])
                link(v.tensor_reduce(top[:, :], logits[:, :, :], AX.X, ALU.max))
                link(v.tensor_tensor(hot[:, :, :], logits[:, :, :], top[:, :].unsqueeze(2).to_broadcast([P, NT, NX]),
                                     ALU.is_equal))
                link(v.tensor_tensor(hot[:, :, :], hot[:, :, :], ranked, ALU.mult))
                link(v.tensor_reduce(top[:, :], hot[:, :, :], AX.X, ALU.max))
                link(v.tensor_tensor(hot[:, :, :], ranked, top[:, :].unsqueeze(2).to_broadcast([P, NT, NX]),
                                     ALU.is_equal))
                v.wait_ge(copied, NT)
                link(v.tensor_scalar(off[:, :], hotT[:, :], 1.0, BIG, ALU.subtract, ALU.mult))


def experts0(nc, io, S, hotT, off):
    B = U * P
    CUT = ((0, 3 * P, 0), (3 * P, B, 512))
    NB = NT // U
    with ExitStack() as stack:
        c = Scope(nc, stack, "f0")
        w1 = c.sb("w1", [128, KC, NX * HX])
        w2 = c.sb("w2", [128, NC0, D])
        b1 = c.sb("b1", [128, NC0])
        b2 = c.sb("b2", [NX, D])
        sel = c.sb("sel", [NX, NC0, 2, HX], BF16)
        hot = c.sb("hot", [NX, B])
        hid = c.sb("hid", [128, 2, B])
        p_h = [c.ps(f"h{i}", (128, 1024)) for i in range(2)]
        p_o = c.ps("o", (128, 1536))
        names = ("loaded", "made", "hidden", "active", "staged", "done", "added")
        loaded, made, hidden, active, staged, done, added = [c.sem(x) for x in names]
        with nc.Block() as block:

            @block.sync
            def _(sp):
                sp.dma_start(w1[:, :, :], io["L0_ffn_W1"].rearrange("(k p) n -> p k n", p=128)).then_inc(loaded, 16)
                sp.dma_start(w2[:, :, :], io["L0_ffn_W2"].rearrange("(c p) n -> p c n", p=128)).then_inc(loaded, 16)
                sp.dma_start(b1[:, :], io["L0_ffn_b1"]).then_inc(loaded, 16)
                sp.dma_start(b2[:, :], io["L0_ffn_b2"]).then_inc(loaded, 16)

            @block.gpsimd
            def _(pool):
                pool.memset(sel[:, :, :, :], 0.0).then_inc(made, 1)
                pool.wait_ge(made, 1)
                pool.affine_select(out=sel[:, :, :, :], in_=sel[:, :, :, :], compare_op=ALU.not_equal, fill=1.0,
                                   base=0, pattern=[[-2, NC0], [-1, 2], [0, HX]], channel_multiplier=1).then_inc(made, 1)

            @block.tensor
            def _(pe):
                pe.wait_ge(loaded, 4 * 16)
                pe.wait_ge(made, 2)
                with pe.Fori(0, NT - U + 1, U) as t0:
                    n0 = t0 * P

                    def make_hidden(ch):
                        pe.wait_ge(active, (t0 // U) * NC0 + ch + 1)
                        for lo, hi, at in CUT:
                            o = p_h[ch % 2][:, at:at + hi - lo]
                            for k in range(KC):
                                pe.matmul(o, w1[:, k, ch * 128:(ch + 1) * 128], S.xnT[:, k, bass.ds(n0 + lo, hi - lo)],
                                          start=(k == 0), stop=False)
                            mm = pe.matmul(o, sel[:, ch, :, :].rearrange("e a h -> e (a h)"),
                                           off[:, bass.ds(n0 + lo, hi - lo)], start=False, stop=True)
                        mm.then_inc(hidden, 1)

                    def add_output(ch):
                        pe.wait_ge(active, (t0 // U) * NC0 + ch + 3)
                        for u in range(U):
                            mm = pe.matmul(p_o[0:P, u * D:(u + 1) * D], hid[:, ch % 2, u * P:(u + 1) * P],
                                           w2[:, ch, :], start=False, stop=(ch == NC0 - 1), skip_group_check=True)
                        mm.then_inc(done, 1)

                    make_hidden(0)
                    pe.wait_ge(staged, t0 // U + 1)
                    for u in range(U):
                        pe.matmul(p_o[0:P, u * D:(u + 1) * D], hot[:, u * P:(u + 1) * P], b2[:, :],
                                  start=False, stop=False, skip_group_check=True)
                    for ch in range(NC0):
                        if ch + 1 < NC0:
                            make_hidden(ch + 1)
                        add_output(ch)

            @block.scalar
            def _(a):
                a.wait_ge(loaded, 4 * 16)
                a.sem_inc(active, 2)
                a.sem_inc(done, 2)
                with a.Fori(0, NT - U + 1, U) as t0:
                    for ch in range(NC0):
                        a.wait_ge(hidden, (t0 // U) * NC0 + ch + 1)
                        a.wait_ge(done, (t0 // U) * NC0 + ch + 1)
                        for lo, hi, at in CUT:
                            ins = a.activation(hid[:, ch % 2, lo:hi], p_h[ch % 2][:, at:at + hi - lo], ACT.Relu,
                                               bias=b1[:, ch:ch + 1])
                        ins.then_inc(active, 1)

            @block.vector
            def _(v):
                v.sem_inc(added, 1)
                with v.Fori(0, NT - U + 1, U) as t0:
                    v.wait_ge(added, t0 + 1)
                    v.memset(p_o[0:P, 0:U * D], 0.0)
                    v.tensor_copy(hot[:, :], hotT[:, bass.ds(t0 * P, B)]).then_inc(staged, 1)
                    v.wait_ge(done, (t0 // U) * NC0 + NC0 + 2)
                    for u in range(U):
                        xt = S.x[:, bass.ds(t0 + u, 1), :].rearrange("p a b -> p (a b)")
                        v.scalar_tensor_tensor(xt, p_o[0:P, u * D:(u + 1) * D], 0.0, xt,
                                               ALU.max, ALU.add).then_inc(added, 1)


def segment_scan(nc, tag, S, out, src, keep, joins, cols, op, reverse=False):
    C = src.shape[1]
    add = op == ALU.add
    combine = ALU.mult if add else ALU.add
    zero = 0.0 if add else -BIG
    with ExitStack() as stack:
        c = Scope(nc, stack, tag)
        gate = c.sb("gate", [P, cols + 1])
        ends = c.sb("ends", [P, C])
        through = c.sb("through", [P, C])
        enters = c.sb("enters", [P, 1])
        endsT = c.sb("endsT", [C, P])
        throughT = c.sb("throughT", [C, P])
        chain = c.sb("chain", [C, P])
        shifted = c.sb("shifted", [C, P])
        begin = c.sb("begin", [P, C])
        p_a, p_b, p_c = c.ps("a"), c.ps("b"), c.ps("c")
        dve, pe_done = c.sem("dve"), c.sem("turned")

        def turned(ap):
            return ap[:, ::-1] if reverse else ap

        with nc.Block() as block:

            @block.vector
            def _(v):
                link = linker(v, dve)
                link(v.memset(gate[:, cols:cols + 1], 1.0))
                link(v.tensor_copy(gate[:, 0:cols], keep))
                join = joins[:, 1:2] if reverse else joins[:, 0:1]
                link(v.tensor_tensor(through[:, 0:1], join, joins[:, 2:3], ALU.mult))
                link(v.tensor_copy(enters[:, :], join))
                if not add:
                    for flag in (gate[:, :], through[:, 0:1], enters[:, :]):
                        link(v.tensor_scalar(flag, flag, 1.0, BIG, ALU.subtract, ALU.mult))
                if C > 1:
                    link(v.tensor_copy(through[:, 1:C], through[:, 0:1].to_broadcast([P, C - 1])))
                gates = turned(gate[:, 1:cols + 1] if reverse else gate[:, 0:cols])

                def scan(begins):
                    for ch in range(C):
                        ins = v.tensor_tensor_scan(turned(out[:, ch, :]), gates, turned(src[:, ch, :]), begins(ch),
                                                   combine, op)
                    link(ins)

                scan(lambda ch: zero)
                at = 0 if reverse else cols - 1
                link(v.tensor_copy(ends[:, :], out[:, :, at]))
                v.wait_ge(pe_done, 1)
                link(v.tensor_copy(endsT[:, :], p_a[0:C, 0:P]))
                link(v.tensor_copy(throughT[:, :], p_b[0:C, 0:P]))
                link(v.tensor_tensor_scan(turned(chain[:, :]), turned(throughT[:, :]), turned(endsT[:, :]), zero,
                                          combine, op))
                link(v.memset(shifted[:, :], zero))
                if reverse:
                    link(v.tensor_copy(shifted[:, 0:P - 1], chain[:, 1:P]))
                else:
                    link(v.tensor_copy(shifted[:, 1:P], chain[:, 0:P - 1]))
                v.sem_inc(pe_done, 1)
                v.wait_ge(pe_done, 3)
                link(v.tensor_scalar(begin[:, :], p_c[0:P, 0:C], enters[:, 0:1], None, combine))
                scan(lambda ch: begin[:, ch:ch + 1])

            @block.tensor
            def _(pe):
                pe.wait_ge(dve, 5 + (0 if add else 3) + (1 if C > 1 else 0) + 1)
                pe.transpose(p_a[0:C, 0:P], ends[:, :], S.ident[0:P, 0:P])
                pe.transpose(p_b[0:C, 0:P], through[:, :], S.ident[0:P, 0:P]).then_inc(pe_done, 1)
                pe.wait_ge(pe_done, 2)
                pe.transpose(p_c[0:P, 0:C], shifted[:, :], S.ident[0:C, 0:C]).then_inc(pe_done, 1)


def layer1_graph(nc, io, S):
    with ExitStack() as stack:
        c = Scope(nc, stack, "g1")
        agg = c.sb("agg", [P, NT, D])
        weight = c.sb("weight", [P, NH, T])
        xn = c.sb("xn", [P, NT, D])
        normalize(nc, "n2", S, xn, S.xnT)
        project1(nc, io, S, agg)
        mix1(nc, io, S)
        scores1(nc, io, S, weight)
        den = softmax1(nc, io, S, c, weight)
        with ExitStack() as s3:
            cw = Scope(nc, s3, "w1")
            walk = Walk(cw, S, "w1")
            with nc.Block() as block:
                @block.sync
                def _(sp):
                    walk.send(sp, io["sums"])

                @block.gpsimd
                def _(pool):
                    walk.gather(pool, io["values"], S.src)

                @block.vector
                def _(v):
                    walk.walk(v, S.keep, weight[:, :, :], NH)

            def ones_first(pool):
                pool.memset(den[:, :, :], 1.0).then_inc(ready, 1)
                pool.wait_ge(ready, 1)
                for t in range(NT):
                    pool.indirect_dma_start(
                        out=den[:, t, :], out_offset=None, in_=io["dens"],
                        in_offset=bass.IndirectOffsetOnAxis(ap=S.last[:, t:t + 1], axis=0),
                        bounds_check=E - 1, oob_is_err=False).then_inc(dens_in, 16)
                pool.wait_ge(dens_in, 16 * NT)

            ready, dens_in = cw.sem("ready"), S.gathers["g1_dens_in"]
            collect(nc, cw, io, S, walk, agg, S.gathers["g1_fetched"], ones_first)
        finish1(nc, io, S, agg, den, xn)


def project1(nc, io, S, agg):
    with ExitStack() as stack:
        c = Scope(nc, stack, "p1")
        w = c.sb("w", [128, KC, 3 * D])
        query = c.sb("query", [128, KC])
        bias = c.sb("bias", [1, 3 * D])
        qk = c.sb("qk", [P, U, 2 * D])
        p_qk = [c.ps(f"qk{i}") for i in range(3)]
        p_v = [c.ps(f"v{i}") for i in range(3)]
        names = ("loaded", "biased", "multiplied", "evacuated", "v_out", "out", "v_sent", "dve")
        loaded, biased, multiplied, evacuated, v_out, out, v_sent, dve = [c.sem(x) for x in names]
        with nc.Block() as block:

            @block.sync
            def _(sp):
                for i, n in enumerate("qkv"):
                    sp.dma_start(w[:, :, i * D:(i + 1) * D],
                                 io[f"L1_gnn_W{n}"].rearrange("(k p) n -> p k n", p=128)).then_inc(loaded, 16)
                    sp.dma_start(bias[0:1, i * D:(i + 1) * D],
                                 io[f"L1_gnn_b{n}"].rearrange("(a n) -> a n", a=1)).then_inc(loaded, 16)
                sp.dma_start(query[:, :], io["L1_gnn_query_emb"].rearrange("(k p) -> p k", p=128)).then_inc(loaded, 16)
                for g in range(NT // U):
                    sp.wait_ge(evacuated, U * (g + 1))
                    for i, n in enumerate(("queries", "keys")):
                        sp.dma_start(io[n].rearrange("(t p) d -> p t d", p=P)[:, g * U:(g + 1) * U, :],
                                     qk[:, :, i * D:(i + 1) * D]).then_inc(out, 16)
                    sp.wait_ge(v_out, U * (g + 1))
                    sp.dma_start(io["values"].rearrange("(t p) d -> p t d", p=P)[:, g * U:(g + 1) * U, :],
                                 agg[:, g * U:(g + 1) * U, :]).then_inc(v_sent, 16)
                sp.wait_ge(out, 32 * (NT // U))
                sp.wait_ge(v_sent, 16 * (NT // U))

            @block.tensor
            def _(pe):
                pe.wait_ge(loaded, 7 * 16)
                for lo, hi, o in ((0, 2 * D, p_qk[0]), (2 * D, 3 * D, p_v[0])):
                    for k in range(KC):
                        mm = pe.matmul(o[0:1, 0:hi - lo], query[:, k:k + 1], w[:, k, lo:hi],
                                       start=(k == 0), stop=(k == KC - 1))
                mm.then_inc(biased, 1)
                pe.wait_ge(dve, 2)
                for t in range(NT):
                    if t >= 3:
                        pe.wait_ge(evacuated, t - 2)
                        pe.wait_ge(v_out, t - 2)
                    for lo, hi, o in ((0, 2 * D, p_qk[t % 3]), (2 * D, 3 * D, p_v[t % 3])):
                        for k in range(KC):
                            pe.matmul(o[0:P, 0:hi - lo], S.xnT[:, k, t * P:(t + 1) * P], w[:, k, lo:hi],
                                      start=(k == 0), stop=False)
                        mm = pe.matmul(o[0:P, 0:hi - lo], S.ones[0:1, 0:P], bias[0:1, lo:hi], start=False, stop=True)
                    mm.then_inc(multiplied, 1)

            @block.scalar
            def _(a):
                for t in range(NT):
                    a.wait_ge(multiplied, t + 1)
                    if t >= U and t % U == 0:
                        a.wait_ge(out, 32 * (t // U))
                    a.activation(qk[:, t % U, :], p_qk[t % 3][0:P, :], ACT.Copy).then_inc(evacuated, 1)

            @block.vector
            def _(v):
                v.wait_ge(biased, 1)
                v.scalar_tensor_tensor(bias[0:1, 0:2 * D], p_qk[0][0:1, :], 0.1, bias[0:1, 0:2 * D],
                                       ALU.mult, ALU.add).then_inc(dve, 1)
                v.scalar_tensor_tensor(bias[0:1, 2 * D:3 * D], p_v[0][0:1, 0:D], 0.1, bias[0:1, 2 * D:3 * D],
                                       ALU.mult, ALU.add).then_inc(dve, 1)
                for t in range(NT):
                    v.wait_ge(multiplied, t + 1)
                    v.tensor_copy(agg[:, t, :], p_v[t % 3][0:P, 0:D]).then_inc(v_out, 1)


def mix1(nc, io, S):
    W = 128
    HW = 32
    PIECES = [(n, min(512, N - n)) for n in range(0, N, 512)]
    with ExitStack() as stack:
        c = Scope(nc, stack, "x1")
        w = c.sb("w", [128, KC, 3 * W])
        wqT = c.sb("wqT", [W, D])
        wout = c.sb("wout", [W, D])
        bout = c.sb("bout", [1, D])
        kT = c.sb("kT", [W, N])
        top = c.sb("top", [W, 8])
        total = c.sb("total", [W, 8])
        norm = c.sb("norm", [W, 2])
        kv = c.sb("kv", [P, 2, 2 * W])
        ctx = c.sb("ctx", [W, W])
        cw = c.sb("cw", [W, D])
        fold = c.sb("fold", [128, KC, D])
        names = ("loaded", "keys", "topped", "raised", "turned", "copied", "context", "dve", "small", "mult", "added")
        loaded, keys, topped, raised, turned, copied, context, dve, small, mult, added = [c.sem(x) for x in names]
        with nc.Block() as block, ExitStack() as ps:
            p_k = [ps.enter_context(nc.psum_tensor(f"x1_p_k{i}", [128, 512], F32)) for i in range(len(PIECES))]
            p_c = ps.enter_context(nc.psum_tensor("x1_p_c", [128, 512], F32))
            p_kv = p_k[0:2]
            p_w, p_f = p_k[2], p_k[3]
            p_o = p_k[4:7]

            @block.sync
            def _(sp):
                sp.dma_start(w[:, :, :], io["L1_mix_W_qkv"].rearrange("(k p) n -> p k n", p=128)).then_inc(loaded, 16)
                sp.dma_start(wqT[:, :], io["L1_mix_W_q_T"]).then_inc(loaded, 16)
                sp.dma_start(wout[:, :], io["L1_mix_W_out"]).then_inc(loaded, 16)
                sp.dma_start(bout[:, :], io["L1_mix_b_out"].rearrange("(a n) -> a n", a=1)).then_inc(loaded, 16)

            @block.tensor
            def _(pe):
                pe.wait_ge(loaded, 4 * 16)
                for i, (n, m) in enumerate(PIECES):
                    for k in range(KC):
                        mm = pe.matmul(p_k[i][:, 0:m], w[:, k, W:2 * W], S.xnT[:, k, n:n + m],
                                       start=(k == 0), stop=(k == KC - 1))
                    mm.then_inc(keys, 1)
                pe.wait_ge(raised, len(PIECES))
                for t in range(NT):
                    if t >= 2:
                        pe.wait_ge(copied, t - 1)
                    pe.transpose(p_kv[t % 2][0:P, 0:W], kT[:, t * P:(t + 1) * P], S.ident[:, :])
                    for k in range(KC):
                        mm = pe.matmul(p_kv[t % 2][0:P, W:2 * W], S.xnT[:, k, t * P:(t + 1) * P], w[:, k, 2 * W:3 * W],
                                       start=(k == 0), stop=(k == KC - 1))
                    mm.then_inc(turned, 1)
                    if t >= 1:
                        pe.wait_ge(copied, t)
                        pe.matmul(p_c[:, 0:W], kv[:, (t - 1) % 2, W:2 * W], kv[:, (t - 1) % 2, 0:W],
                                  start=(t == 1), stop=False).then_inc(context, 1)
                pe.wait_ge(copied, NT)
                pe.matmul(p_c[:, 0:W], kv[:, (NT - 1) % 2, W:2 * W], kv[:, (NT - 1) % 2, 0:W],
                          start=False, stop=True).then_inc(context, 1)
                pe.wait_ge(dve, 8)
                pe.matmul(p_w[:, 0:D], ctx[:, :], wout[:, :], start=True, stop=True).then_inc(small, 1)
                pe.wait_ge(dve, 9)
                for k in range(KC):
                    mm = pe.matmul(p_f[:, k * D:(k + 1) * D], wqT[:, k * 128:(k + 1) * 128], cw[:, :],
                                   start=True, stop=True)
                mm.then_inc(small, 1)
                pe.wait_ge(dve, 10)
                for t in range(NT):
                    if t >= 3:
                        pe.wait_ge(added, t - 2)
                    o = p_o[t % 3][0:P, 0:D]
                    for k in range(KC):
                        pe.matmul(o, S.xnT[:, k, t * P:(t + 1) * P], fold[:, k, :], start=(k == 0), stop=False)
                    pe.matmul(o, S.ones[0:1, 0:P], bout[0:1, :], start=False, stop=True).then_inc(mult, 1)

            @block.scalar
            def _(a):
                a.wait_ge(topped, 1)
                for i, (n, m) in enumerate(PIECES):
                    a.activation(kT[:, n:n + m], p_k[i][:, 0:m], ACT.Exp, bias=norm[:, 0:1],
                                 accum_out=total[:, i:i + 1]).then_inc(raised, 1)
                for t in range(NT):
                    a.wait_ge(turned, t + 1)
                    if t >= 2:
                        a.wait_ge(context, t - 1)
                    a.activation(kv[:, t % 2, :], p_kv[t % 2][0:P, 0:2 * W], ACT.Copy).then_inc(copied, 1)

            @block.vector
            def _(v):
                link = linker(v, dve)
                for i, (n, m) in enumerate(PIECES):
                    v.wait_ge(keys, i + 1)
                    ins = v.tensor_reduce(top[:, i:i + 1], p_k[i][:, 0:m], AX.X, ALU.max)
                link(ins)
                link(v.tensor_reduce(norm[:, 1:2], top[:, 0:len(PIECES)], AX.X, ALU.max))
                link(v.tensor_scalar(norm[:, 0:1], norm[:, 1:2], -1.0, None, ALU.mult))
                v.sem_inc(topped, 1)
                v.wait_ge(raised, len(PIECES))
                link(v.tensor_reduce(norm[:, 1:2], total[:, 0:len(PIECES)], AX.X, ALU.add))
                link(v.reciprocal(norm[:, 1:2], norm[:, 1:2]))
                link(v.tensor_scalar(norm[:, 1:2], norm[:, 1:2], float(HW) ** -0.5, None, ALU.mult))
                link(v.memset(ctx[:, :], 0.0))
                v.wait_ge(context, NT)
                for h in range(W // HW):
                    blk = slice(h * HW, (h + 1) * HW)
                    ins = v.tensor_copy(ctx[blk, blk], p_c[blk, blk])
                link(ins)
                v.wait_ge(small, 1)
                link(v.tensor_scalar(cw[:, :], p_w[:, 0:D], norm[:, 1:2], None, ALU.mult))
                v.wait_ge(small, 2)
                link(v.tensor_copy(fold[:, :, :], p_f[:, :].rearrange("p (k n) -> p k n", k=KC)))
                for t in range(NT):
                    v.wait_ge(mult, t + 1)
                    v.tensor_tensor(S.x[:, t, :], S.x[:, t, :], p_o[t % 3][0:P, 0:D], ALU.add).then_inc(added, 1)


def scores1(nc, io, S, weight):
    NR = 64
    with ExitStack() as stack:
        c = Scope(nc, stack, "s1")
        rel = c.sb("rel", [NR, HD])
        rel4 = c.sb("rel4", [NR, NH, HD])
        idx = c.sb("idx", [P, RING, 2, G], I32)
        keys = c.sb("keys", [P, RING, G, D])
        queries = c.sb("queries", [P, RING, G, D])
        hot = c.sb("hot", [P, 2, G, NR])
        hotT = c.sb("hotT", [NR, 2, G, P])
        p_t = [c.ps(f"t{i}", (128, 1024)) for i in range(1)]
        p_r = [c.ps(f"r{i}", (128, 1536)) for i in range(2)]
        names = ("loaded", "dve", "indexed", "asked", "free", "hot", "turned", "copied", "related")
        loaded, dve, indexed, asked, free, hot_made, turned, copied, related = [c.sem(x) for x in names]
        got = [S.gathers[f"s1_got{g}"] for g in range(RING)]
        with nc.Block() as block:

            @block.sync
            def _(sp):
                sp.dma_start(rel[:, :], io["L1_gnn_rel_w"]).then_inc(loaded, 16)

            @block.gpsimd
            def _(pool):
                with pool.Fori(0, T - STEP + 1, STEP) as t0:
                    for g in range(RING):
                        pool.wait_ge(free, t0 // G + g + 1)
                        pool.tensor_copy(idx[:, g, 0, :], S.src[:, bass.ds(t0 + g * G, G)]).then_inc(indexed, 1)
                        pool.tensor_copy(idx[:, g, 1, :], S.dst[:, bass.ds(t0 + g * G, G)]).then_inc(indexed, 1)
                        pool.wait_ge(indexed, (t0 // G) * 2 + 2 * g + 2)
                        pool.sem_inc(asked, 1)
                        for j in range(G):
                            for i, (rows, table) in enumerate(((keys, "keys"), (queries, "queries"))):
                                pool.indirect_dma_start(
                                    out=rows[:, g, j, :], out_offset=None, in_=io[table],
                                    in_offset=bass.IndirectOffsetOnAxis(ap=idx[:, g, i, j:j + 1], axis=0),
                                ).then_inc(got[g], 16)

            @block.vector
            def _(v):
                v.wait_ge(loaded, 16)
                v.tensor_scalar(rel4[:, :, :], rel[:, :].unsqueeze(1).to_broadcast([NR, NH, HD]), 0.2, None,
                                ALU.mult).then_inc(dve, 1)
                v.sem_inc(free, RING)
                v.wait_ge(dve, 1)
                with v.Fori(0, T - STEP + 1, STEP) as t0:
                    link = linker(v, dve, (t0 // STEP) * (3 * RING) + 1)

                    def one_hot(g):
                        v.wait_ge(turned, t0 // G + g + (1 if g == 0 else 0))
                        v.tensor_tensor(hot[:, g % 2, :, :],
                                        S.typ[:, bass.ds(t0 + g * G, G)].unsqueeze(2).to_broadcast([P, G, NR]),
                                        S.nodes[:, 0:NR].unsqueeze(1).to_broadcast([P, G, NR]),
                                        ALU.is_equal).then_inc(hot_made, 1)

                    one_hot(0)
                    for g in range(RING):
                        if g + 1 < RING:
                            one_hot(g + 1)
                        v.wait_ge(got[g], (t0 // STEP) * (32 * G) + 32 * G)
                        v.wait_ge(related, t0 // G + g + 3)
                        k, q = keys[:, g, :, :], queries[:, g, :, :]
                        link(v.tensor_tensor(k, k, p_r[g % 2][0:P, 0:G * D].rearrange("p (t d) -> p t d", d=D), ALU.add))
                        link(v.tensor_tensor(k, k, q, ALU.mult))
                        link(v.tensor_reduce(weight[:, :, bass.ds(t0 + g * G, G)].rearrange("p h t -> p t h"),
                                             k.rearrange("p t (h d) -> p t h d", h=NH), AX.X, ALU.add))
                        v.sem_inc(free, 1)

            @block.tensor
            def _(pe):
                pe.wait_ge(dve, 1)
                pe.sem_inc(turned, 1)
                pe.sem_inc(related, 2)
                with pe.Fori(0, T - STEP + 1, STEP) as t0:
                    for g in range(RING):
                        pe.wait_ge(hot_made, t0 // G + g + 1)
                        pe.wait_ge(copied, t0 // G + g + 1)
                        for j in range(G):
                            mm = pe.matmul(p_t[0][0:NR, j * 128:j * 128 + P], hot[:, g % 2, j, :], S.ident[0:P, 0:P],
                                           start=True, stop=True)
                        mm.then_inc(turned, 1)
                        pe.wait_ge(copied, t0 // G + g + 2)
                        pe.wait_ge(free, t0 // G + g + (RING if g == 0 else RING - 1))
                        for j in range(G):
                            mm = pe.matmul(p_r[g % 2][0:P, j * D:(j + 1) * D], hotT[:, g % 2, j, :],
                                           rel4[:, :, :].rearrange("r h d -> r (h d)"), start=True, stop=True)
                        mm.then_inc(related, 1)

            @block.scalar
            def _(a):
                a.sem_inc(copied, 1)
                with a.Fori(0, T - STEP + 1, STEP) as t0:
                    for g in range(RING):
                        a.wait_ge(turned, t0 // G + g + 2)
                        a.wait_ge(related, t0 // G + g + (2 if g == 0 else 1))
                        a.activation(hotT[:, g % 2, :, :],
                                     p_t[0][0:NR, 0:G * 128].rearrange("r (j p) -> r j p", p=128)[:, :, 0:P],
                                     ACT.Copy).then_inc(copied, 1)


def softmax1(nc, io, S, c, weight):
    den = c.sb("den", [P, NT, NH])
    with ExitStack() as stack:
        c = Scope(nc, stack, "m1")
        top = c.sb("top", [P, NH, T])
        top2 = c.sb("top2", [P, NH, T])
        sums = c.sb("sums", [P, T, NH])
        dve, raised, out = c.sem("dve"), c.sem("raised"), c.sem("out")
        segment_scan(nc, "m1a", S, top[:, :, :], weight[:, :, :], S.keep[:, :], S.joins, T, ALU.max)
        segment_scan(nc, "m1b", S, top2[:, :, :], top[:, :, :], S.keep[:, :], S.joins, T, ALU.max, reverse=True)
        with nc.Block() as block:

            @block.vector
            def _(v):
                v.tensor_tensor(weight[:, :, :], weight[:, :, :], top2[:, :, :], ALU.subtract).then_inc(dve, 1)

            @block.scalar
            def _(a):
                a.wait_ge(dve, 1)
                a.activation(weight[:, :, :], weight[:, :, :], ACT.Exp, scale=float(HD) ** -0.5)
        segment_scan(nc, "m1c", S, top[:, :, :], weight[:, :, :], S.keep[:, :], S.joins, T, ALU.add)
        with nc.Block() as block:

            @block.vector
            def _(v):
                v.tensor_copy(sums[:, :, :].rearrange("p t h -> p h t"), top[:, :, :]).then_inc(raised, 1)

            @block.sync
            def _(sp):
                sp.wait_ge(raised, 1)
                sp.dma_start(io["dens"].rearrange("(p t) h -> p t h", p=P), sums[:, :, :]).then_inc(out, 16)
                sp.wait_ge(out, 16)
    return den


def finish1(nc, io, S, agg, den, xn):
    with ExitStack() as stack:
        c = Scope(nc, stack, "o1")
        w = c.sb("w", [128, KC, D])
        bo = c.sb("bo", [1, D])
        gamma = c.sb("gamma", [P, D])
        beta = c.sb("beta", [P, D])
        aT = c.sb("aT", [128, 2, KC, P])
        stats = c.sb("stats", [P, NT, 6])
        mean, diff, var, std = [c.sb(x, [P, NT]) for x in ("mean", "diff", "var", "std")]
        p_t = [c.ps(f"t{i}") for i in range(2)]
        p_o = [c.ps(f"o{i}") for i in range(3)]
        names = ("loaded", "dve", "turned", "copied", "mult", "added", "rooted", "ready", "counted")
        loaded, dve, turned, copied, mult, added, rooted, ready, counted = [c.sem(x) for x in names]
        with nc.Block() as block:

            @block.sync
            def _(sp):
                sp.dma_start(w[:, :, :], io["L1_gnn_Wo"].rearrange("(k p) n -> p k n", p=128)).then_inc(loaded, 16)
                sp.dma_start(bo[:, :], io["L1_gnn_bo"].rearrange("(a n) -> a n", a=1)).then_inc(loaded, 16)
                for name, tile in (("L1_gnn_gamma", gamma), ("L1_gnn_beta", beta)):
                    sp.dma_start(tile[:, :], io[name].rearrange("(a n) -> a n", a=1).to_broadcast([P, D])).then_inc(loaded, 16)

            @block.tensor
            def _(pe):
                pe.wait_ge(loaded, 4 * 16)
                pe.wait_ge(ready, 1)
                for t in range(NT + 1):
                    if t < NT:
                        if t >= 2:
                            pe.wait_ge(copied, t - 1)
                        for k in range(KC):
                            mm = pe.transpose(p_t[t % 2][:, k * P:(k + 1) * P], agg[:, t, k * 128:(k + 1) * 128],
                                              S.ident[0:P, 0:P])
                        mm.then_inc(turned, 1)
                    if t >= 1:
                        s = t - 1
                        pe.wait_ge(copied, s + 1)
                        if s >= 3:
                            pe.wait_ge(added, s - 2)
                        o = p_o[s % 3][0:P, 0:D]
                        for k in range(KC):
                            pe.matmul(o, aT[:, s % 2, k, :], w[:, k, :], start=(k == 0), stop=False)
                        pe.matmul(o, S.ones[0:1, 0:P], bo[0:1, :], start=False, stop=True).then_inc(mult, 1)

            @block.scalar
            def _(a):
                for t in range(NT):
                    a.wait_ge(turned, t + 1)
                    if t >= 2:
                        a.wait_ge(mult, t - 1)
                    a.activation(aT[:, t % 2, :, :], p_t[t % 2][:, 0:KC * P].rearrange("q (k p) -> q k p", k=KC),
                                 ACT.Copy).then_inc(copied, 1)
                a.wait_ge(counted, MV_STEPS)
                a.activation(std[:, :], var[:, :], ACT.Sqrt).then_inc(rooted, 1)

            @block.vector
            def _(v):
                link = linker(v, dve)
                link(v.reciprocal(den[:, :, :], den[:, :, :]))
                link(v.tensor_tensor(agg[:, :, :].rearrange("p t (h d) -> p (t h) d", h=NH),
                                     agg[:, :, :].rearrange("p t (h d) -> p (t h) d", h=NH),
                                     den[:, :, :].rearrange("p t h -> p (t h)").unsqueeze(2).to_broadcast([P, NT * NH, HD]),
                                     ALU.mult))
                v.sem_inc(ready, 1)
                for t in range(NT):
                    v.wait_ge(mult, t + 1)
                    v.tensor_tensor(xn[:, t, :], xn[:, t, :], p_o[t % 3][0:P, 0:D], ALU.add).then_inc(added, 1)
                    v.wait_ge(added, t + 1)
                    link(v.bn_stats(stats[:, t, :], xn[:, t, :]))
                mean_and_var(linker(v, counted), stats, v, mean[:, :], var[:, :], diff[:, :])
                v.wait_ge(rooted, 1)
                link(v.reciprocal(std[:, :], std[:, :]))
                for t in range(NT):
                    link(v.tensor_scalar(xn[:, t, :], xn[:, t, :], mean[:, t:t + 1], std[:, t:t + 1],
                                         ALU.subtract, ALU.mult))
                v.wait_ge(loaded, 4 * 16)
                link(v.tensor_tensor(xn[:, :, :], xn[:, :, :], gamma[:, :].unsqueeze(1).to_broadcast([P, NT, D]), ALU.mult))
                link(v.tensor_tensor(xn[:, :, :], xn[:, :, :], beta[:, :].unsqueeze(1).to_broadcast([P, NT, D]), ALU.add))
                v.tensor_tensor(S.x[:, :, :], S.x[:, :, :], xn[:, :, :], ALU.add)


def sort_routing_edges(nc, io, S):
    with ExitStack() as stack:
        c = Scope(nc, stack, "so")
        iota_lo = c.sb("iota_lo", [128, LO])
        iota_hi = c.sb("iota_hi", [128, HI])
        src = c.sb("src", [128, GT], I32)
        dst = c.sb("dst", [128, GT], I32)
        dstf = c.sb("dstf", [128, GT])
        digit_lo = c.sb("digit_lo", [128, GT], I32)
        digit_hi = c.sb("digit_hi", [128, GT], I32)
        hot_lo = c.sb("hot_lo", [128, 2, GB, LO], BF16)
        hot_hi = c.sb("hot_hi", [128, GT, HI], BF16)
        tri = c.sb("tri", [128, 128])
        count = c.sb("count", [128, GT, HI])
        upto = c.sb("upto", [128, GT, HI])
        deg, total, start = [c.sb(x, [128, HI]) for x in ("deg", "total", "start")]
        row = c.sb("row", [128, 2, GB * 128], I32)
        row_lo = c.sb("row_lo", [128, 2, GB * 128], I32)
        hotT = c.sb("hotT", [128, 2, GB * 128])
        junk = c.sb("junk", [128, GB, 128], BF16)
        picked = c.sb("picked", [128, GB, HI])
        place = c.sb("place", [128, GT])
        rank = c.sb("rank", [128, GT])
        place_i = c.sb("place_i", [128, GT], I32)
        record = c.sb("record", [128, GT, 2], I32)
        loop_i = c.sb("loop_i", [128, HI], I32)
        last_i = c.sb("last_i", [128, HI], I32)
        loop_rec = c.sb("loop_rec", [128, HI, 2], I32)
        pad = c.sb("pad", [1, GP - GN, 2], I32)
        ring_i = c.sb("ring_i", [128, 2, GB], I32)
        ring_r = c.sb("ring_r", [128, 2, GB, 2], I32)
        p_n = [c.ps(f"n{i}") for i in range(2)]
        p_s = c.ps("s")
        p_g = [c.ps(f"g{i}") for i in range(2)]
        names = ("loaded", "made", "hot_made", "counted", "copied", "dve", "summed", "hotT_made",
                 "fetched", "used", "placed", "staged", "asked", "last_out")
        (loaded, made, hot_made, counted, copied, dve, summed, hotT_made, fetched, used, placed, staged,
         asked, last_out) = [c.sem(x) for x in names]
        sent = [S.gathers[f"so_sent{i}"] for i in range(2)]
        rows_in = [c.sem(f"rows_in{i}") for i in range(2)]
        loops_sent = S.gathers["so_loops_sent"]
        with nc.Block() as block:

            @block.sync
            def _(sp):
                for i, tile in enumerate((src, dst)):
                    sp.dma_start(tile[:, :], io["edge_columns"][i]).then_inc(loaded, 16)
                flat = io["L1_ffn_edge_index"][1:2, :]
                with sp.Fori(0, GT - 2 * GB + 1, 2 * GB) as t0:
                    for i in range(2):
                        sp.wait_ge(used, t0 // GB + i + 1)
                        sp.dma_start(row[:, i, :], flat[:, bass.ds((t0 + i * GB) * 128, GB * 128)]
                                     .to_broadcast([128, GB * 128])).then_inc(rows_in[i], 16)
                sp.wait_ge(placed, 1)
                sp.dma_start(io["last2"].rearrange("(h l) -> l h", l=LO), last_i[:, :]).then_inc(last_out, 16)
                sp.dma_start(io["sorted"][GN:GP, :].rearrange("(a n) c -> a n c", a=1), pad[:, :, :]).then_inc(last_out, 16)
                sp.wait_ge(last_out, 32)

            @block.gpsimd
            def _(pool):
                pool.iota(iota_lo[:, :], [[1, LO]], base=0, channel_multiplier=0,
                          allow_small_or_imprecise_dtypes=True).then_inc(made, 1)
                pool.iota(iota_hi[:, :], [[1, HI]], base=0, channel_multiplier=0,
                          allow_small_or_imprecise_dtypes=True).then_inc(made, 1)
                pool.iota(loop_rec[:, :, :], [[LO, HI], [0, 2]], base=0, channel_multiplier=1).then_inc(made, 1)
                pool.affine_select(out=tri[:, :], in_=S.ones[:, :], compare_op=ALU.is_ge, fill=0.0, base=0,
                                   pattern=[[1, 128]], channel_multiplier=-1).then_inc(made, 1)
                pool.memset(pad[:, :, 0:1], 0).then_inc(made, 1)
                pool.memset(pad[:, :, 1:2], N).then_inc(made, 1)
                pool.wait_ge(placed, 1)
                for h in range(HI):
                    pool.indirect_dma_start(
                        out=io["sorted"], out_offset=bass.IndirectOffsetOnAxis(ap=loop_i[:, h:h + 1], axis=0),
                        in_=loop_rec[:, h, :], in_offset=None,
                        bounds_check=GN - 1, oob_is_err=False).then_inc(loops_sent, 16)
                with pool.Fori(0, GT - 2 * GB + 1, 2 * GB) as t0:
                    for i in range(2):
                        pool.tensor_copy(ring_i[:, i, :], place_i[:, bass.ds(t0 + i * GB, GB)]).then_inc(staged, 1)
                        pool.tensor_copy(ring_r[:, i, :, :], record[:, bass.ds(t0 + i * GB, GB), :]).then_inc(staged, 1)
                        pool.wait_ge(staged, (t0 // GB) * 2 + 2 * i + 2)
                        pool.sem_inc(asked, 1)
                        for j in range(GB):
                            pool.indirect_dma_start(
                                out=io["sorted"],
                                out_offset=bass.IndirectOffsetOnAxis(ap=ring_i[:, i, j:j + 1], axis=0),
                                in_=ring_r[:, i, j, :], in_offset=None).then_inc(sent[i], 16)
                    for i in range(2):
                        pool.wait_ge(sent[i], (t0 // (2 * GB)) * (16 * GB) + 16 * GB)
                        pool.sem_inc(asked, 1)
                pool.wait_ge(loops_sent, 16 * HI)

            @block.tensor
            def _(pe):
                pe.sem_inc(counted, 2)
                with pe.Fori(0, GT - 2 * GB + 1, 2 * GB) as t0:
                    for i in range(2):
                        pe.wait_ge(hot_made, t0 // GB + i + 1)
                        pe.wait_ge(copied, t0 // GB + i + 1)
                        for j in range(GB):
                            mm = pe.matmul(p_n[i][:, j * HI:(j + 1) * HI], hot_lo[:, i, j, :],
                                           hot_hi[:, bass.ds(t0 + i * GB + j, 1), :].rearrange("p a b -> p (a b)"),
                                           start=True, stop=True)
                        mm.then_inc(counted, 1)
                pe.wait_ge(summed, 1)
                pe.wait_ge(made, 6)
                pe.matmul(p_s[:, 0:HI], S.ones[:, :], deg[:, :], start=True, stop=True)
                pe.matmul(p_s[:, 64:64 + HI], tri[:, :], deg[:, :], start=True, stop=True).then_inc(summed, 1)
                pe.wait_ge(summed, 3)
                with pe.Fori(0, GT - 2 * GB + 1, 2 * GB) as t0:
                    for i in range(2):
                        pe.wait_ge(hotT_made, t0 // GB + i + 1)
                        pe.wait_ge(used, t0 // GB + i + 1)
                        for j in range(GB):
                            mm = pe.matmul(p_g[i][:, j * HI:(j + 1) * HI], hotT[:, i, j * 128:(j + 1) * 128],
                                           upto[:, bass.ds(t0 + i * GB + j, 1), :].rearrange("p a b -> p (a b)"),
                                           start=True, stop=True)
                        mm.then_inc(fetched, 1)

            @block.scalar
            def _(a):
                a.sem_inc(copied, 2)
                with a.Fori(0, GT - 2 * GB + 1, 2 * GB) as t0:
                    for i in range(2):
                        a.wait_ge(counted, t0 // GB + i + 1 + 2)
                        a.activation(count[:, bass.ds(t0 + i * GB, GB), :].rearrange("p a b -> p (a b)"),
                                     p_n[i][:, 0:GB * HI], ACT.Copy).then_inc(copied, 1)

            @block.vector
            def _(v):
                link = linker(v, dve)
                v.sem_inc(used, 2)
                v.wait_ge(loaded, 32)
                link(v.tensor_scalar(digit_lo[:, :], dst[:, :], LO - 1, None, ALU.bitwise_and))
                link(v.tensor_scalar(digit_hi[:, :], dst[:, :], 7, None, ALU.logical_shift_right))
                link(v.tensor_copy(dstf[:, :], dst[:, :]))
                link(v.tensor_copy(record[:, :, 0], src[:, :]))
                link(v.tensor_copy(record[:, :, 1], dst[:, :]))
                v.wait_ge(made, 6)
                with v.Fori(0, GT - 2 * GB + 1, 2 * GB) as t0:
                    for i in range(2):
                        v.wait_ge(counted, t0 // GB + i + 1)
                        t = t0 + i * GB
                        v.tensor_tensor(hot_lo[:, i, :, :],
                                        digit_lo[:, bass.ds(t, GB)].unsqueeze(2).to_broadcast([128, GB, LO]),
                                        iota_lo[:, :].unsqueeze(1).to_broadcast([128, GB, LO]), ALU.is_equal)
                        v.tensor_tensor(hot_hi[:, bass.ds(t, GB), :],
                                        digit_hi[:, bass.ds(t, GB)].unsqueeze(2).to_broadcast([128, GB, HI]),
                                        iota_hi[:, :].unsqueeze(1).to_broadcast([128, GB, HI]),
                                        ALU.is_equal).then_inc(hot_made, 1)
                v.wait_ge(copied, GT // GB + 2)
                for h in range(HI):
                    ins = v.tensor_tensor_scan(upto[:, :, h], S.ones[:, 0:1].to_broadcast([128, GT]), count[:, :, h],
                                               0.0, ALU.mult, ALU.add)
                link(ins)
                link(v.tensor_scalar(deg[:, :], upto[:, GT - 1, :], 1.0, None, ALU.add))
                v.sem_inc(summed, 1)
                v.wait_ge(summed, 2)
                one = S.ones[:, 0:HI]
                link(v.tensor_copy(total[:, :], p_s[:, 0:HI]))
                link(v.tensor_tensor_scan(start[:, :], one, total[:, :], 0.0, ALU.mult, ALU.add))
                link(v.tensor_tensor(start[:, :], start[:, :], total[:, :], ALU.subtract))
                link(v.tensor_tensor(start[:, :], start[:, :], p_s[:, 64:64 + HI], ALU.add))
                link(v.tensor_scalar(total[:, :], start[:, :], 1.0, None, ALU.subtract))
                link(v.tensor_copy(last_i[:, :], total[:, :]))
                link(v.tensor_tensor(start[:, :], start[:, :], deg[:, :], ALU.subtract))
                link(v.tensor_copy(loop_i[:, :], start[:, :]))
                link(v.tensor_scalar(start[:, :], start[:, :], 1.0, None, ALU.add))
                link(v.tensor_tensor(upto[:, :, :], upto[:, :, :], count[:, :, :], ALU.subtract))
                link(v.tensor_tensor(upto[:, :, :], upto[:, :, :],
                                     start[:, :].unsqueeze(1).to_broadcast([128, GT, HI]), ALU.add))
                v.sem_inc(summed, 1)
                with v.Fori(0, GT - 2 * GB + 1, 2 * GB) as t0:
                    link = linker(v, dve, (t0 // (2 * GB)) * 6 + 18)
                    for i in range(2):
                        v.wait_ge(rows_in[i], (t0 // (2 * GB)) * 16 + 16)
                        link(v.tensor_scalar(row_lo[:, i, :], row[:, i, :], LO - 1, None, ALU.bitwise_and))
                        v.tensor_scalar(hotT[:, i, :], row_lo[:, i, :], S.row[:, 0:1], None,
                                        ALU.is_equal).then_inc(hotT_made, 1)
                        for j in range(GB):
                            t = t0 + i * GB + j
                            v.scalar_tensor_tensor(junk[:, j, :], row[:, i, j * 128:(j + 1) * 128], dstf[:, bass.ds(t, 1)],
                                                   S.below[:, :], ALU.is_equal, ALU.mult,
                                                   accum_out=rank[:, bass.ds(t, 1)])
                        v.wait_ge(fetched, t0 // GB + i + 1)
                        link(v.tensor_tensor(picked[:, :, :], p_g[i][:, 0:GB * HI].rearrange("p (a b) -> p a b", b=HI),
                                             hot_hi[:, bass.ds(t0 + i * GB, GB), :], ALU.mult))
                        link(v.tensor_reduce(place[:, bass.ds(t0 + i * GB, GB)], picked[:, :, :], AX.X, ALU.add))
                        v.sem_inc(used, 1)
                link = linker(v, dve, (GT // (2 * GB)) * 6 + 18)
                link(v.tensor_tensor(place[:, :], place[:, :], rank[:, :], ALU.add))
                link(v.tensor_copy(place_i[:, :], place[:, :]))
                v.sem_inc(placed, 1)


def layer1_experts(nc, io, S):
    with ExitStack() as stack:
        c = Scope(nc, stack, "f1")
        gates = c.sb("gates", [P, NT, NX1])
        normalize(nc, "n3", S, None, S.xnT)
        attend1(nc, io, S, gates)
        experts1(nc, io, S, gates)


def attend1(nc, io, S, gates):
    CH = NH * NX1
    C20 = CH + NH
    C24 = CH + 2 * NH
    RG = 16
    with ExitStack() as stack:
        c = Scope(nc, stack, "a1")
        joins = c.sb("joins", [P, 4])
        keep = c.sb("keep", [P, GC])
        starts = c.sb("starts", [P, GC])
        edges = c.sb("edges", [P, GC, 2], I32)
        vals = c.sb("vals", [P, C24, GC])
        pay = c.sb("pay", [P, C20, GC])
        work = c.sb("work", [P, NH, GC])
        best = c.sb("best", [P, NH, GC])
        node = c.sb("node", [P, NT, C20])
        last = c.sb("last", [P, NT], I32)
        with ExitStack() as s2:
            c2 = Scope(nc, s2, "a2")
            w = c2.sb("w", [128, KC, CH])
            att = c2.sb("att", [P, 2, CH])
            h = c2.sb("h", [P, NT, C24])
            prod = c2.sb("prod", [P, NT, CH])
            first = c2.sb("first", [P, 4], I32)
            firstf = c2.sb("firstf", [P, 4])
            dstf = c2.sb("dstf", [P, GC])
            ring_i = c2.sb("ring_i", [P, 2, RG], I32)
            ring = c2.sb("ring", [P, 2, RG, C24])
            p_h = c2.ps("h")
            names = ("loaded", "cleared", "mult", "dve", "tabled", "sent", "staged", "asked", "free")
            loaded, cleared, mult, dve, tabled, sent, staged, asked, free = [c2.sem(x) for x in names]
            got = [S.gathers[f"a1_got{i}"] for i in range(2)]
            with nc.Block() as block:

                @block.sync
                def _(sp):
                    sp.dma_start(w[:, :, :], io["L1_ffn_W_gat"].rearrange("(k p) n -> p k n", p=128)).then_inc(loaded, 16)
                    for i, n in enumerate(("src", "dst")):
                        sp.dma_start(att[:, i, :], io[f"L1_ffn_att_{n}"].rearrange("(a h) e -> a (h e)", a=1)
                                     .to_broadcast([P, CH])).then_inc(loaded, 16)
                    sp.dma_start(edges[:, :, :], io["sorted"].rearrange("(p t) c -> p t c", p=P)).then_inc(loaded, 16)
                    sp.dma_start(last[:, :], io["last2"][0:N].rearrange("(t p) -> p t", p=P)).then_inc(loaded, 16)
                    d2 = io["sorted"].rearrange("(p t) c -> p t c", p=P)
                    sp.wait_ge(cleared, 1)
                    sp.dma_start(first[0:P - 1, 0:1], d2[1:P, 0, 1:2]).then_inc(loaded, 16)
                    sp.dma_start(first[1:P, 1:2], d2[0:P - 1, GC - 1, 1:2]).then_inc(loaded, 16)
                    sp.wait_ge(tabled, 1)
                    sp.dma_start(io["gat"].rearrange("(t p) c -> p t c", p=P), h[:, :, :]).then_inc(sent, 16)

                @block.tensor
                def _(pe):
                    pe.wait_ge(loaded, 7 * 16)
                    for t in range(NT):
                        for k in range(KC):
                            mm = pe.matmul(p_h[0:P, t * CH:(t + 1) * CH], S.xnT[:, k, t * P:(t + 1) * P], w[:, k, :],
                                           start=(k == 0), stop=(k == KC - 1))
                    mm.then_inc(mult, 1)

                @block.gpsimd
                def _(pool):
                    pool.wait_ge(sent, 16)
                    with pool.Fori(0, GC - 2 * RG + 1, 2 * RG) as t0:
                        for i in range(2):
                            pool.wait_ge(free, t0 // RG + i + 1)
                            pool.tensor_copy(ring_i[:, i, :], edges[:, bass.ds(t0 + i * RG, RG), 0]).then_inc(staged, 1)
                            pool.wait_ge(staged, t0 // RG + i + 1)
                            pool.sem_inc(asked, 1)
                            for j in range(RG):
                                pool.indirect_dma_start(
                                    out=ring[:, i, j, :], out_offset=None, in_=io["gat"],
                                    in_offset=bass.IndirectOffsetOnAxis(ap=ring_i[:, i, j:j + 1], axis=0),
                                ).then_inc(got[i], 16)

                @block.vector
                def _(v):
                    link = linker(v, dve)
                    link(v.memset(first[:, :], -1))
                    v.sem_inc(cleared, 1)
                    v.sem_inc(free, 2)
                    v.wait_ge(mult, 1)
                    link(v.tensor_copy(h[:, :, 0:CH], p_h[0:P, 0:NT * CH].rearrange("p (t c) -> p t c", c=CH)))
                    for i in range(2):
                        link(v.tensor_tensor(prod[:, :, :], h[:, :, 0:CH],
                                             att[:, i, :].unsqueeze(1).to_broadcast([P, NT, CH]), ALU.mult))
                        link(v.tensor_reduce(h[:, :, CH + i * NH:CH + (i + 1) * NH],
                                             prod[:, :, :].rearrange("p t (h e) -> p t h e", e=NX1), AX.X, ALU.add))
                    v.sem_inc(tabled, 1)
                    link(v.tensor_copy(dstf[:, :], edges[:, :, 1]))
                    link(v.tensor_copy(firstf[:, :], first[:, :]))
                    link(v.memset(keep[:, :], 1.0))
                    link(v.tensor_tensor(keep[:, 1:GC], dstf[:, 1:GC], dstf[:, 0:GC - 1], ALU.is_equal))
                    link(v.tensor_tensor(joins[:, 0:1], firstf[:, 1:2], dstf[:, 0:1], ALU.is_equal))
                    link(v.tensor_tensor(joins[:, 1:2], firstf[:, 0:1], dstf[:, GC - 1:GC], ALU.is_equal))
                    link(v.tensor_tensor(joins[:, 2:3], dstf[:, 0:1], dstf[:, GC - 1:GC], ALU.is_equal))
                    link(v.tensor_scalar(starts[:, :], keep[:, :], -1.0, 1.0, ALU.mult, ALU.add))
                    link(v.tensor_scalar(starts[:, 0:1], joins[:, 0:1], -1.0, 1.0, ALU.mult, ALU.add))
                    with v.Fori(0, GC - 2 * RG + 1, 2 * RG) as t0:
                        link = linker(v, dve, (t0 // RG) + 15)
                        for i in range(2):
                            v.wait_ge(got[i], (t0 // (2 * RG)) * (16 * RG) + 16 * RG)
                            link(v.tensor_copy(vals[:, :, bass.ds(t0 + i * RG, RG)].rearrange("p c t -> p t c"),
                                               ring[:, i, :, :]))
                            v.sem_inc(free, 1)
                    link = linker(v, dve, GC // RG + 15)
                    link(v.tensor_tensor(vals[:, CH + NH:C24, :], vals[:, CH + NH:C24, :],
                                         starts[:, :].unsqueeze(1).to_broadcast([P, NH, GC]), ALU.mult))
        segment_scan(nc, "sa", S, work[:, :, :], vals[:, CH + NH:C24, :], keep[:, :], joins, GC, ALU.add)
        logits = vals[:, CH:CH + NH, :]
        with ExitStack() as s2:
            c2 = Scope(nc, s2, "a3")
            dve = c2.sem("dve")
            with nc.Block() as block:
                @block.vector
                def _(v):
                    link = linker(v, dve)
                    link(v.tensor_tensor(logits, logits, work[:, :, :], ALU.add))
                    link(v.scalar_tensor_tensor(work[:, :, :], logits, 0.2, logits, ALU.mult, ALU.max))
        segment_scan(nc, "sb", S, best[:, :, :], work[:, :, :], keep[:, :], joins, GC, ALU.max)
        segment_scan(nc, "sc", S, logits, best[:, :, :], keep[:, :], joins, GC, ALU.max, reverse=True)
        with ExitStack() as s2:
            c2 = Scope(nc, s2, "a4")
            dve, raised = c2.sem("dve"), c2.sem("raised")
            with nc.Block() as block:
                @block.scalar
                def _(a):
                    a.wait_ge(dve, 1)
                    a.activation(pay[:, CH:C20, :], work[:, :, :], ACT.Exp).then_inc(raised, 1)

                @block.vector
                def _(v):
                    v.tensor_tensor(work[:, :, :], work[:, :, :], logits, ALU.subtract).then_inc(dve, 1)
                    v.wait_ge(raised, 1)
                    for hd in range(NH):
                        v.tensor_tensor(pay[:, hd * NX1:(hd + 1) * NX1, :], vals[:, hd * NX1:(hd + 1) * NX1, :],
                                        pay[:, CH + hd:CH + hd + 1, :].to_broadcast([P, NX1, GC]), ALU.mult)
        total = vals[:, 0:C20, :]
        segment_scan(nc, "sd", S, total, pay[:, :, :], keep[:, :], joins, GC, ALU.add)
        with ExitStack() as s2:
            c2 = Scope(nc, s2, "a5")
            flat = pay[:, :, :].rearrange("p c t -> p (c t)").rearrange("p (t c) -> p t c", c=C20)
            small = c2.sb("small", [P, 3, CH])
            z = c2.sb("z", [P, NT, CH])
            sq = c2.sb("sq", [P, NT, CH])
            mean, var, std, top, low = [c2.sb(x, [P, NT]) for x in ("mean", "var", "std", "top", "low")]
            score, hot1, hot2 = [c2.sb(x, [P, NT, NX1]) for x in ("score", "hot1", "hot2")]
            rec = c2.sb("rec", [P, NT, NH])
            order = c2.sb("order", [P, NX1])
            names = ("loaded", "dve", "sent", "made", "rooted", "raised")
            fetched = S.gathers["a1_fetched"]
            loaded, dve, sent, made, rooted, raised = [c2.sem(x) for x in names]
            with nc.Block() as block:

                @block.sync
                def _(sp):
                    for i, n in enumerate(("b_gat", "ln_gamma", "ln_beta")):
                        sp.dma_start(small[:, i, :], io[f"L1_ffn_{n}"].rearrange("(a n) -> a n", a=1)
                                     .to_broadcast([P, CH])).then_inc(loaded, 16)
                    sp.wait_ge(dve, 1)
                    sp.dma_start(io["gsum"].rearrange("(p t) c -> p t c", p=P), flat).then_inc(sent, 16)
                    sp.wait_ge(sent, 16)

                @block.gpsimd
                def _(pool):
                    pool.iota(order[:, :], [[-1, NX1]], base=NX1, channel_multiplier=0,
                              allow_small_or_imprecise_dtypes=True).then_inc(made, 1)
                    pool.wait_ge(sent, 16)
                    for t in range(NT):
                        pool.indirect_dma_start(
                            out=node[:, t, :], out_offset=None, in_=io["gsum"],
                            in_offset=bass.IndirectOffsetOnAxis(ap=last[:, t:t + 1], axis=0)).then_inc(fetched, 16)

                @block.scalar
                def _(a):
                    a.wait_ge(dve, 12)
                    a.activation(std[:, :], var[:, :], ACT.Sqrt).then_inc(rooted, 1)
                    a.wait_ge(dve, 30)
                    a.activation(top[:, :], low[:, :], ACT.Exp).then_inc(raised, 1)

                @block.vector
                def _(v):
                    link = linker(v, dve)
                    link(v.tensor_copy(flat.rearrange("p t c -> p c t"), total))
                    v.wait_ge(fetched, 16 * NT)
                    v.wait_ge(loaded, 48)
                    v.wait_ge(made, 1)

                    def wide(x, n=CH):
                        return x.unsqueeze(2).to_broadcast([P, NT, n])

                    def rows(i):
                        return small[:, i, :].unsqueeze(1).to_broadcast([P, NT, CH])

                    link(v.tensor_scalar(rec[:, :, :], node[:, :, CH:C20], 1e-16, None, ALU.add))
                    link(v.reciprocal(rec[:, :, :], rec[:, :, :]))
                    for hd in range(NH):
                        ins = v.tensor_tensor(z[:, :, hd * NX1:(hd + 1) * NX1], node[:, :, hd * NX1:(hd + 1) * NX1],
                                              wide(rec[:, :, hd], NX1), ALU.mult)
                    link(ins)
                    link(v.tensor_tensor(z[:, :, :], z[:, :, :], rows(0), ALU.add))
                    link(v.tensor_reduce(mean[:, :], z[:, :, :], AX.X, ALU.add))
                    link(v.tensor_scalar(mean[:, :], mean[:, :], 1.0 / CH, None, ALU.mult))
                    link(v.tensor_tensor(z[:, :, :], z[:, :, :], wide(mean[:, :]), ALU.subtract))
                    link(v.tensor_tensor(sq[:, :, :], z[:, :, :], z[:, :, :], ALU.mult))
                    link(v.tensor_reduce(var[:, :], sq[:, :, :], AX.X, ALU.add))
                    link(v.tensor_scalar(var[:, :], var[:, :], 1.0 / CH, None, ALU.mult))
                    link(v.tensor_scalar(var[:, :], var[:, :], EPS, None, ALU.add))
                    v.wait_ge(rooted, 1)
                    link(v.reciprocal(std[:, :], std[:, :]))
                    link(v.tensor_tensor(z[:, :, :], z[:, :, :], wide(std[:, :]), ALU.mult))
                    link(v.tensor_tensor(z[:, :, :], z[:, :, :], rows(1), ALU.mult))
                    link(v.tensor_tensor(z[:, :, :], z[:, :, :], rows(2), ALU.add))
                    link(v.tensor_reduce(score[:, :, :], z[:, :, :].rearrange("p t (h e) -> p t e h", e=NX1),
                                         AX.X, ALU.add))
                    link(v.tensor_scalar(score[:, :, :], score[:, :, :], 1.0 / NH, None, ALU.mult))
                    ranked = order[:, :].unsqueeze(1).to_broadcast([P, NT, NX1])

                    def first_best(hot, best):
                        link(v.tensor_reduce(best, score[:, :, :], AX.X, ALU.max))
                        link(v.tensor_tensor(hot, score[:, :, :], wide(best, NX1), ALU.is_equal))
                        link(v.tensor_tensor(hot, hot, ranked, ALU.mult))
                        link(v.tensor_reduce(mean[:, :], hot, AX.X, ALU.max))
                        link(v.tensor_tensor(hot, ranked, wide(mean[:, :], NX1), ALU.is_equal))

                    first_best(hot1[:, :, :], top[:, :])        
                    link(v.scalar_tensor_tensor(score[:, :, :], hot1[:, :, :], -BIG, score[:, :, :],
                                                ALU.mult, ALU.add))
                    first_best(hot2[:, :, :], low[:, :])        
                    link(v.tensor_tensor(low[:, :], low[:, :], top[:, :], ALU.subtract))
                    v.wait_ge(raised, 1)
                    link(v.tensor_scalar(var[:, :], top[:, :], 1.0, None, ALU.add))
                    link(v.reciprocal(var[:, :], var[:, :]))
                    link(v.tensor_tensor(top[:, :], top[:, :], var[:, :], ALU.mult))
                    link(v.tensor_tensor(hot1[:, :, :], hot1[:, :, :], wide(var[:, :], NX1), ALU.mult))
                    link(v.tensor_tensor(hot2[:, :, :], hot2[:, :, :], wide(top[:, :], NX1), ALU.mult))
                    v.tensor_tensor(gates[:, :, :], hot1[:, :, :], hot2[:, :, :], ALU.add)


def experts1(nc, io, S, gates):
    B = U * P
    CUT = ((0, 3 * P, 0), (3 * P, B, 512))
    NCH = HX1 // 128
    with ExitStack() as stack:
        c = Scope(nc, stack, "h1")
        w1 = c.sb("w1", [128, KC, NX1 * HX1])
        w2 = c.sb("w2", [128, NX1 * NCH, D])
        b1 = c.sb("b1", [128, NX1 * NCH])
        b2 = c.sb("b2", [1, NX1, 2, D])
        hid = c.sb("hid", [128, 2, B])
        p_h = [c.ps(f"h{i}", (128, 1024)) for i in range(2)]
        p_o = c.ps("o", (128, 1536))
        names = ("loaded", "hidden", "active", "done", "emptied", "dve")
        loaded, hidden, active, done, emptied, dve = [c.sem(x) for x in names]
        ALLC = NX1 * NCH
        with nc.Block() as block:

            @block.sync
            def _(sp):
                sp.dma_start(w1[:, :, :], io["L1_ffn_W1"].rearrange("(k p) n -> p k n", p=128)).then_inc(loaded, 16)
                sp.dma_start(w2[:, :, :], io["L1_ffn_W2"].rearrange("(c p) n -> p c n", p=128)).then_inc(loaded, 16)
                sp.dma_start(b1[:, :], io["L1_ffn_b1"]).then_inc(loaded, 16)
                for i in range(2):
                    sp.dma_start(b2[:, :, i, :], io["L1_ffn_b2"].rearrange("(a e) n -> a e n", a=1)).then_inc(loaded, 16)

            @block.tensor
            def _(pe):
                pe.wait_ge(loaded, 5 * 16)
                with pe.Fori(0, NT - U + 1, U) as t0:
                    n0 = t0 * P

                    def make_hidden(ch):
                        pe.wait_ge(active, (t0 // U) * ALLC + ch + 1)
                        for lo, hi, at in CUT:
                            for k in range(KC):
                                mm = pe.matmul(p_h[ch % 2][:, at:at + hi - lo], w1[:, k, ch * 128:(ch + 1) * 128],
                                               S.xnT[:, k, bass.ds(n0 + lo, hi - lo)],
                                               start=(k == 0), stop=(k == KC - 1))
                        mm.then_inc(hidden, 1)

                    def add_output(ch):
                        e = ch // NCH
                        if ch % NCH == 0:
                            pe.wait_ge(emptied, (t0 // U) * NX1 + e + 1)
                            for lo, hi in ((0, 512), (512, 1024), (1024, U * D)):
                                pe.matmul(p_o[0:P, lo:hi], S.ones[0:1, 0:P],
                                          b2[0:1, e, :, :].rearrange("a i n -> a (i n)")[:, 0:hi - lo],
                                          start=True, stop=False, skip_group_check=True)
                        pe.wait_ge(active, (t0 // U) * ALLC + ch + 3)
                        for u in range(U):
                            mm = pe.matmul(p_o[0:P, u * D:(u + 1) * D], hid[:, ch % 2, u * P:(u + 1) * P],
                                           w2[:, ch, :], start=False, stop=(ch % NCH == NCH - 1), skip_group_check=True)
                        mm.then_inc(done, 1)

                    make_hidden(0)
                    for ch in range(ALLC):
                        if ch + 1 < ALLC:
                            make_hidden(ch + 1)
                        add_output(ch)

            @block.scalar
            def _(a):
                a.wait_ge(loaded, 5 * 16)
                a.sem_inc(active, 2)
                a.sem_inc(done, 2)
                with a.Fori(0, NT - U + 1, U) as t0:
                    for ch in range(ALLC):
                        a.wait_ge(hidden, (t0 // U) * ALLC + ch + 1)
                        a.wait_ge(done, (t0 // U) * ALLC + ch + 1)
                        for lo, hi, at in CUT:
                            ins = a.activation(hid[:, ch % 2, lo:hi], p_h[ch % 2][:, at:at + hi - lo], ACT.Gelu,
                                               bias=b1[:, ch:ch + 1])
                        ins.then_inc(active, 1)

            @block.vector
            def _(v):
                v.sem_inc(emptied, 1)
                with v.Fori(0, NT - U + 1, U) as t0:
                    link = linker(v, dve, (t0 // U) * NX1)
                    for e in range(NX1):
                        v.wait_ge(done, (t0 // U) * ALLC + (e + 1) * NCH + 2)
                        for u in range(U):
                            xt = S.x[:, bass.ds(t0 + u, 1), :].rearrange("p a b -> p (a b)")
                            ins = v.scalar_tensor_tensor(xt, p_o[0:P, u * D:(u + 1) * D],
                                                         gates[:, bass.ds(t0 + u, 1), e], xt, ALU.mult, ALU.add)
                        link(ins)
                        v.sem_inc(emptied, 1)


class State:
    pass


_TRANSPOSED = {"L0_gnn_W", "L0_ffn_router_w"}


def build(nc, io, out):
    with ExitStack() as stack:
        stack.enter_context(nc.allow_non_contiguous_dma(reason="single columns, small vectors"))
        c = Scope(nc, stack, "all")
        S = State()
        S.gathers = {name: c.sem(name) for name in GATHER_SEMAPHORES}
        S.first_semaphore = min(nc.free_semaphores)
        S.x = c.sb("x", [P, NT, D])
        S.ident = c.sb("ident", [128, 128])
        S.ones = c.sb("ones", [128, 128])
        S.below = c.sb("below", [128, 128])
        S.row = c.sb("row", [128, 1])
        S.nodes = c.sb("nodes", [P, N])
        S.dst = c.sb("dst", [P, T], I32)
        S.dstf = c.sb("dstf", [P, T])
        S.src = c.sb("src", [P, T], I32)
        S.typ = c.sb("typ", [P, T])
        S.w = c.sb("w", [P, T])
        S.keep = c.sb("keep", [P, T])
        S.joins = c.sb("joins", [P, 4])
        S.goes_on = c.sb("goes_on", [P, 1])
        S.last = c.sb("last", [P, NT], I32)
        load_and_count(nc, io, S)
        sort_routing_edges(nc, io, S)
        S.xnT = c.sb("xnT", [128, KC, N])
        normalize(nc, "n0", S, None, S.xnT)
        layer0_graph(nc, io, S)
        normalize(nc, "n1", S, None, S.xnT)
        layer0_experts(nc, io, S)
        clear_semaphores(nc, io, S)
        layer1_graph(nc, io, S)
        clear_semaphores(nc, io, S)
        layer1_experts(nc, io, S)
        done = c.sem("done")
        with nc.Block() as block:
            @block.sync
            def _(sp):
                sp.dma_start(out.rearrange("(t p) d -> p t d", p=P), S.x[:, :, :]).then_inc(done, 16)
                sp.wait_ge(done, 16)


_SCRATCH = {
    "last": ((LO * HI,), I32),
    "table": ((N, D), F32),
    "sums": ((E, D), F32),
    "queries": ((N, D), F32),
    "keys": ((N, D), F32),
    "values": ((N, D), F32),
    "dens": ((E, NH), F32),
    "sorted": ((GP, 2), I32),
    "last2": ((LO * HI,), I32),
    "gat": ((N, 24), F32),
    "gsum": ((GP, 20), F32),
}


def kernel(**inputs):
    import numpy as _np
    import concourse.bacc as _bacc
    from concourse.bass_utils import run_bass_kernel_spmd as _run

    nc = _bacc.Bacc("TRN2", target_bir_lowering=False, num_devices=1)
    arrays, io = {}, {}
    inputs["L0_mix_W_v_T"] = _np.asarray(inputs["L0_mix_W_qkv"])[:, 2 * D:].T
    inputs["L1_mix_W_q_T"] = _np.asarray(inputs["L1_mix_W_qkv"])[:, 0:128].T
    edges = _np.asarray(inputs["L1_ffn_edge_index"])
    inputs["edge_columns"] = edges.reshape(2, GT, 128).transpose(0, 2, 1)
    inputs["L1_ffn_W1"] = _np.asarray(inputs["L1_ffn_W1"]).transpose(1, 0, 2).reshape(D, NX1 * HX1)
    inputs["L1_ffn_b1"] = _np.asarray(inputs["L1_ffn_b1"]).reshape(NX1 * HX1 // 128, 128).T
    inputs["L1_ffn_W2"] = _np.asarray(inputs["L1_ffn_W2"]).reshape(NX1 * HX1, D)
    w1 = _np.asarray(inputs["L0_ffn_W1"])
    inputs["L0_ffn_W1"] = w1.transpose(1, 0, 2).reshape(D, NX * HX)
    inputs["L0_ffn_b1"] = _np.asarray(inputs["L0_ffn_b1"]).reshape(NC0, 128).T
    inputs["L0_ffn_W2"] = _np.asarray(inputs["L0_ffn_W2"]).reshape(NX * HX, D)
    for name, a in inputs.items():
        a = _np.asarray(a)
        if name in _TRANSPOSED:
            a = a.T
        a = _np.ascontiguousarray(a)
        arrays[f"in_{name}"] = a
        io[name] = nc.dram_tensor(f"in_{name}", a.shape, mybir.dt.from_np(a.dtype), kind="ExternalInput").ap()
    for name, (shape, dt) in _SCRATCH.items():
        io[name] = nc.dram_tensor(f"s_{name}", list(shape), dt, kind="Internal").ap()
    out = nc.dram_tensor("out", (N, D), F32, kind="ExternalOutput").ap()
    build(nc, io, out)
    r = _run(nc, [arrays], core_ids=[0])
    return r.results[0]["out"]
```

```python
from contextlib import ExitStack

import concourse.bass as bass
from concourse import mybir

F32 = mybir.dt.float32
BF16 = mybir.dt.bfloat16
I32 = mybir.dt.int32
U32 = mybir.dt.uint32
ALU = mybir.AluOpType
ACT = mybir.ActivationFunctionType
AX = mybir.AxisListType

D = 256
KC = D // 128
P = 125
N = 3125
NT = N // P
U = 5
E = 53125
T = E // P
G = 5
RING = 5
STEP = G * RING
ITERS = T // STEP
BIG = 1.0e30
EPS = 1e-5
NH = 4
HD = D // NH
NX = 32
HX = 64
NC0 = NX * HX // 128
LO = 128
HI = 25
GE = 32768
GB = 13
QB = 4
GT = GB * QB * (N // 125 // 5)
PAD = 25 * 128 - 1
GN = GE + N
GC = 288
GP = P * GC
NX1 = 4
HX1 = 512
NCH1 = HX1 // 128
EARLY = 3


def linker(eng, sem, base=0):
    count = [0]

    def link(ins):
        count[0] += 1
        ins.then_inc(sem, 1)
        eng.wait_ge(sem, base + count[0])

    return link


GATHER_SEMAPHORES = (
    [f"w0_got{g}" for g in range(RING)] + [f"w1_got{g}" for g in range(RING)] +
    [f"s1_got{g}" for g in range(RING)] + ["g0_fetched", "g1_fetched", "g1_dens_in", "so_sent0", "so_sent1",
                                           "so_loops_sent", "a1_got0", "a1_got1", "a1_fetched"])


class Scope:

    def __init__(self, nc, stack, tag):
        self.nc, self.stack, self.tag = nc, stack, tag

    def sb(self, name, shape, dt=F32):
        return self.stack.enter_context(self.nc.sbuf_tensor(f"{self.tag}_{name}", shape, dt))

    def ps(self, name, shape=(128, 512), dt=F32):
        return self.stack.enter_context(self.nc.psum_tensor(f"{self.tag}_p_{name}", list(shape), dt))

    def sem(self, name):
        return self.stack.enter_context(self.nc.semaphore(f"{self.tag}_{name}"))


def clear_semaphores(nc, io, S):
    with nc.Block() as block:

        @block.sync
        def _(sp):
            sp.sem_clear(range(S.first_semaphore, 256))


def load(nc, io, S):
    with ExitStack() as stack:
        c = Scope(nc, stack, "load")
        first = c.sb("first", [P, 4], I32)
        firstf = c.sb("firstf", [P, 4])
        loaded, made, dve, filled = [c.sem(x) for x in ("loaded", "made", "dve", "filled")]
        with nc.Block() as block:

            @block.sync
            def _(sp):
                sp.dma_start(S.dst[:, :], io["dst"].rearrange("(p t) -> p t", p=P)).then_inc(loaded, 16)
                sp.dma_start(S.src[:, 0:T], io["src"].rearrange("(p t) -> p t", p=P)).then_inc(loaded, 16)
                sp.dma_start(S.w[:, :], io["edge_weight"].rearrange("(p t) -> p t", p=P)).then_inc(loaded, 16)
                sp.wait_ge(filled, 1)
                d2 = io["dst"].rearrange("(p t) -> p t", p=P)
                sp.dma_start(first[0:P - 1, 0:1], d2[1:P, 0:1]).then_inc(loaded, 16)
                sp.dma_start(first[1:P, 1:2], d2[0:P - 1, T - 1:T]).then_inc(loaded, 16)
                sp.dma_start(S.x[:, :, :], io["x"].rearrange("(t p) d -> p t d", p=P)).then_inc(loaded, 16)
                sp.dma_start(S.rsrc[:, :], io["edge_columns"][0]).then_inc(loaded, 16)
                sp.dma_start(S.rdst[:, :], io["edge_columns"][1]).then_inc(loaded, 16)

            @block.gpsimd
            def _(pool):
                pool.iota(S.iota_lo[:, :], [[1, LO]], base=0, channel_multiplier=0,
                          allow_small_or_imprecise_dtypes=True).then_inc(made, 1)
                pool.iota(S.row[:, :], [[0, 1]], base=0, channel_multiplier=1,
                          allow_small_or_imprecise_dtypes=True).then_inc(made, 1)
                pool.memset(S.ones[:, :], 1.0).then_inc(made, 1)
                pool.memset(S.ident[:, :], 0.0).then_inc(made, 1)
                pool.wait_ge(made, 4)
                pool.affine_select(out=S.ident[:, :], in_=S.ident[:, :], compare_op=ALU.not_equal, fill=1.0, base=0,
                                   pattern=[[-1, 128]], channel_multiplier=1).then_inc(made, 1)
                pool.affine_select(out=S.tri[:, :], in_=S.ones[:, :], compare_op=ALU.is_ge, fill=0.0, base=0,
                                   pattern=[[1, 128]], channel_multiplier=-1).then_inc(made, 1)
                pool.affine_select(out=S.below[:, :], in_=S.ones[:, :], compare_op=ALU.is_gt, fill=0.0, base=0,
                                   pattern=[[-1, 128]], channel_multiplier=1).then_inc(made, 1)

            @block.vector
            def _(v):
                link = linker(v, dve)
                link(v.memset(first[:, :], -1))
                v.memset(S.src[:, T:T + STEP], 0)
                v.sem_inc(filled, 1)
                v.wait_ge(loaded, 8 * 16)
                link(v.tensor_copy(S.dstf[:, :], S.dst[:, :]))
                link(v.tensor_copy(firstf[:, :], first[:, :]))
                link(v.memset(S.keep[:, :], 1.0))
                link(v.tensor_tensor(S.keep[:, 1:T], S.dstf[:, 1:T], S.dstf[:, 0:T - 1], ALU.is_equal))
                link(v.tensor_tensor(S.joins[:, 0:1], firstf[:, 1:2], S.dstf[:, 0:1], ALU.is_equal))
                link(v.tensor_tensor(S.joins[:, 1:2], firstf[:, 0:1], S.dstf[:, T - 1:T], ALU.is_equal))
                link(v.tensor_tensor(S.joins[:, 2:3], S.dstf[:, 0:1], S.dstf[:, T - 1:T], ALU.is_equal))
                link(v.scalar_tensor_tensor(S.goes_on[:, :], S.dstf[:, T - 1:T], 1.0, S.joins[:, 1:2],
                                            ALU.add, ALU.mult))
                link(v.tensor_scalar(S.goes_on[:, :], S.goes_on[:, :], 1.0, None, ALU.subtract))
                for lo, hi, dst in ((S.dst_lo, S.dst_hi, S.dst), (S.rdst_lo, S.rdst_hi, S.rdst)):
                    link(v.tensor_scalar(lo[:, :], dst[:, :], LO - 1, None, ALU.bitwise_and))
                    link(v.tensor_scalar(hi[:, :], dst[:, :], 7, None, ALU.logical_shift_right))


MV_STEPS = 8


def mean_and_var(link, stats, v, mean, var, diff, scale=1.0, eps=EPS):
    me, qe, mo, qo = [stats[:, :, i] for i in (1, 2, 4, 5)]
    link(v.tensor_tensor(mean, me, mo, ALU.add))
    link(v.tensor_scalar(mean, mean, 0.5, None, ALU.mult))
    link(v.tensor_tensor(diff, me, mo, ALU.subtract))
    link(v.scalar_tensor_tensor(diff, diff, 0.25, diff, ALU.mult, ALU.mult))
    link(v.tensor_tensor(var, qe, qo, ALU.add))
    link(v.tensor_scalar(var, var, 1.0 / D, None, ALU.mult))
    link(v.tensor_tensor(var, var, diff, ALU.add))
    link(v.tensor_scalar(var, var, scale, eps, ALU.mult, ALU.add))


def normalize(nc, tag, S, xn, xnT):
    with ExitStack() as stack:
        c = Scope(nc, stack, tag)
        stats = c.sb("stats", [P, NT, 6])
        mean = c.sb("mean", [P, NT])
        diff = c.sb("diff", [P, NT])
        var = c.sb("var", [P, NT])
        std = c.sb("std", [P, NT])
        rstd = c.sb("rstd", [P, NT])
        tile = c.sb("tile", [P, U, D])
        p_t = [c.ps(f"t{u}") for u in range(U)]
        counted, spread, rooted, normed, turned, copied = [
            c.sem(x) for x in ("counted", "spread", "rooted", "normed", "turned", "copied")]
        with nc.Block() as block:

            @block.vector
            def _(v):
                with v.Fori(0, NT) as t:
                    v.bn_stats(stats[:, bass.ds(t, 1), :].rearrange("p a b -> p (a b)"),
                               S.x[:, bass.ds(t, 1), :].rearrange("p a b -> p (a b)")).then_inc(counted, 1)
                v.wait_ge(counted, NT)
                mean_and_var(linker(v, spread), stats, v, mean[:, :], var[:, :], diff[:, :])
                v.wait_ge(rooted, 1)
                v.reciprocal(rstd[:, :], std[:, :]).then_inc(spread, 1)
                v.wait_ge(spread, MV_STEPS + 1)
                with v.Fori(0, NT - U + 1, U) as t0:
                    for u in range(U):
                        t = t0 + u
                        v.wait_ge(turned, t + 1)
                        v.tensor_scalar(tile[:, u, :], S.x[:, bass.ds(t, 1), :].rearrange("p a b -> p (a b)"),
                                        mean[:, bass.ds(t, 1)], rstd[:, bass.ds(t, 1)],
                                        ALU.subtract, ALU.mult).then_inc(normed, 1)
                        if xn is not None:
                            v.tensor_scalar(xn[:, bass.ds(t, 1), :].rearrange("p a b -> p (a b)"),
                                            S.x[:, bass.ds(t, 1), :].rearrange("p a b -> p (a b)"),
                                            mean[:, bass.ds(t, 1)], rstd[:, bass.ds(t, 1)],
                                            ALU.subtract, ALU.mult)

            @block.tensor
            def _(pe):
                pe.sem_inc(turned, U)
                with pe.Fori(0, NT - U + 1, U) as t0:
                    for u in range(U):
                        pe.wait_ge(normed, t0 + u + 1)
                        pe.wait_ge(copied, t0 + u + 1)
                        for k in range(KC):
                            mm = pe.transpose(p_t[u][:, k * P:(k + 1) * P], tile[:, u, k * 128:(k + 1) * 128],
                                              S.ident[0:P, 0:P])
                        mm.then_inc(turned, 1)

            @block.scalar
            def _(a):
                a.wait_ge(spread, MV_STEPS)
                a.activation(std[:, :], var[:, :], ACT.Sqrt).then_inc(rooted, 1)
                a.sem_inc(copied, U)
                with a.Fori(0, NT - U + 1, U) as t0:
                    for u in range(U):
                        a.wait_ge(turned, t0 + u + 1 + U)
                        a.activation(xnT[:, :, bass.ds((t0 + u) * P, P)],
                                     p_t[u][:, 0:KC * P].rearrange("q (k p) -> q k p", k=KC),
                                     ACT.Copy).then_inc(copied, 1)


class Walk:

    def __init__(self, c, S, tag):
        self.idx = c.sb("w_idx", [P, RING, G], I32)
        self.all_rows = c.sb("w_rows", [128, RING, G, D])
        self.rows = self.all_rows[0:P, :, :, :]
        self.sums = c.sb("w_sums", [P, RING, G, D])
        self.end = self.sums[:, RING - 1, G - 1, :]
        self.asked, self.walked, self.free = [c.sem(x) for x in ("w_asked", "w_walked", "w_free")]
        self.got = [S.gathers[f"{tag}_got{g}"] for g in range(RING)]
        self.sent = [c.sem(f"w_sent{g}") for g in range(RING)]

    def gather(self, pool, table):
        with pool.Fori(0, T - STEP + 1, STEP) as t0:
            for g in range(RING):
                pool.wait_ge(self.free, t0 // G + g + 1)
                pool.sem_inc(self.asked, 1)
                for j in range(G):
                    pool.indirect_dma_start(
                        out=self.rows[:, g, j, :], out_offset=None, in_=table,
                        in_offset=bass.IndirectOffsetOnAxis(ap=self.idx[:, g, j:j + 1], axis=0),
                    ).then_inc(self.got[g], 16)

    def begin(self, v, src):
        v.memset(self.end, 0.0).then_inc(self.walked, 1)
        v.tensor_copy(self.idx[:, :, :], src[:, 0:STEP].rearrange("p (g t) -> p g t", g=RING)).then_inc(self.free, RING)

    def walk(self, v, src, keep, weights, heads, begin, end, beside):
        with v.Fori(begin * STEP, (end - 1) * STEP + 1, STEP) as t0:
            link = linker(v, self.walked, (t0 // STEP) * (RING * (G + 1)) + 1)
            for g in range(RING):
                beside(g, t0 + g * G, t0 // G + g, t0 // STEP)
                v.wait_ge(self.got[g], (t0 // STEP) * (16 * G) + 16 * G)
                rows = self.rows[:, g, :, :]
                scale = weights[:, :, bass.ds(t0 + g * G, G)].rearrange("p h t -> p t h")
                link(v.tensor_tensor(rows.rearrange("p t (h d) -> p t h d", h=heads),
                                     rows.rearrange("p t (h d) -> p t h d", h=heads),
                                     scale.unsqueeze(3).to_broadcast([P, G, heads, D // heads]), ALU.mult))
                v.wait_ge(self.sent[g], (t0 // STEP) * 16 + 16)
                before = self.sums[:, (g - 1) % RING, G - 1, :]
                for j in range(G):
                    link(v.scalar_tensor_tensor(self.sums[:, g, j, :], before, keep[:, bass.ds(t0 + g * G + j, 1)],
                                                self.rows[:, g, j, :], ALU.mult, ALU.add))
                    before = self.sums[:, g, j, :]
                v.tensor_copy(self.idx[:, g, :], src[:, bass.ds(t0 + STEP + g * G, G)]).then_inc(self.free, 1)

    def send(self, sp, sums):
        for g in range(RING):
            sp.sem_inc(self.sent[g], 16)
        view = sums.rearrange("(p t) d -> p t d", p=P)
        with sp.Fori(0, T - STEP + 1, STEP) as t0:
            for g in range(RING):
                sp.wait_ge(self.free, t0 // G + g + 1 + RING)
                sp.dma_start(view[:, bass.ds(t0 + g * G, G), :], self.sums[:, g, :, :]).then_inc(self.sent[g], 16)
        for g in range(RING):
            sp.wait_ge(self.sent[g], 16 * (ITERS + 1))


def collect(nc, c, io, S, walk, agg, fetched, before_fetch, p_count=None):
    carry = c.sb("carry", [P, N])
    p_c = [c.ps(f"carry{i}") for i in range(4)]
    ready, carried, added, made = [c.sem(x) for x in ("c_ready", "c_carried", "c_added", "c_made")]
    if p_count is not None:
        ends = Ends(c)
    with nc.Block() as block:

        @block.sync
        def _(sp):
            if p_count is not None:
                ends.store(sp, io, S)

        @block.gpsimd
        def _(pool):
            pool.iota(carry[:, :], [[1, N]], base=0, channel_multiplier=0,
                      allow_small_or_imprecise_dtypes=True).then_inc(made, 1)
            before_fetch(pool)
            if p_count is not None:
                pool.wait_ge(ends.fetched, 32)
            for t in range(NT):
                pool.indirect_dma_start(
                    out=agg[:, t, :], out_offset=None, in_=io["sums"],
                    in_offset=bass.IndirectOffsetOnAxis(ap=S.last[:, t:t + 1], axis=0),
                    bounds_check=E - 1, oob_is_err=False).then_inc(fetched, 16)

        @block.vector
        def _(v):
            if p_count is not None:
                ends.find(v, p_count)
            v.wait_ge(made, 1)
            v.tensor_scalar(carry[:, :], carry[:, :], S.goes_on[:, 0:1], None, ALU.is_equal).then_inc(ready, 1)
            if p_count is not None:
                place_nodes(v, ends, S)
            v.wait_ge(fetched, 16 * NT)
            for t in range(NT):
                v.wait_ge(carried, t + 1)
                v.tensor_tensor(agg[:, t, :], agg[:, t, :], p_c[t % 4][0:P, 0:D], ALU.add).then_inc(added, 1)
            v.wait_ge(added, NT)

        @block.tensor
        def _(pe):
            if p_count is not None:
                ends.sum(pe, S, ends.degree, 0)
            pe.wait_ge(ready, 1)
            for t in range(4):
                pe.matmul(p_c[t][0:P, 0:D], carry[:, t * P:(t + 1) * P], walk.end,
                          start=True, stop=True).then_inc(carried, 1)
            if p_count is not None:
                ends.sum(pe, S, ends.degree2, 1)
            for t in range(4, NT):
                if t >= 4:
                    pe.wait_ge(added, t - 3)
                pe.matmul(p_c[t % 4][0:P, 0:D], carry[:, t * P:(t + 1) * P], walk.end,
                          start=True, stop=True).then_inc(carried, 1)


class Ends:

    def __init__(self, c):
        self.degree, self.degree2, self.total, self.upto, self.last, self.start = [
            c.sb(x, [128, HI]) for x in ("degree", "degree2", "total", "upto", "last", "start")]
        self.last_i = c.sb("last_i", [128, HI], I32)
        self.p_s = c.ps("ends")
        self.dve, self.asked, self.summed, self.stored, self.fetched = [
            c.sem(x) for x in ("e_dve", "e_asked", "e_summed", "e_stored", "e_fetched")]
        self.rlast_out = c.sem("e_rlast_out")
        self.placed, self.step = c.sem("e_placed"), c.sem("e_step")

    def sum(self, pe, S, degree, i):
        at = 128 * i
        pe.wait_ge(self.asked, i + 1)
        pe.matmul(self.p_s[:, at:at + HI], S.ones[:, :], degree[:, :], start=True, stop=True)
        pe.matmul(self.p_s[:, at + 64:at + 64 + HI], S.tri[:, :], degree[:, :], start=True,
                  stop=True).then_inc(self.summed, 1)

    def cumulate(self, v, link, i):
        at = 128 * i
        v.wait_ge(self.summed, i + 1)
        link(v.tensor_copy(self.total[:, :], self.p_s[:, at:at + HI]))
        link(v.memset(self.start[:, :], 1.0))
        link(v.tensor_tensor_scan(self.upto[:, :], self.start[:, :], self.total[:, :], 0.0, ALU.mult, ALU.add))
        link(v.tensor_tensor(self.upto[:, :], self.upto[:, :], self.total[:, :], ALU.subtract))
        link(v.tensor_tensor(self.upto[:, :], self.upto[:, :], self.p_s[:, at + 64:at + 64 + HI], ALU.add))

    def find(self, v, p_count):
        link = linker(v, self.dve)
        link(v.tensor_copy(self.degree[:, :], p_count))
        v.sem_inc(self.asked, 1)
        self.cumulate(v, link, 0)
        link(v.tensor_scalar(self.last[:, :], self.degree[:, :], 0.0, None, ALU.is_equal))
        link(v.scalar_tensor_tensor(self.last[:, :], self.last[:, :], 3.0e7, self.upto[:, :], ALU.mult, ALU.add))
        link(v.tensor_scalar(self.last[:, :], self.last[:, :], 1.0, None, ALU.subtract))
        link(v.tensor_copy(self.last_i[:, :], self.last[:, :]))
        v.sem_inc(self.stored, 1)

    def store(self, sp, io, S):
        sp.wait_ge(self.stored, 1)
        sp.dma_start(io["last"].rearrange("(h l) -> l h", l=LO), self.last_i[:, :]).then_inc(self.fetched, 16)
        sp.wait_ge(self.fetched, 16)
        sp.dma_start(S.last[:, :], io["last"][0:N].rearrange("(t p) -> p t", p=P)).then_inc(self.fetched, 16)
        sp.wait_ge(self.placed, 1)
        sp.dma_start(io["last2"].rearrange("(h l) -> l h", l=LO), S.rlast_i[:, :]).then_inc(self.rlast_out, 16)
        sp.wait_ge(self.rlast_out, 16)


def place_nodes(v, ends, S):
    step = linker(v, ends.step)
    for h in range(HI):
        ins = v.tensor_tensor_scan(S.count[:, :, h], S.ones[:, 0:1].to_broadcast([128, GT + 1]), S.count[:, :, h],
                                   0.0, ALU.mult, ALU.add)
    step(ins)
    step(v.tensor_scalar(ends.degree2[:, :], S.count[:, GT, :], 1.0, None, ALU.add))
    v.sem_inc(ends.asked, 1)
    ends.cumulate(v, step, 1)
    step(v.tensor_scalar(ends.last[:, :], ends.upto[:, :], 1.0, None, ALU.subtract))
    step(v.tensor_copy(S.rlast_i[:, :], ends.last[:, :]))
    step(v.tensor_tensor(ends.upto[:, :], ends.upto[:, :], ends.degree2[:, :], ALU.subtract))
    step(v.tensor_copy(S.loop_i[:, :], ends.upto[:, :]))
    step(v.tensor_scalar(ends.upto[:, :], ends.upto[:, :], 1.0, None, ALU.add))
    step(v.tensor_tensor(S.count[:, 0:GT, :], S.count[:, 0:GT, :],
                         ends.upto[:, :].unsqueeze(1).to_broadcast([128, GT, HI]), ALU.add))
    v.tensor_copy(S.rdstf[:, :], S.rdst[:, :]).then_inc(ends.placed, 1)


def layer0_graph(nc, io, S):
    with ExitStack() as stack:
        c = Scope(nc, stack, "g0")
        kvT = c.sb("kvT", [128, KC, D])
        knorm = c.sb("knorm", [128, KC])
        walk = Walk(c, S, "w0")
        with ExitStack() as s2:
            q2T = Scope(nc, s2, "m0").sb("q2T", [128, KC, N])
            project0(nc, io, S, kvT, knorm, q2T, walk)
            p_count = c.ps("count")
            mix0(nc, io, S, kvT, knorm, q2T, walk, p_count)
        agg = c.sb("agg", [P, NT, D])

        def clear(pool):
            pool.memset(agg[:, :, :], 0.0).then_inc(cleared, 1)
            pool.wait_ge(cleared, 1)

        cleared = c.sem("cleared")
        with ExitStack() as s3:
            collect(nc, Scope(nc, s3, "g0c"), io, S, walk, agg, S.gathers["g0_fetched"], clear, p_count[:, 0:HI])
        with nc.Block() as block:
            @block.vector
            def _(v):
                v.tensor_tensor(S.x[:, :, :], S.x[:, :, :], agg[:, :, :], ALU.add)


def project0(nc, io, S, kvT, knorm, q2T, walk):
    W4 = 4 * D
    with ExitStack() as stack:
        c = Scope(nc, stack, "p0")
        w = c.sb("w", [128, KC, W4])
        bias = c.sb("bias", [1, W4])
        qk, vy, sq = [x.rearrange("p g j d -> p (g j d)").rearrange("p (u n) -> p u n", u=U)
                      for x in (walk.rows[:, 0:2, :, :], walk.rows[:, 2:4, :, :], walk.sums[:, 0:2, :, :])]
        ksq = walk.sums[:, 2, :, :]
        xT = walk.all_rows[:, 4, :, 0:KC * P].rearrange("q u (k p) -> q u k p", k=KC)
        junk = c.sb("junk", [P, D])
        stats = c.sb("stats", [P, 2 * U, 6])
        mean, diff, var, r, root, f = [c.sb(x, [P, 2 * U]) for x in ("mean", "diff", "var", "r", "root", "f")]
        ss = c.sb("ss", [P, U])
        p_qk = [c.ps(f"qk{i}") for i in range(2)]
        p_vy = [c.ps(f"vy{i}") for i in range(2)]
        p_t = c.ps("t")
        p_kv = c.ps("kv")
        p_ss = c.ps("ss")
        p_n = c.ps("n")
        hot_lo = c.sb("hot_lo", [128, 2, GB, LO], BF16)
        hot_made, counted, count_out = [c.sem(x) for x in ("hot_made", "counted", "count_out")]
        names = ("loaded", "cleared", "staged", "multiplied", "evacuated", "table_out", "dve", "centred",
                 "squared", "sum_ready", "rooted", "scaled", "turned", "copied", "pooled", "group")
        (loaded, cleared, staged, multiplied, evacuated, table_out, dve, centred, squared, sum_ready, rooted,
         scaled, turned, copied, pooled, group) = [c.sem(x) for x in names]
        with nc.Block() as block:

            @block.sync
            def _(sp):
                sp.dma_start(w[:, :, 0:3 * D], io["L0_mix_W_qkv"].rearrange("(k p) n -> p k n", p=128)).then_inc(loaded, 16)
                sp.dma_start(w[:, :, 3 * D:W4], io["L0_gnn_W"].rearrange("(k p) n -> p k n", p=128)).then_inc(loaded, 16)
                sp.wait_ge(cleared, 1)
                sp.dma_start(bias[0:1, 0:3 * D], io["L0_mix_b_qkv"].rearrange("(a n) -> a n", a=1)).then_inc(loaded, 16)
                sp.sem_inc(table_out, 16)
                table = io["table"].rearrange("(t p) d -> p t d", p=P)
                with sp.Fori(0, NT - U + 1, U) as t0:
                    sp.wait_ge(evacuated, t0 + U + 2)
                    sp.dma_start(table[:, bass.ds(t0, U), :], vy[:, :, D:2 * D]).then_inc(table_out, 16)
                sp.wait_ge(table_out, 16 * (NT // U + 1))

            @block.gpsimd
            def _(pool):
                pool.memset(bias[:, :], 0.0).then_inc(cleared, 1)
                with pool.Fori(0, NT - U + 1, U) as t0:
                    for u in range(U):
                        pool.wait_ge(multiplied, t0 + u + 1)
                        pool.tensor_copy(xT[:, u, :, :], S.xnT[:, :, bass.ds((t0 + u) * P, P)]).then_inc(staged, 1)

            @block.tensor
            def _(pe):
                pe.wait_ge(loaded, 3 * 16)
                pe.wait_ge(dve, 2)
                pe.sem_inc(multiplied, U)
                pe.sem_inc(group, 1)
                pe.sem_inc(counted, 2)
                with pe.Fori(0, NT - U + 1, U) as t0:
                    for u in range(U):
                        pe.wait_ge(staged, t0 + u + 1)
                        pe.wait_ge(evacuated, t0 + u + (2 if u == 0 else 1))
                        for o, (p_o, lo) in enumerate(((p_qk, 0), (p_vy, 2 * D))):
                            for k in range(KC):
                                pe.matmul(p_o[u % 2][0:P, :], xT[:, u, k, :], w[:, k, lo:lo + 2 * D],
                                          start=(k == 0), stop=False)
                            mm = pe.matmul(p_o[u % 2][0:P, :], S.ones[0:1, 0:P], bias[0:1, lo:lo + 2 * D],
                                           start=False, stop=True)
                        mm.then_inc(multiplied, 1)
                    for b in range(QB):
                        nb = (t0 // U) * QB + b
                        pe.wait_ge(hot_made, nb + 1)
                        pe.wait_ge(count_out, nb + 1)
                        for j in range(GB):
                            mm = pe.matmul(p_n[:, j * HI:(j + 1) * HI], hot_lo[:, b % 2, j, :],
                                           S.hot_hi[:, bass.ds(nb * GB + j, 1), :].rearrange("p a b -> p (a b)"),
                                           start=True, stop=True)
                        mm.then_inc(counted, 1)
                    pe.wait_ge(scaled, t0 // U + 1)
                    for u in range(U):
                        pe.wait_ge(copied, t0 + u + 1)
                        for k in range(KC):
                            mm = pe.transpose(p_t[:, k * P:(k + 1) * P], sq[:, u, k * 128:(k + 1) * 128],
                                              S.ident[0:P, 0:P])
                        mm.then_inc(turned, 1)
                        for k in range(KC):
                            pe.matmul(p_kv[:, k * D:(k + 1) * D], vy[:, u, k * 128:(k + 1) * 128],
                                      sq[:, u, D:2 * D], start=False, stop=True, skip_group_check=True)
                            mm = pe.matmul(p_ss[:, k:k + 1], ksq[:, u, k * 128:(k + 1) * 128], S.ones[0:P, 0:1],
                                           start=False, stop=True, skip_group_check=True)
                    mm.then_inc(group, 1)

            @block.scalar
            def _(a):
                a.sem_inc(evacuated, 2)
                a.sem_inc(copied, 1)
                a.sem_inc(count_out, 1)
                with a.Fori(0, NT - U + 1, U) as t0:
                    a.wait_ge(group, t0 // U + 1)
                    a.wait_ge(table_out, 16 * (t0 // U) + 16)
                    for u in range(U):
                        a.wait_ge(multiplied, t0 + u + 1 + U)
                        a.activation(qk[:, u, :], p_qk[u % 2][0:P, :], ACT.Copy)
                        a.activation(vy[:, u, :], p_vy[u % 2][0:P, :], ACT.Copy).then_inc(evacuated, 1)
                    for b in range(QB):
                        nb = (t0 // U) * QB + b
                        a.wait_ge(counted, nb + 1 + 2)
                        a.activation(S.count[:, bass.ds(nb * GB + 1, GB), :].rearrange("p a b -> p (a b)"),
                                     p_n[:, 0:GB * HI], ACT.Copy).then_inc(count_out, 1)
                    a.wait_ge(centred, t0 // U + 1)
                    for j in range(2 * U):
                        half = qk[:, j // 2, (j % 2) * D:(j % 2 + 1) * D]
                        a.activation(sq[:, j // 2, (j % 2) * D:(j % 2 + 1) * D], half, ACT.Square,
                                     bias=mean[:, j:j + 1]).then_inc(squared, 1)
                    a.wait_ge(sum_ready, t0 // U + 1)
                    a.activation(root[:, 0:U], ss[:, :], ACT.Sqrt).then_inc(rooted, 1)
                    for u in range(U):
                        a.wait_ge(turned, t0 + u + 1)
                        a.activation(q2T[:, :, bass.ds((t0 + u) * P, P)],
                                     p_t[:, 0:KC * P].rearrange("q (k p) -> q k p", k=KC),
                                     ACT.Copy).then_inc(copied, 1)

            @block.vector
            def _(v):
                link = linker(v, dve)
                link(v.memset(p_kv[:, :], 0.0))
                link(v.memset(p_ss[:, :], 0.0))
                v.memset(S.count[:, 0, :], 0.0)
                per = 2 * U + MV_STEPS + 2 + U + 4 + 2 * U + 1
                with v.Fori(0, NT - U + 1, U) as t0:
                    base = (t0 // U) * per + 2
                    link = linker(v, dve, base)
                    for b in range(QB):
                        nb = (t0 // U) * QB + b
                        v.wait_ge(counted, nb + 1)
                        v.tensor_tensor(hot_lo[:, b % 2, :, :],
                                        S.rdst_lo[:, bass.ds(nb * GB, GB)].unsqueeze(2).to_broadcast([128, GB, LO]),
                                        S.iota_lo[:, :].unsqueeze(1).to_broadcast([128, GB, LO]), ALU.is_equal)
                        v.tensor_tensor(S.hot_hi[:, bass.ds(nb * GB, GB), :],
                                        S.rdst_hi[:, bass.ds(nb * GB, GB)].unsqueeze(2).to_broadcast([128, GB, HI]),
                                        S.iota_lo[:, 0:HI].unsqueeze(1).to_broadcast([128, GB, HI]),
                                        ALU.is_equal).then_inc(hot_made, 1)
                    v.wait_ge(evacuated, t0 + U + 2)
                    for j in range(2 * U):
                        link(v.bn_stats(stats[:, j, :], qk[:, j // 2, (j % 2) * D:(j % 2 + 1) * D]))
                    mean_and_var(link, stats, v, mean[:, :], var[:, :], diff[:, :], float(D), 1e-7)
                    link(v.tensor_scalar(mean[:, :], mean[:, :], -1.0, None, ALU.mult))
                    link(v.reciprocal(r[:, :], var[:, :]))
                    v.sem_inc(centred, 1)
                    v.wait_ge(squared, (t0 // U) * (2 * U) + 2 * U)
                    for u in range(U):
                        link(v.tensor_tensor_reduce(junk[:, :], sq[:, u, 0:D], sq[:, u, 0:D], 1.0, 0.0,
                                                    ALU.mult, ALU.add, ss[:, u:u + 1]))
                    v.sem_inc(sum_ready, 1)
                    v.wait_ge(rooted, t0 // U + 1)
                    rq = r[:, 0:2 * U:2]
                    link(v.tensor_tensor(f[:, 0:U], root[:, 0:U], rq, ALU.mult))
                    link(v.tensor_scalar(f[:, 0:U], f[:, 0:U], 1e-12, None, ALU.max))
                    link(v.reciprocal(f[:, 0:U], f[:, 0:U]))
                    link(v.tensor_tensor(f[:, 0:U], f[:, 0:U], rq, ALU.mult))
                    for u in range(U):
                        link(v.tensor_scalar(sq[:, u, 0:D], sq[:, u, 0:D], f[:, u:u + 1], None, ALU.mult))
                        link(v.tensor_scalar(sq[:, u, D:2 * D], sq[:, u, D:2 * D], r[:, 2 * u + 1:2 * u + 2], None,
                                             ALU.mult))
                    link(v.tensor_tensor(ksq[:, :, :], sq[:, :, D:2 * D], sq[:, :, D:2 * D], ALU.mult))
                    v.sem_inc(scaled, 1)
                v.wait_ge(group, NT // U + 1)
                v.tensor_copy(kvT[:, :, :], p_kv[:, :].rearrange("p (k n) -> p k n", k=KC))
                v.tensor_copy(knorm[:, :], p_ss[:, 0:KC])


def mix0(nc, io, S, kvT, knorm, q2T, walk, p_count):
    TWICE = NT - ITERS
    SPANS = ((0, TWICE, {0: lambda i: i * 2, 2: lambda i: i * 2 + 1}), (TWICE, ITERS, {2: lambda i: i + TWICE}))
    SLOT = {0: 0, 2: 1}
    with ExitStack() as stack:
        c = Scope(nc, stack, "x0")
        wout = c.sb("wout", [128, KC, D])
        wvT = c.sb("wvT", [128, KC, D])
        bv = c.sb("bv", [128, KC])
        rows = c.sb("rows", [1, 3, D])
        root = c.sb("root", [128, KC])
        kvw = c.sb("kvw", [128, KC, D])
        wvw = c.sb("wvw", [128, KC, D])
        xq = c.sb("xq", [128, 2, 2 * KC, P])
        p_a, p_b, p_r = c.ps("a"), c.ps("b"), c.ps("r")
        p_o = [c.ps(f"o{i}") for i in range(2)]
        hot_lo = c.sb("hot_lo", [P, 2, G, LO], BF16)
        hot_hi = c.sb("hot_hi", [P, 2, G, HI], BF16)
        names = ("loaded", "small", "rooted", "dve", "staged", "multiplied", "added", "hot_made", "counted", "zeroed")
        loaded, small, rooted, dve, staged, multiplied, added, hot_made, counted, zeroed = [c.sem(x) for x in names]
        with nc.Block() as block:

            @block.sync
            def _(sp):
                sp.dma_start(wout[:, :, :], io["L0_mix_W_out"].rearrange("(k p) n -> p k n", p=128)).then_inc(loaded, 16)
                sp.dma_start(wvT[:, :, :], io["L0_mix_W_v_T"].rearrange("(k p) n -> p k n", p=128)).then_inc(loaded, 16)
                sp.dma_start(bv[:, :], io["L0_mix_b_qkv"][2 * D:3 * D].rearrange("(k p) -> p k", p=128)).then_inc(loaded, 16)
                sp.dma_start(rows[0:1, 0, :], io["L0_mix_b_out"].rearrange("(a n) -> a n", a=1)).then_inc(loaded, 16)
                sp.dma_start(rows[0:1, 1, :], io["L0_gnn_b"].rearrange("(a n) -> a n", a=1)).then_inc(loaded, 16)
                walk.send(sp, io["sums"])

            @block.gpsimd
            def _(pool):
                walk.gather(pool, io["table"])

            @block.tensor
            def _(pe):
                pe.wait_ge(loaded, 5 * 16)
                for m in range(KC):
                    for k in range(KC):
                        pe.matmul(p_a[:, m * D:(m + 1) * D], kvT[:, k, m * 128:(m + 1) * 128], wout[:, k, :],
                                  start=(k == 0), stop=(k == KC - 1))
                    for k in range(KC):
                        pe.matmul(p_b[:, m * D:(m + 1) * D], wvT[:, k, m * 128:(m + 1) * 128], wout[:, k, :],
                                  start=(k == 0), stop=(k == KC - 1))
                for k in range(KC):
                    mm = pe.matmul(p_r[0:1, 0:D], bv[:, k:k + 1], wout[:, k, :], start=(k == 0), stop=(k == KC - 1))
                mm.then_inc(small, 1)
                pe.wait_ge(dve, 8)
                pe.sem_inc(multiplied, 2)
                pe.sem_inc(counted, 2)
                pe.wait_ge(zeroed, 1)
                for begin, end, tile in SPANS:
                    with pe.Fori(begin * STEP, (end - 1) * STEP + 1, STEP) as t0:
                        for g in range(RING):
                            pe.wait_ge(hot_made, t0 // G + g + 1)
                            for j in range(G):
                                mm = pe.matmul(p_count[:, 0:HI], hot_lo[:, g % 2, j, :], hot_hi[:, g % 2, j, :],
                                               start=False, stop=True, skip_group_check=True)
                            mm.then_inc(counted, 1)
                            if g not in tile:
                                continue
                            t, slot = tile[g](t0 // STEP), SLOT[g]
                            pe.wait_ge(staged, t + 1)
                            pe.wait_ge(added, t + 1)
                            o = p_o[slot][0:P, 0:D]
                            for k in range(KC):
                                pe.matmul(o, xq[:, slot, k, :], wvw[:, k, :], start=(k == 0), stop=False)
                                pe.matmul(o, xq[:, slot, KC + k, :], kvw[:, k, :], start=False, stop=False)
                            pe.matmul(o, S.ones[0:1, 0:P], rows[0:1, 2, :], start=False,
                                      stop=True).then_inc(multiplied, 1)

            @block.scalar
            def _(a):
                a.activation(root[:, :], knorm[:, :], ACT.Sqrt).then_inc(rooted, 1)
                for begin, end, tile in SPANS:
                    with a.Fori(begin, end) as i:
                        for g in tile:
                            t, slot = tile[g](i), SLOT[g]
                            a.wait_ge(multiplied, t + 2)
                            a.activation(xq[:, slot, 0:KC, :], S.xnT[:, :, bass.ds(t * P, P)], ACT.Copy)
                            a.activation(xq[:, slot, KC:2 * KC, :], q2T[:, :, bass.ds(t * P, P)],
                                         ACT.Copy).then_inc(staged, 1)

            @block.vector
            def _(v):
                link = linker(v, dve)
                walk.begin(v, S.src)
                v.wait_ge(rooted, 1)
                link(v.tensor_scalar(root[:, :], root[:, :], 1e-12, None, ALU.max))
                link(v.reciprocal(root[:, :], root[:, :]))
                link(v.tensor_scalar(root[:, :], root[:, :], float(N) ** -0.5, None, ALU.mult))
                v.wait_ge(small, 1)
                for k in range(KC):
                    link(v.tensor_scalar(kvw[:, k, :], p_a[:, k * D:(k + 1) * D], root[:, k:k + 1], None, ALU.mult))
                link(v.tensor_copy(wvw[:, :, :], p_b[:, :].rearrange("p (k n) -> p k n", k=KC)))
                link(v.tensor_tensor(rows[0:1, 2, :], rows[0:1, 0, :], rows[0:1, 1, :], ALU.add))
                link(v.tensor_tensor(rows[0:1, 2, :], rows[0:1, 2, :], p_r[0:1, 0:D], ALU.add))
                v.memset(p_count[:, 0:HI], 0.0).then_inc(zeroed, 1)
                v.sem_inc(added, 1)

                def one_hot(g, t, n):
                    v.wait_ge(counted, n + (2 if g == 0 else 1))
                    v.tensor_tensor(hot_lo[:, g % 2, :, :],
                                    S.dst_lo[:, bass.ds(t, G)].unsqueeze(2).to_broadcast([P, G, LO]),
                                    S.iota_lo[0:P, :].unsqueeze(1).to_broadcast([P, G, LO]), ALU.is_equal)
                    v.tensor_tensor(hot_hi[:, g % 2, :, :],
                                    S.dst_hi[:, bass.ds(t, G)].unsqueeze(2).to_broadcast([P, G, HI]),
                                    S.iota_lo[0:P, 0:HI].unsqueeze(1).to_broadcast([P, G, HI]),
                                    ALU.is_equal).then_inc(hot_made, 1)

                for begin, end, tile in SPANS:

                    def beside(g, t, n, i):
                        one_hot(g, t, n)
                        if g - 1 in tile:
                            m = tile[g - 1](i)
                            xt = S.x[:, bass.ds(m, 1), :].rearrange("p a b -> p (a b)")
                            v.wait_ge(multiplied, m + 1 + 2)
                            v.tensor_tensor(xt, xt, p_o[SLOT[g - 1]][0:P, 0:D], ALU.add).then_inc(added, 1)

                    walk.walk(v, S.src, S.keep, S.w[:, :].unsqueeze(1), 1, begin, end, beside)
                v.wait_ge(counted, T // G + 2)


def layer0_experts(nc, io, S):
    with ExitStack() as stack:
        c = Scope(nc, stack, "e0")
        hot = c.sb("hot", [P, NT, NX])
        hotT = c.sb("hotT", [NX, N])
        off = c.sb("off", [NX, N], BF16)
        route0(nc, io, S, hot, hotT, off)
        experts0(nc, io, S, hotT, off)


def route0(nc, io, S, hot, hotT, off):
    with ExitStack() as stack:
        c = Scope(nc, stack, "r0")
        rw = c.sb("rw", [128, KC, NX])
        rb = c.sb("rb", [1, NX])
        logits = c.sb("logits", [P, NT, NX])
        order = c.sb("order", [P, NX])
        top = c.sb("top", [P, NT])
        half = 512 // NX
        p_l = [c.ps(f"l{i}") for i in range(2)]
        p_t = [c.ps(f"t{i}") for i in range(2)]
        loaded, made, routed, dve, turned, copied = [
            c.sem(x) for x in ("loaded", "made", "routed", "dve", "turned", "copied")]
        with nc.Block() as block:

            @block.sync
            def _(sp):
                sp.dma_start(rw[:, :, :], io["L0_ffn_router_w"].rearrange("(k p) n -> p k n", p=128)).then_inc(loaded, 16)
                sp.dma_start(rb[:, :], io["L0_ffn_router_b"].rearrange("(a n) -> a n", a=1)).then_inc(loaded, 16)

            @block.gpsimd
            def _(pool):
                pool.iota(order[:, :], [[-1, NX]], base=NX, channel_multiplier=0,
                          allow_small_or_imprecise_dtypes=True).then_inc(made, 1)

            @block.tensor
            def _(pe):
                pe.wait_ge(loaded, 32)
                for t in range(NT):
                    o = p_l[t // half][0:P, (t % half) * NX:(t % half + 1) * NX]
                    for k in range(KC):
                        pe.matmul(o, S.xnT[:, k, t * P:(t + 1) * P], rw[:, k, :], start=(k == 0), stop=False)
                    mm = pe.matmul(o, S.ones[0:1, 0:P], rb[0:1, :], start=False, stop=True)
                mm.then_inc(routed, 1)
                pe.wait_ge(dve, 7)
                for t in range(NT):
                    if t >= 2:
                        pe.wait_ge(copied, t - 1)
                    pe.transpose(p_t[t % 2][0:NX, 0:P], hot[:, t, :], S.ident[0:P, 0:P]).then_inc(turned, 1)

            @block.scalar
            def _(a):
                for t in range(NT):
                    a.wait_ge(turned, t + 1)
                    a.activation(hotT[:, t * P:(t + 1) * P], p_t[t % 2][0:NX, 0:P], ACT.Copy).then_inc(copied, 1)

            @block.vector
            def _(v):
                link = linker(v, dve)
                v.wait_ge(routed, 1)
                v.wait_ge(made, 1)
                link(v.tensor_copy(logits[:, 0:half, :], p_l[0][0:P, 0:half * NX].rearrange("p (t e) -> p t e", e=NX)))
                link(v.tensor_copy(logits[:, half:NT, :],
                                   p_l[1][0:P, 0:(NT - half) * NX].rearrange("p (t e) -> p t e", e=NX)))
                ranked = order[:, :].unsqueeze(1).to_broadcast([P, NT, NX])
                link(v.tensor_reduce(top[:, :], logits[:, :, :], AX.X, ALU.max))
                link(v.tensor_tensor(hot[:, :, :], logits[:, :, :], top[:, :].unsqueeze(2).to_broadcast([P, NT, NX]),
                                     ALU.is_equal))
                link(v.tensor_tensor(hot[:, :, :], hot[:, :, :], ranked, ALU.mult))
                link(v.tensor_reduce(top[:, :], hot[:, :, :], AX.X, ALU.max))
                link(v.tensor_tensor(hot[:, :, :], ranked, top[:, :].unsqueeze(2).to_broadcast([P, NT, NX]),
                                     ALU.is_equal))
                v.wait_ge(copied, NT)
                link(v.tensor_scalar(off[:, :], hotT[:, :], 1.0, BIG, ALU.subtract, ALU.mult))


def experts0(nc, io, S, hotT, off):
    B = U * P
    CUT = ((0, 3 * P, 0), (3 * P, B, 512))
    NB = NT // U
    with ExitStack() as stack:
        c = Scope(nc, stack, "f0")
        w1 = c.sb("w1", [128, KC, NX * HX])
        w2 = c.sb("w2", [128, NC0, D])
        b1 = c.sb("b1", [128, NC0])
        b2 = c.sb("b2", [NX, D])
        sel = c.sb("sel", [NX, NC0, 2, HX], BF16)
        hot = c.sb("hot", [NX, B])
        hid = c.sb("hid", [128, 2, B])
        p_h = [c.ps(f"h{i}", (128, 1024)) for i in range(2)]
        p_o = c.ps("o", (128, 1536))
        sort = Places(c, S)
        names = ("loaded", "made", "hidden", "active", "staged", "done", "added")
        loaded, made, hidden, active, staged, done, added = [c.sem(x) for x in names]
        with nc.Block() as block:

            @block.sync
            def _(sp):
                sp.dma_start(w1[:, :, :], io["L0_ffn_W1"].rearrange("(k p) n -> p k n", p=128)).then_inc(loaded, 16)
                sp.dma_start(w2[:, :, :], io["L0_ffn_W2"].rearrange("(c p) n -> p c n", p=128)).then_inc(loaded, 16)
                sp.dma_start(b1[:, :], io["L0_ffn_b1"]).then_inc(loaded, 16)
                sp.dma_start(b2[:, :], io["L0_ffn_b2"]).then_inc(loaded, 16)
                sort.load_rows(sp, io)

            @block.gpsimd
            def _(pool):
                pool.memset(sel[:, :, :, :], 0.0).then_inc(made, 1)
                pool.wait_ge(made, 1)
                pool.affine_select(out=sel[:, :, :, :], in_=sel[:, :, :, :], compare_op=ALU.not_equal, fill=1.0,
                                   base=0, pattern=[[-2, NC0], [-1, 2], [0, HX]], channel_multiplier=1).then_inc(made, 1)
                sort.scatter(pool, io, S)

            @block.tensor
            def _(pe):
                pe.wait_ge(loaded, 4 * 16)
                pe.wait_ge(made, 2)
                with pe.Fori(0, NT - U + 1, U) as t0:
                    n0 = t0 * P

                    def make_hidden(ch):
                        pe.wait_ge(active, (t0 // U) * NC0 + ch + 1)
                        for lo, hi, at in CUT:
                            o = p_h[ch % 2][:, at:at + hi - lo]
                            for k in range(KC):
                                pe.matmul(o, w1[:, k, ch * 128:(ch + 1) * 128], S.xnT[:, k, bass.ds(n0 + lo, hi - lo)],
                                          start=(k == 0), stop=False)
                            mm = pe.matmul(o, sel[:, ch, :, :].rearrange("e a h -> e (a h)"),
                                           off[:, bass.ds(n0 + lo, hi - lo)], start=False, stop=True)
                        mm.then_inc(hidden, 1)

                    def add_output(ch):
                        pe.wait_ge(active, (t0 // U) * NC0 + ch + 3)
                        for u in range(U):
                            mm = pe.matmul(p_o[0:P, u * D:(u + 1) * D], hid[:, ch % 2, u * P:(u + 1) * P],
                                           w2[:, ch, :], start=False, stop=(ch == NC0 - 1), skip_group_check=True)
                        mm.then_inc(done, 1)

                    make_hidden(0)
                    pe.wait_ge(staged, t0 // U + 1)
                    for u in range(U):
                        pe.matmul(p_o[0:P, u * D:(u + 1) * D], hot[:, u * P:(u + 1) * P], b2[:, :],
                                  start=False, stop=False, skip_group_check=True)
                    for ch in range(NC0):
                        if ch + 1 < NC0:
                            make_hidden(ch + 1)
                        add_output(ch)
                        if ch % (NC0 // QB) == 1:
                            sort.fetch(pe, S, t0 // U, ch // (NC0 // QB))

            @block.scalar
            def _(a):
                a.wait_ge(loaded, 4 * 16)
                a.sem_inc(active, 2)
                a.sem_inc(done, 2)
                with a.Fori(0, NT - U + 1, U) as t0:
                    for ch in range(NC0):
                        a.wait_ge(hidden, (t0 // U) * NC0 + ch + 1)
                        a.wait_ge(done, (t0 // U) * NC0 + ch + 1)
                        for lo, hi, at in CUT:
                            ins = a.activation(hid[:, ch % 2, lo:hi], p_h[ch % 2][:, at:at + hi - lo], ACT.Relu,
                                               bias=b1[:, ch:ch + 1])
                        ins.then_inc(active, 1)

            @block.vector
            def _(v):
                v.sem_inc(added, 1)
                sort.begin(v)
                with v.Fori(0, NT - U + 1, U) as t0:
                    v.wait_ge(added, t0 + 1)
                    v.memset(p_o[0:P, 0:U * D], 0.0)
                    v.tensor_copy(hot[:, :], hotT[:, bass.ds(t0 * P, B)]).then_inc(staged, 1)
                    for b in range(QB):
                        sort.rank_and_place(v, S, t0 // U, b)
                    v.wait_ge(done, (t0 // U) * NC0 + NC0 + 2)
                    for u in range(U):
                        xt = S.x[:, bass.ds(t0 + u, 1), :].rearrange("p a b -> p (a b)")
                        v.scalar_tensor_tensor(xt, p_o[0:P, u * D:(u + 1) * D], 0.0, xt,
                                               ALU.max, ALU.add).then_inc(added, 1)


class Places:

    def __init__(self, c, S):
        self.row = c.sb("z_row", [128, 2, GB * 128], I32)
        self.row_lo = c.sb("z_row_lo", [128, GB * 128], I32)
        self.hotT = c.sb("z_hotT", [128, GB * 128])
        self.junk = c.sb("z_junk", [128, GB, 128], BF16)
        self.picked = c.sb("z_picked", [128, GB, HI])
        self.place = c.sb("z_place", [128, GB])
        self.rank = c.sb("z_rank", [128, GB])
        self.place_i = c.sb("z_place_i", [128, 2, GB], I32)
        self.record = c.sb("z_record", [128, 2, GB, 2], I32)
        self.loop_rec = c.sb("z_loop_rec", [128, HI, 2], I32)
        self.pad = c.sb("z_pad", [1, GP - GN, 2], I32)
        self.p_g = c.ps("z_g")
        self.hot_made, self.fetched, self.step, self.ready, self.used, self.made, self.pads, self.asked = [
            c.sem("z_" + x) for x in ("hot_made", "fetched", "step", "ready", "used", "made", "pads", "asked")]
        self.rows_in = [c.sem(f"z_rows_in{i}") for i in range(2)]
        self.sent = [S.gathers[f"so_sent{i}"] for i in range(2)]
        self.loops_sent = S.gathers["so_loops_sent"]

    def load_rows(self, sp, io):
        sp.wait_ge(self.made, 3)
        sp.dma_start(io["sorted"][GN:GP, :].rearrange("(a n) c -> a n c", a=1), self.pad[:, :, :]).then_inc(self.pads, 16)
        with sp.Fori(0, GT // GB - 1, 2) as n0:
            for i in range(2):
                sp.wait_ge(self.used, n0 + i + 1)
                sp.dma_start(self.row[:, i, :], io["edge_row"][:, bass.ds((n0 + i) * GB * 128, GB * 128)]
                             .to_broadcast([128, GB * 128])).then_inc(self.rows_in[i], 16)
        sp.wait_ge(self.pads, 16)

    def fetch(self, pe, S, i, b):
        n = i * QB + b
        pe.wait_ge(self.hot_made, n + 1)
        pe.wait_ge(self.used, n + 2)
        for j in range(GB):
            mm = pe.matmul(self.p_g[:, j * HI:(j + 1) * HI], self.hotT[:, j * 128:(j + 1) * 128],
                           S.count[:, bass.ds(n * GB + j, 1), :].rearrange("p a b -> p (a b)"), start=True, stop=True)
        mm.then_inc(self.fetched, 1)

    def begin(self, v):
        v.sem_inc(self.used, 2)

    def rank_and_place(self, v, S, i, b):
        n = i * QB + b
        link = linker(v, self.step, n * 6)
        v.wait_ge(self.rows_in[b % 2], (i * (QB // 2) + b // 2) * 16 + 16)
        link(v.tensor_scalar(self.row_lo[:, :], self.row[:, b % 2, :], LO - 1, None, ALU.bitwise_and))
        v.tensor_scalar(self.hotT[:, :], self.row_lo[:, :], S.row[:, 0:1], None, ALU.is_equal).then_inc(self.hot_made, 1)
        for j in range(GB):
            ins = v.scalar_tensor_tensor(self.junk[:, j, :], self.row[:, b % 2, j * 128:(j + 1) * 128],
                                         S.rdstf[:, bass.ds(n * GB + j, 1)], S.below[:, :], ALU.is_equal, ALU.mult,
                                         accum_out=self.rank[:, j:j + 1])
        link(ins)
        v.wait_ge(self.fetched, n + 1)
        link(v.tensor_tensor(self.picked[:, :, :], self.p_g[:, 0:GB * HI].rearrange("p (a b) -> p a b", b=HI),
                             S.hot_hi[:, bass.ds(n * GB, GB), :], ALU.mult))
        link(v.tensor_reduce(self.place[:, :], self.picked[:, :, :], AX.X, ALU.add))
        link(v.tensor_tensor(self.place[:, :], self.place[:, :], self.rank[:, :], ALU.add))
        v.wait_ge(self.asked, n + 1)
        v.tensor_copy(self.record[:, b % 2, :, 0], S.rsrc[:, bass.ds(n * GB, GB)])
        v.tensor_copy(self.record[:, b % 2, :, 1], S.rdst[:, bass.ds(n * GB, GB)])
        link(v.tensor_copy(self.place_i[:, b % 2, :], self.place[:, :]))
        v.sem_inc(self.ready, 1)
        v.sem_inc(self.used, 1)

    def scatter(self, pool, io, S):
        pool.iota(self.loop_rec[:, :, :], [[LO, HI], [0, 2]], base=0, channel_multiplier=1).then_inc(self.made, 1)
        pool.memset(self.pad[:, :, 0:1], 0).then_inc(self.made, 1)
        pool.memset(self.pad[:, :, 1:2], N).then_inc(self.made, 1)
        pool.wait_ge(self.made, 3)
        for h in range(HI):
            pool.indirect_dma_start(
                out=io["sorted"], out_offset=bass.IndirectOffsetOnAxis(ap=S.loop_i[:, h:h + 1], axis=0),
                in_=self.loop_rec[:, h, :], in_offset=None,
                bounds_check=GN - 1, oob_is_err=False).then_inc(self.loops_sent, 16)
        pool.sem_inc(self.asked, 2)
        with pool.Fori(0, GT // GB - 1, 2) as n0:
            for i in range(2):
                pool.wait_ge(self.ready, n0 + i + 1)
                pool.sem_inc(self.made, 1)
                for j in range(GB):
                    pool.indirect_dma_start(
                        out=io["sorted"], out_offset=bass.IndirectOffsetOnAxis(ap=self.place_i[:, i, j:j + 1], axis=0),
                        in_=self.record[:, i, j, :], in_offset=None,
                        bounds_check=GN - 1, oob_is_err=False).then_inc(self.sent[i], 16)
                pool.wait_ge(self.sent[i], (n0 // 2) * (16 * GB) + 16 * GB)
                pool.sem_inc(self.asked, 1)
        pool.wait_ge(self.loops_sent, 16 * HI)


def segment_scan(nc, tag, S, out, src, keep, joins, cols, op, reverse=False):
    C = src.shape[1]
    add = op == ALU.add
    combine = ALU.mult if add else ALU.add
    zero = 0.0 if add else -BIG
    with ExitStack() as stack:
        c = Scope(nc, stack, tag)
        gate = c.sb("gate", [P, cols + 1])
        ends = c.sb("ends", [P, C])
        through = c.sb("through", [P, C])
        enters = c.sb("enters", [P, 1])
        endsT = c.sb("endsT", [C, P])
        throughT = c.sb("throughT", [C, P])
        chain = c.sb("chain", [C, P])
        shifted = c.sb("shifted", [C, P])
        begin = c.sb("begin", [P, C])
        p_a, p_b, p_c = c.ps("a"), c.ps("b"), c.ps("c")
        dve, pe_done = c.sem("dve"), c.sem("turned")

        def turned(ap):
            return ap[:, ::-1] if reverse else ap

        with nc.Block() as block:

            @block.vector
            def _(v):
                link = linker(v, dve)
                link(v.memset(gate[:, cols:cols + 1], 1.0))
                link(v.tensor_copy(gate[:, 0:cols], keep))
                join = joins[:, 1:2] if reverse else joins[:, 0:1]
                link(v.tensor_tensor(through[:, 0:1], join, joins[:, 2:3], ALU.mult))
                link(v.tensor_copy(enters[:, :], join))
                if not add:
                    for flag in (gate[:, :], through[:, 0:1], enters[:, :]):
                        link(v.tensor_scalar(flag, flag, 1.0, BIG, ALU.subtract, ALU.mult))
                if C > 1:
                    link(v.tensor_copy(through[:, 1:C], through[:, 0:1].to_broadcast([P, C - 1])))
                gates = turned(gate[:, 1:cols + 1] if reverse else gate[:, 0:cols])

                def scan(begins):
                    for ch in range(C):
                        ins = v.tensor_tensor_scan(turned(out[:, ch, :]), gates, turned(src[:, ch, :]), begins(ch),
                                                   combine, op)
                    link(ins)

                scan(lambda ch: zero)
                at = 0 if reverse else cols - 1
                link(v.tensor_copy(ends[:, :], out[:, :, at]))
                v.wait_ge(pe_done, 1)
                link(v.tensor_copy(endsT[:, :], p_a[0:C, 0:P]))
                link(v.tensor_copy(throughT[:, :], p_b[0:C, 0:P]))
                link(v.tensor_tensor_scan(turned(chain[:, :]), turned(throughT[:, :]), turned(endsT[:, :]), zero,
                                          combine, op))
                link(v.memset(shifted[:, :], zero))
                if reverse:
                    link(v.tensor_copy(shifted[:, 0:P - 1], chain[:, 1:P]))
                else:
                    link(v.tensor_copy(shifted[:, 1:P], chain[:, 0:P - 1]))
                v.sem_inc(pe_done, 1)
                v.wait_ge(pe_done, 3)
                link(v.tensor_scalar(begin[:, :], p_c[0:P, 0:C], enters[:, 0:1], None, combine))
                scan(lambda ch: begin[:, ch:ch + 1])

            @block.tensor
            def _(pe):
                pe.wait_ge(dve, 5 + (0 if add else 3) + (1 if C > 1 else 0) + 1)
                pe.transpose(p_a[0:C, 0:P], ends[:, :], S.ident[0:P, 0:P])
                pe.transpose(p_b[0:C, 0:P], through[:, :], S.ident[0:P, 0:P]).then_inc(pe_done, 1)
                pe.wait_ge(pe_done, 2)
                pe.transpose(p_c[0:P, 0:C], shifted[:, :], S.ident[0:C, 0:C]).then_inc(pe_done, 1)


def layer1_graph(nc, io, S):
    with ExitStack() as stack:
        c = Scope(nc, stack, "g1")
        agg = c.sb("agg", [P, NT, D])
        xn = c.sb("xn", [P, NT, D])
        with ExitStack() as s2:
            S.xnT = Scope(nc, s2, "n2").sb("xnT", [128, KC, N])
            normalize(nc, "n2", S, xn, S.xnT)
            project1(nc, io, S, agg)
            mix1(nc, io, S)
        ends = c.sb("ends", [P, D + NH])
        with ExitStack() as s2:
            c2 = Scope(nc, s2, "t1")
            top = c2.sb("top", [P, NH, T + 1])
            den = c2.sb("den", [P, NH, T + 1])
            attend_edges(nc, io, S, top, den, ends)
            settle_edges(nc, io, S, top, den, ends)
        den = c.sb("dens", [P, NT, 2 * NH])
        collect1(nc, io, S, agg, den, ends)
        finish1(nc, io, S, agg, den[:, :, NH:2 * NH], xn)


def project1(nc, io, S, agg):
    with ExitStack() as stack:
        c = Scope(nc, stack, "p1")
        w = c.sb("w", [128, KC, 3 * D])
        query = c.sb("query", [128, KC])
        bias = c.sb("bias", [1, 3 * D])
        qk = c.sb("qk", [P, U, 2 * D])
        p_qk = [c.ps(f"qk{i}") for i in range(3)]
        p_v = [c.ps(f"v{i}") for i in range(3)]
        names = ("loaded", "biased", "multiplied", "evacuated", "v_out", "out", "v_sent", "dve")
        loaded, biased, multiplied, evacuated, v_out, out, v_sent, dve = [c.sem(x) for x in names]
        with nc.Block() as block:

            @block.sync
            def _(sp):
                for i, n in enumerate("qkv"):
                    sp.dma_start(w[:, :, i * D:(i + 1) * D],
                                 io[f"L1_gnn_W{n}"].rearrange("(k p) n -> p k n", p=128)).then_inc(loaded, 16)
                    sp.dma_start(bias[0:1, i * D:(i + 1) * D],
                                 io[f"L1_gnn_b{n}"].rearrange("(a n) -> a n", a=1)).then_inc(loaded, 16)
                sp.dma_start(query[:, :], io["L1_gnn_query_emb"].rearrange("(k p) -> p k", p=128)).then_inc(loaded, 16)
                for g in range(NT // U):
                    sp.wait_ge(evacuated, U * (g + 1))
                    for i, table in enumerate((io["queries"], io["keys_values"][:, 0:D])):
                        sp.dma_start(table.rearrange("(t p) d -> p t d", p=P)[:, g * U:(g + 1) * U, :],
                                     qk[:, :, i * D:(i + 1) * D]).then_inc(out, 16)
                    sp.wait_ge(v_out, U * (g + 1))
                    sp.dma_start(io["keys_values"][:, D:2 * D].rearrange("(t p) d -> p t d", p=P)[:, g * U:(g + 1) * U, :],
                                 agg[:, g * U:(g + 1) * U, :]).then_inc(v_sent, 16)
                sp.wait_ge(out, 32 * (NT // U))
                sp.wait_ge(v_sent, 16 * (NT // U))

            @block.tensor
            def _(pe):
                pe.wait_ge(loaded, 7 * 16)
                for lo, hi, o in ((0, 2 * D, p_qk[0]), (2 * D, 3 * D, p_v[0])):
                    for k in range(KC):
                        mm = pe.matmul(o[0:1, 0:hi - lo], query[:, k:k + 1], w[:, k, lo:hi],
                                       start=(k == 0), stop=(k == KC - 1))
                mm.then_inc(biased, 1)
                pe.wait_ge(dve, 2)
                for t in range(NT):
                    if t >= 3:
                        pe.wait_ge(evacuated, t - 2)
                        pe.wait_ge(v_out, t - 2)
                    for lo, hi, o in ((0, 2 * D, p_qk[t % 3]), (2 * D, 3 * D, p_v[t % 3])):
                        for k in range(KC):
                            pe.matmul(o[0:P, 0:hi - lo], S.xnT[:, k, t * P:(t + 1) * P], w[:, k, lo:hi],
                                      start=(k == 0), stop=False)
                        mm = pe.matmul(o[0:P, 0:hi - lo], S.ones[0:1, 0:P], bias[0:1, lo:hi], start=False, stop=True)
                    mm.then_inc(multiplied, 1)

            @block.scalar
            def _(a):
                for t in range(NT):
                    a.wait_ge(multiplied, t + 1)
                    if t >= U and t % U == 0:
                        a.wait_ge(out, 32 * (t // U))
                    a.activation(qk[:, t % U, :], p_qk[t % 3][0:P, :], ACT.Copy).then_inc(evacuated, 1)

            @block.vector
            def _(v):
                v.wait_ge(biased, 1)
                v.scalar_tensor_tensor(bias[0:1, 0:2 * D], p_qk[0][0:1, :], 0.1, bias[0:1, 0:2 * D],
                                       ALU.mult, ALU.add).then_inc(dve, 1)
                v.scalar_tensor_tensor(bias[0:1, 2 * D:3 * D], p_v[0][0:1, 0:D], 0.1, bias[0:1, 2 * D:3 * D],
                                       ALU.mult, ALU.add).then_inc(dve, 1)
                for t in range(NT):
                    v.wait_ge(multiplied, t + 1)
                    v.tensor_copy(agg[:, t, :], p_v[t % 3][0:P, 0:D]).then_inc(v_out, 1)


def mix1(nc, io, S):
    W = 128
    HW = 32
    PIECES = [(n, min(512, N - n)) for n in range(0, N, 512)]
    with ExitStack() as stack:
        c = Scope(nc, stack, "x1")
        w = c.sb("w", [128, KC, 3 * W])
        wqT = c.sb("wqT", [W, D])
        wout = c.sb("wout", [W, D])
        bout = c.sb("bout", [1, D])
        kT = c.sb("kT", [W, N])
        top = c.sb("top", [W, 8])
        total = c.sb("total", [W, 8])
        norm = c.sb("norm", [W, 2])
        kv = c.sb("kv", [P, 2, 2 * W])
        ctx = c.sb("ctx", [W, W])
        cw = c.sb("cw", [W, D])
        fold = c.sb("fold", [128, KC, D])
        names = ("loaded", "keys", "topped", "raised", "turned", "copied", "context", "dve", "small", "mult", "added")
        loaded, keys, topped, raised, turned, copied, context, dve, small, mult, added = [c.sem(x) for x in names]
        with nc.Block() as block, ExitStack() as ps:
            p_k = [ps.enter_context(nc.psum_tensor(f"x1_p_k{i}", [128, 512], F32)) for i in range(len(PIECES))]
            p_c = ps.enter_context(nc.psum_tensor("x1_p_c", [128, 512], F32))
            p_kv = p_k[0:2]
            p_w, p_f = p_k[2], p_k[3]
            p_o = p_k[4:7]

            @block.sync
            def _(sp):
                sp.dma_start(w[:, :, :], io["L1_mix_W_qkv"].rearrange("(k p) n -> p k n", p=128)).then_inc(loaded, 16)
                sp.dma_start(wqT[:, :], io["L1_mix_W_q_T"]).then_inc(loaded, 16)
                sp.dma_start(wout[:, :], io["L1_mix_W_out"]).then_inc(loaded, 16)
                sp.dma_start(bout[:, :], io["L1_mix_b_out"].rearrange("(a n) -> a n", a=1)).then_inc(loaded, 16)

            @block.tensor
            def _(pe):
                pe.wait_ge(loaded, 4 * 16)
                for i, (n, m) in enumerate(PIECES):
                    for k in range(KC):
                        mm = pe.matmul(p_k[i][:, 0:m], w[:, k, W:2 * W], S.xnT[:, k, n:n + m],
                                       start=(k == 0), stop=(k == KC - 1))
                    mm.then_inc(keys, 1)
                pe.wait_ge(raised, len(PIECES))
                for t in range(NT):
                    if t >= 2:
                        pe.wait_ge(copied, t - 1)
                    pe.transpose(p_kv[t % 2][0:P, 0:W], kT[:, t * P:(t + 1) * P], S.ident[:, :])
                    for k in range(KC):
                        mm = pe.matmul(p_kv[t % 2][0:P, W:2 * W], S.xnT[:, k, t * P:(t + 1) * P], w[:, k, 2 * W:3 * W],
                                       start=(k == 0), stop=(k == KC - 1))
                    mm.then_inc(turned, 1)
                    if t >= 1:
                        pe.wait_ge(copied, t)
                        pe.matmul(p_c[:, 0:W], kv[:, (t - 1) % 2, W:2 * W], kv[:, (t - 1) % 2, 0:W],
                                  start=(t == 1), stop=False).then_inc(context, 1)
                pe.wait_ge(copied, NT)
                pe.matmul(p_c[:, 0:W], kv[:, (NT - 1) % 2, W:2 * W], kv[:, (NT - 1) % 2, 0:W],
                          start=False, stop=True).then_inc(context, 1)
                pe.wait_ge(dve, 8)
                pe.matmul(p_w[:, 0:D], ctx[:, :], wout[:, :], start=True, stop=True).then_inc(small, 1)
                pe.wait_ge(dve, 9)
                for k in range(KC):
                    mm = pe.matmul(p_f[:, k * D:(k + 1) * D], wqT[:, k * 128:(k + 1) * 128], cw[:, :],
                                   start=True, stop=True)
                mm.then_inc(small, 1)
                pe.wait_ge(dve, 10)
                for t in range(NT):
                    if t >= 3:
                        pe.wait_ge(added, t - 2)
                    o = p_o[t % 3][0:P, 0:D]
                    for k in range(KC):
                        pe.matmul(o, S.xnT[:, k, t * P:(t + 1) * P], fold[:, k, :], start=(k == 0), stop=False)
                    pe.matmul(o, S.ones[0:1, 0:P], bout[0:1, :], start=False, stop=True).then_inc(mult, 1)

            @block.scalar
            def _(a):
                a.wait_ge(topped, 1)
                for i, (n, m) in enumerate(PIECES):
                    a.activation(kT[:, n:n + m], p_k[i][:, 0:m], ACT.Exp, bias=norm[:, 0:1],
                                 accum_out=total[:, i:i + 1]).then_inc(raised, 1)
                for t in range(NT):
                    a.wait_ge(turned, t + 1)
                    if t >= 2:
                        a.wait_ge(context, t - 1)
                    a.activation(kv[:, t % 2, :], p_kv[t % 2][0:P, 0:2 * W], ACT.Copy).then_inc(copied, 1)

            @block.vector
            def _(v):
                link = linker(v, dve)
                for i, (n, m) in enumerate(PIECES):
                    v.wait_ge(keys, i + 1)
                    ins = v.tensor_reduce(top[:, i:i + 1], p_k[i][:, 0:m], AX.X, ALU.max)
                link(ins)
                link(v.tensor_reduce(norm[:, 1:2], top[:, 0:len(PIECES)], AX.X, ALU.max))
                link(v.tensor_scalar(norm[:, 0:1], norm[:, 1:2], -1.0, None, ALU.mult))
                v.sem_inc(topped, 1)
                v.wait_ge(raised, len(PIECES))
                link(v.tensor_reduce(norm[:, 1:2], total[:, 0:len(PIECES)], AX.X, ALU.add))
                link(v.reciprocal(norm[:, 1:2], norm[:, 1:2]))
                link(v.tensor_scalar(norm[:, 1:2], norm[:, 1:2], float(HW) ** -0.5, None, ALU.mult))
                link(v.memset(ctx[:, :], 0.0))
                v.wait_ge(context, NT)
                for h in range(W // HW):
                    blk = slice(h * HW, (h + 1) * HW)
                    ins = v.tensor_copy(ctx[blk, blk], p_c[blk, blk])
                link(ins)
                v.wait_ge(small, 1)
                link(v.tensor_scalar(cw[:, :], p_w[:, 0:D], norm[:, 1:2], None, ALU.mult))
                v.wait_ge(small, 2)
                link(v.tensor_copy(fold[:, :, :], p_f[:, :].rearrange("p (k n) -> p k n", k=KC)))
                for t in range(NT):
                    v.wait_ge(mult, t + 1)
                    v.tensor_tensor(S.x[:, t, :], S.x[:, t, :], p_o[t % 3][0:P, 0:D], ALU.add).then_inc(added, 1)


def attend_edges(nc, io, S, top, den, ends):
    NR = 64
    LAST = T - STEP
    with ExitStack() as stack:
        c = Scope(nc, stack, "ae")
        rel = c.sb("rel", [NR, HD])
        rel4 = c.sb("rel4", [NR, NH, HD])
        types = c.sb("types", [NR, G * P], I32)
        hotT = c.sb("hotT", [NR, 2, G * P])
        idx = c.sb("idx", [P, RING, 2, G], I32)
        kv = c.sb("kv", [P, RING, G, 2 * D])
        queries = c.sb("queries", [P, RING, G, D])
        sums = c.sb("sums", [P, RING, G, D])
        gate = c.sb("gate", [P, T])
        score = c.sb("score", [P, 2, NH, G])
        arg = c.sb("arg", [P, 2, 2, NH, G])
        fade_p = c.sb("fade_p", [P, 2, 2, NH, G])
        p_k = [c.ps(f"k{i}", (128, 1536)) for i in range(2)]
        names = ("loaded", "begun", "asked", "hot_made", "related", "scored", "raised", "weighted",
                 "scores", "states", "free")
        loaded, begun, asked, hot_made, related, scored, raised, weighted, scores, states, free = [
            c.sem(x) for x in names]
        types_in = c.sem("types_in")
        got = [S.gathers[f"s1_got{g}"] for g in range(RING)]
        got_q = [S.gathers[f"w1_got{g}"] for g in range(RING)]
        sent = [c.sem(f"sent{g}") for g in range(RING)]

        def passes(eng):
            with eng.Fori(0, LAST - STEP + 1, STEP) as t0:
                for g in range(RING):
                    yield t0 + g * G, t0 // G + g, t0 // STEP, g, False
            for g in range(RING):
                yield LAST + g * G, LAST // G + g, LAST // STEP, g, True

        def before(g):
            return 1 if g == 0 else 2

        with nc.Block() as block:

            @block.sync
            def _(sp):
                sp.dma_start(rel[:, :], io["L1_gnn_rel_w"]).then_inc(loaded, 16)
                for g in range(RING):
                    sp.sem_inc(sent[g], 16)
                view = io["sums"].rearrange("(p t) d -> p t d", p=P)

                def load_types(t, n):
                    sp.wait_ge(hot_made, n + 2)
                    sp.dma_start(types[:, :], io["type_row"][:, bass.ds(t * P, G * P)]
                                 .to_broadcast([NR, G * P])).then_inc(types_in, 16)

                for n in range(3):
                    load_types(n * G, n)
                for t, n, q, g, last in passes(sp):
                    if not (last and g + 3 >= RING):
                        load_types(t + 3 * G, n + 3)
                    sp.wait_ge(states, n + 1 + 1)
                    sp.dma_start(view[:, bass.ds(t, G), :], sums[:, g, :, :]).then_inc(sent[g], 16)
                for g in range(RING):
                    sp.wait_ge(sent[g], 16 * (ITERS + 1))

            @block.gpsimd
            def _(pool):
                with pool.Fori(0, T - STEP + 1, STEP) as t0:
                    for g in range(RING):
                        pool.wait_ge(free, t0 // G + g + 1)
                        pool.sem_inc(asked, 1)
                        for i, (rows, table, sem) in enumerate(((kv, "keys_values", got), (queries, "queries", got_q))):
                            for j in range(G):
                                pool.indirect_dma_start(
                                    out=rows[:, g, j, :], out_offset=None, in_=io[table],
                                    in_offset=bass.IndirectOffsetOnAxis(ap=idx[:, g, i, j:j + 1], axis=0),
                                ).then_inc(sem[g], 16)

            @block.tensor
            def _(pe):
                pe.wait_ge(begun, 1)
                for t, n, q, g, last in passes(pe):
                    pe.wait_ge(hot_made, n + 1 + 2)
                    pe.wait_ge(scored, n + 2 - before(g) + 1)
                    for j in range(G):
                        pe.matmul(p_k[g % 2][0:P, j * D:(j + 1) * D], hotT[:, g % 2, j * P:(j + 1) * P],
                                  rel4[:, :, :].rearrange("r h d -> r (h d)"), start=True, stop=False,
                                  skip_group_check=True)
                        if j == 0:
                            pe.wait_ge(got[g], q * (16 * G) + 16 * G)
                        mm = pe.matmul(p_k[g % 2][0:P, j * D:(j + 1) * D], S.ident[0:P, 0:P], kv[:, g, j, 0:D],
                                       start=False, stop=True, skip_group_check=True)
                    mm.then_inc(related, 1)

            @block.scalar
            def _(a):
                a.sem_inc(raised, 2)
                for t, n, q, g, last in passes(a):
                    a.wait_ge(scored, n + 1 + 2)
                    a.wait_ge(states, n + 2 - before(g))
                    a.activation(fade_p[:, g % 2, :, :, :], arg[:, g % 2, :, :, :], ACT.Exp,
                                 scale=float(HD) ** -0.5).then_inc(raised, 1)
                    a.wait_ge(raised, n + 1 + 2)
                    for j in range(G):
                        for h in range(NH):
                            part = kv[:, g, j, D + h * HD:D + (h + 1) * HD]
                            ins = a.activation(part, part, ACT.Copy, scale=fade_p[:, g % 2, 1, h, j:j + 1])
                    ins.then_inc(weighted, 1)

            @block.vector
            def _(v):
                link = linker(v, begun)
                v.wait_ge(loaded, 16)
                v.tensor_scalar(gate[:, :], S.keep[:, :], 1.0, BIG, ALU.subtract, ALU.mult)
                v.memset(top[:, :, 0:1], -BIG)
                v.memset(den[:, :, 0:1], 0.0)
                v.memset(sums[:, RING - 1, G - 1, :], 0.0)
                link(v.tensor_scalar(rel4[:, :, :], rel[:, :].unsqueeze(1).to_broadcast([NR, NH, HD]), 0.2, None,
                                     ALU.mult))
                v.tensor_copy(idx[:, :, 0, :], S.src[:, 0:STEP].rearrange("p (g t) -> p g t", g=RING))
                v.tensor_copy(idx[:, :, 1, :],
                              S.dst[:, 0:STEP].rearrange("p (g t) -> p g t", g=RING)).then_inc(free, RING)
                v.sem_inc(hot_made, 2)
                v.sem_inc(scored, 2)
                v.sem_inc(states, 1)

                def one_hot(n, g, first=False):
                    v.wait_ge(types_in, n * 16 + 16)
                    if not first:
                        v.wait_ge(related, n - before(g) + 1)
                    v.tensor_scalar(hotT[:, g % 2, :], types[:, :], S.row[0:NR, 0:1], None,
                                    ALU.is_equal).then_inc(hot_made, 1)

                def score_group(t, n, q, g):
                    link = linker(v, scores, n * 5)
                    v.wait_ge(related, n + 1)
                    v.wait_ge(got_q[g], q * (16 * G) + 16 * G)
                    qs = queries[:, g, :, :]
                    link(v.tensor_tensor(qs, qs, p_k[g % 2][0:P, 0:G * D].rearrange("p (t d) -> p t d", d=D), ALU.mult))
                    link(v.tensor_reduce(score[:, g % 2, :, :].rearrange("p h t -> p t h"),
                                         qs.rearrange("p t (h d) -> p t h d", h=NH), AX.X, ALU.add))
                    for h in range(NH):
                        ins = v.tensor_tensor_scan(top[:, h, bass.ds(t + 1, G)], gate[:, bass.ds(t, G)],
                                                   score[:, g % 2, h, :], top[:, h, bass.ds(t, 1)], ALU.add, ALU.max)
                    link(ins)
                    v.wait_ge(raised, n + 2 - before(g) + 1)
                    was, now = top[:, :, bass.ds(t, G)], top[:, :, bass.ds(t + 1, G)]
                    link(v.tensor_tensor(arg[:, g % 2, 0, :, :], was,
                                         gate[:, bass.ds(t, G)].unsqueeze(1).to_broadcast([P, NH, G]), ALU.add))
                    v.tensor_tensor(arg[:, g % 2, 1, :, :], score[:, g % 2, :, :], now, ALU.subtract)
                    link(v.tensor_tensor(arg[:, g % 2, 0, :, :], arg[:, g % 2, 0, :, :], now, ALU.subtract))
                    v.sem_inc(scored, 1)

                def add_group(t, n, q, g, last, walked):
                    v.wait_ge(weighted, n + 1)
                    v.wait_ge(sent[g], q * 16 + 16)
                    f = fade_p[:, g % 2, :, :, :]
                    for h in range(NH):
                        v.tensor_tensor_scan(den[:, h, bass.ds(t + 1, G)], f[:, 0, h, :], f[:, 1, h, :],
                                             den[:, h, bass.ds(t, 1)], ALU.mult, ALU.add)
                    link = linker(v, walked, n * G)
                    was = sums[:, (g - 1) % RING, G - 1, :]
                    for j in range(G):
                        for h in range(NH):
                            hs = slice(h * HD, (h + 1) * HD)
                            ins = v.scalar_tensor_tensor(sums[:, g, j, hs], was[:, hs], f[:, 0, h, j:j + 1],
                                                         kv[:, g, j, D + h * HD:D + (h + 1) * HD], ALU.mult, ALU.add)
                        link(ins)
                        was = sums[:, g, j, :]
                    v.sem_inc(states, 1)
                    if not last:
                        v.tensor_copy(idx[:, g, 0, :], S.src[:, bass.ds(t + STEP, G)])
                        v.tensor_copy(idx[:, g, 1, :], S.dst[:, bass.ds(t + STEP, G)]).then_inc(free, 1)

                walked = c.sem("walked")
                one_hot(0, 0, first=True)
                one_hot(1, 1, first=True)
                score_group(0, 0, 0, 0)
                for t, n, q, g, last in passes(v):
                    g2 = (g + 2) % RING
                    if not (last and g + 2 >= RING):
                        one_hot(n + 2, g2)
                    if not (last and g + 1 >= RING):
                        score_group(t + G, n + 1, q + (g + 1) // RING, (g + 1) % RING)
                    add_group(t, n, q, g, last, walked)
                v.tensor_copy(ends[:, 0:D], sums[:, RING - 1, G - 1, :])


def settle_edges(nc, io, S, top, den, ends):
    with ExitStack() as stack:
        c = Scope(nc, stack, "m1")
        whole = c.sb("whole", [P, NH, T])
        best = c.sb("best", [P, NH, T])
        pair = c.sb("pair", [P, T, 2 * NH])
        dve, raised, out = c.sem("dve"), c.sem("raised"), c.sem("out")
        own = top[:, :, 1:T + 1]
        segment_scan(nc, "m1a", S, best[:, :, :], own, S.keep[:, :], S.joins, T, ALU.max)
        segment_scan(nc, "m1b", S, whole[:, :, :], best[:, :, :], S.keep[:, :], S.joins, T, ALU.max, reverse=True)
        with nc.Block() as block:

            @block.scalar
            def _(a):
                a.wait_ge(dve, 1)
                a.activation(best[:, :, :], whole[:, :, :], ACT.Exp, scale=float(HD) ** -0.5).then_inc(raised, 1)

            @block.vector
            def _(v):
                link = linker(v, dve)
                link(v.tensor_tensor(whole[:, :, :], own, whole[:, :, :], ALU.subtract))
                v.wait_ge(raised, 1)
                v.tensor_copy(pair[:, :, 0:NH].rearrange("p t h -> p h t"), best[:, :, :])
                link(v.tensor_tensor(pair[:, :, NH:2 * NH].rearrange("p t h -> p h t"), den[:, :, 1:T + 1],
                                     best[:, :, :], ALU.mult))
                v.tensor_copy(ends[:, D:D + NH], pair[:, T - 1, NH:2 * NH])
                for h in range(NH):
                    hs = slice(h * HD, (h + 1) * HD)
                    v.tensor_scalar(ends[:, hs], ends[:, hs], best[:, h, T - 1:T], None, ALU.mult)

            @block.sync
            def _(sp):
                sp.wait_ge(dve, 2)
                sp.dma_start(io["dens"].rearrange("(p t) h -> p t h", p=P), pair[:, :, :]).then_inc(out, 16)
                sp.wait_ge(out, 16)


def collect1(nc, io, S, agg, den, ends):
    with ExitStack() as stack:
        c = Scope(nc, stack, "c1")
        carry = c.sb("carry", [P, N])
        p_c = [c.ps(f"carry{i}") for i in range(4)]
        ready, carried, added, made, scaled = [c.sem(x) for x in ("ready", "carried", "added", "made", "scaled")]
        fetched, dens_in = S.gathers["g1_fetched"], S.gathers["g1_dens_in"]
        with nc.Block() as block:

            @block.gpsimd
            def _(pool):
                pool.iota(carry[:, :], [[1, N]], base=0, channel_multiplier=0,
                          allow_small_or_imprecise_dtypes=True).then_inc(made, 1)
                for t in range(NT):
                    pool.indirect_dma_start(
                        out=agg[:, t, :], out_offset=None, in_=io["sums"],
                        in_offset=bass.IndirectOffsetOnAxis(ap=S.last[:, t:t + 1], axis=0),
                        bounds_check=E - 1, oob_is_err=False).then_inc(fetched, 16)
                pool.wait_ge(made, 2)
                for t in range(NT):
                    pool.indirect_dma_start(
                        out=den[:, t, :], out_offset=None, in_=io["dens"],
                        in_offset=bass.IndirectOffsetOnAxis(ap=S.last[:, t:t + 1], axis=0),
                        bounds_check=E - 1, oob_is_err=False).then_inc(dens_in, 16)

            @block.vector
            def _(v):
                v.wait_ge(made, 1)
                v.memset(den[:, :, :], 1.0).then_inc(made, 1)
                v.tensor_scalar(carry[:, :], carry[:, :], S.goes_on[:, 0:1], None, ALU.is_equal).then_inc(ready, 1)
                v.wait_ge(fetched, 16 * NT)
                v.wait_ge(dens_in, 16 * NT)
                for h in range(NH):
                    v.tensor_tensor(agg[:, :, h * HD:(h + 1) * HD], agg[:, :, h * HD:(h + 1) * HD],
                                    den[:, :, h:h + 1].to_broadcast([P, NT, HD]), ALU.mult).then_inc(scaled, 1)
                v.wait_ge(scaled, NH)
                for t in range(NT):
                    v.wait_ge(carried, t + 1)
                    v.tensor_tensor(den[:, t, NH:2 * NH], den[:, t, NH:2 * NH], p_c[t % 4][0:P, D:D + NH], ALU.add)
                    v.tensor_tensor(agg[:, t, :], agg[:, t, :], p_c[t % 4][0:P, 0:D], ALU.add).then_inc(added, 1)

            @block.tensor
            def _(pe):
                pe.wait_ge(ready, 1)
                for t in range(NT):
                    if t >= 4:
                        pe.wait_ge(added, t - 3)
                    pe.matmul(p_c[t % 4][0:P, 0:D + NH], carry[:, t * P:(t + 1) * P], ends[:, :],
                              start=True, stop=True).then_inc(carried, 1)


def finish1(nc, io, S, agg, den, xn):
    with ExitStack() as stack:
        c = Scope(nc, stack, "o1")
        w = c.sb("w", [128, KC, D])
        bo = c.sb("bo", [1, D])
        gamma = c.sb("gamma", [P, D])
        beta = c.sb("beta", [P, D])
        aT = c.sb("aT", [128, 2, KC, P])
        stats = c.sb("stats", [P, NT, 6])
        mean, diff, var, std = [c.sb(x, [P, NT]) for x in ("mean", "diff", "var", "std")]
        p_t = [c.ps(f"t{i}") for i in range(2)]
        p_o = [c.ps(f"o{i}") for i in range(3)]
        names = ("loaded", "dve", "turned", "copied", "mult", "added", "rooted", "ready", "counted")
        loaded, dve, turned, copied, mult, added, rooted, ready, counted = [c.sem(x) for x in names]
        with nc.Block() as block:

            @block.sync
            def _(sp):
                sp.dma_start(w[:, :, :], io["L1_gnn_Wo"].rearrange("(k p) n -> p k n", p=128)).then_inc(loaded, 16)
                sp.dma_start(bo[:, :], io["L1_gnn_bo"].rearrange("(a n) -> a n", a=1)).then_inc(loaded, 16)
                for name, tile in (("L1_gnn_gamma", gamma), ("L1_gnn_beta", beta)):
                    sp.dma_start(tile[:, :], io[name].rearrange("(a n) -> a n", a=1).to_broadcast([P, D])).then_inc(loaded, 16)

            @block.tensor
            def _(pe):
                pe.wait_ge(loaded, 4 * 16)
                pe.wait_ge(ready, 1)
                for t in range(NT + 1):
                    if t < NT:
                        if t >= 2:
                            pe.wait_ge(copied, t - 1)
                        for k in range(KC):
                            mm = pe.transpose(p_t[t % 2][:, k * P:(k + 1) * P], agg[:, t, k * 128:(k + 1) * 128],
                                              S.ident[0:P, 0:P])
                        mm.then_inc(turned, 1)
                    if t >= 1:
                        s = t - 1
                        pe.wait_ge(copied, s + 1)
                        if s >= 3:
                            pe.wait_ge(added, s - 2)
                        o = p_o[s % 3][0:P, 0:D]
                        for k in range(KC):
                            pe.matmul(o, aT[:, s % 2, k, :], w[:, k, :], start=(k == 0), stop=False)
                        pe.matmul(o, S.ones[0:1, 0:P], bo[0:1, :], start=False, stop=True).then_inc(mult, 1)

            @block.scalar
            def _(a):
                for t in range(NT):
                    a.wait_ge(turned, t + 1)
                    if t >= 2:
                        a.wait_ge(mult, t - 1)
                    a.activation(aT[:, t % 2, :, :], p_t[t % 2][:, 0:KC * P].rearrange("q (k p) -> q k p", k=KC),
                                 ACT.Copy).then_inc(copied, 1)
                a.wait_ge(counted, MV_STEPS)
                a.activation(std[:, :], var[:, :], ACT.Sqrt).then_inc(rooted, 1)

            @block.vector
            def _(v):
                link = linker(v, dve)
                link(v.reciprocal(den, den))
                for h in range(NH):
                    ins = v.tensor_tensor(agg[:, :, h * HD:(h + 1) * HD], agg[:, :, h * HD:(h + 1) * HD],
                                          den[:, :, h:h + 1].to_broadcast([P, NT, HD]), ALU.mult)
                link(ins)
                v.sem_inc(ready, 1)
                for t in range(NT):
                    v.wait_ge(mult, t + 1)
                    v.tensor_tensor(xn[:, t, :], xn[:, t, :], p_o[t % 3][0:P, 0:D], ALU.add).then_inc(added, 1)
                    v.wait_ge(added, t + 1)
                    link(v.bn_stats(stats[:, t, :], xn[:, t, :]))
                mean_and_var(linker(v, counted), stats, v, mean[:, :], var[:, :], diff[:, :])
                v.wait_ge(rooted, 1)
                link(v.reciprocal(std[:, :], std[:, :]))
                for t in range(NT):
                    link(v.tensor_scalar(xn[:, t, :], xn[:, t, :], mean[:, t:t + 1], std[:, t:t + 1],
                                         ALU.subtract, ALU.mult))
                v.wait_ge(loaded, 4 * 16)
                link(v.tensor_tensor(xn[:, :, :], xn[:, :, :], gamma[:, :].unsqueeze(1).to_broadcast([P, NT, D]), ALU.mult))
                link(v.tensor_tensor(xn[:, :, :], xn[:, :, :], beta[:, :].unsqueeze(1).to_broadcast([P, NT, D]), ALU.add))
                v.tensor_tensor(S.x[:, :, :], S.x[:, :, :], xn[:, :, :], ALU.add)


def layer1_experts(nc, io, S):
    with ExitStack() as stack:
        c = Scope(nc, stack, "f1")
        gates = c.sb("gates", [P, NT, NX1])
        S.xnT = c.sb("xnT", [128, KC, N])
        outs = c.sb("outs", [P, EARLY, NT, D])
        normalize(nc, "n3", S, None, S.xnT)
        attend1(nc, io, S, gates, outs)
        combine1(nc, io, S, gates, outs)


def attend1(nc, io, S, gates, outs):
    CH = NH * NX1
    C20 = CH + NH
    C24 = CH + 2 * NH
    RG = 16
    with ExitStack() as stack:
        c = Scope(nc, stack, "a1")
        joins = c.sb("joins", [P, 4])
        keep = c.sb("keep", [P, GC])
        starts = c.sb("starts", [P, GC])
        edges = c.sb("edges", [P, GC, 2], I32)
        vals = c.sb("vals", [P, C24, GC])
        work = c.sb("work", [P, NH, GC])
        last = c.sb("last", [P, NT], I32)
        with ExitStack() as s2:
            c2 = Scope(nc, s2, "a2")
            w = c2.sb("w", [128, KC, CH])
            att = c2.sb("att", [P, 2, CH])
            h = c2.sb("h", [P, NT, C24])
            prod = c2.sb("prod", [P, NT, CH])
            first = c2.sb("first", [P, 4], I32)
            firstf = c2.sb("firstf", [P, 4])
            dstf = c2.sb("dstf", [P, GC])
            ring_i = c2.sb("ring_i", [P, 2, RG], I32)
            ring = c2.sb("ring", [P, 2, RG, C24])
            p_h = c2.ps("h")
            experts = Experts1(c2, io, S, 0, EARLY)
            names = ("loaded", "cleared", "mult", "dve", "tabled", "sent", "staged", "asked", "free")
            loaded, cleared, mult, dve, tabled, sent, staged, asked, free = [c2.sem(x) for x in names]
            got = [S.gathers[f"a1_got{i}"] for i in range(2)]
            with nc.Block() as block:

                @block.sync
                def _(sp):
                    sp.dma_start(w[:, :, :], io["L1_ffn_W_gat"].rearrange("(k p) n -> p k n", p=128)).then_inc(loaded, 16)
                    for i, n in enumerate(("src", "dst")):
                        sp.dma_start(att[:, i, :], io[f"L1_ffn_att_{n}"].rearrange("(a h) e -> a (h e)", a=1)
                                     .to_broadcast([P, CH])).then_inc(loaded, 16)
                    sp.dma_start(edges[:, :, :], io["sorted"].rearrange("(p t) c -> p t c", p=P)).then_inc(loaded, 16)
                    sp.dma_start(last[:, :], io["last2"][0:N].rearrange("(t p) -> p t", p=P)).then_inc(loaded, 16)
                    d2 = io["sorted"].rearrange("(p t) c -> p t c", p=P)
                    sp.wait_ge(cleared, 1)
                    sp.dma_start(first[0:P - 1, 0:1], d2[1:P, 0, 1:2]).then_inc(loaded, 16)
                    sp.dma_start(first[1:P, 1:2], d2[0:P - 1, GC - 1, 1:2]).then_inc(loaded, 16)
                    experts.load(sp)
                    sp.wait_ge(tabled, 1)
                    sp.dma_start(io["gat"].rearrange("(t p) c -> p t c", p=P), h[:, :, :]).then_inc(sent, 16)

                @block.tensor
                def _(pe):
                    pe.wait_ge(loaded, 7 * 16)
                    for t in range(NT):
                        for k in range(KC):
                            mm = pe.matmul(p_h[0:P, t * CH:(t + 1) * CH], S.xnT[:, k, t * P:(t + 1) * P], w[:, k, :],
                                           start=(k == 0), stop=(k == KC - 1))
                    mm.then_inc(mult, 1)
                    experts.multiply(pe)

                @block.scalar
                def _(a):
                    experts.activate(a, outs)

                @block.gpsimd
                def _(pool):
                    pool.wait_ge(sent, 16)
                    with pool.Fori(0, GC - 2 * RG + 1, 2 * RG) as t0:
                        for i in range(2):
                            pool.wait_ge(free, t0 // RG + i + 1)
                            pool.tensor_copy(ring_i[:, i, :], edges[:, bass.ds(t0 + i * RG, RG), 0]).then_inc(staged, 1)
                            pool.wait_ge(staged, t0 // RG + i + 1)
                            pool.sem_inc(asked, 1)
                            for j in range(RG):
                                pool.indirect_dma_start(
                                    out=ring[:, i, j, :], out_offset=None, in_=io["gat"],
                                    in_offset=bass.IndirectOffsetOnAxis(ap=ring_i[:, i, j:j + 1], axis=0),
                                ).then_inc(got[i], 16)

                @block.vector
                def _(v):
                    link = linker(v, dve)
                    link(v.memset(first[:, :], -1))
                    v.sem_inc(cleared, 1)
                    v.sem_inc(free, 2)
                    v.wait_ge(mult, 1)
                    link(v.tensor_copy(h[:, :, 0:CH], p_h[0:P, 0:NT * CH].rearrange("p (t c) -> p t c", c=CH)))
                    for i in range(2):
                        link(v.tensor_tensor(prod[:, :, :], h[:, :, 0:CH],
                                             att[:, i, :].unsqueeze(1).to_broadcast([P, NT, CH]), ALU.mult))
                        link(v.tensor_reduce(h[:, :, CH + i * NH:CH + (i + 1) * NH],
                                             prod[:, :, :].rearrange("p t (h e) -> p t h e", e=NX1), AX.X, ALU.add))
                    v.sem_inc(tabled, 1)
                    link(v.tensor_copy(dstf[:, :], edges[:, :, 1]))
                    link(v.tensor_copy(firstf[:, :], first[:, :]))
                    link(v.memset(keep[:, :], 1.0))
                    link(v.tensor_tensor(keep[:, 1:GC], dstf[:, 1:GC], dstf[:, 0:GC - 1], ALU.is_equal))
                    link(v.tensor_tensor(joins[:, 0:1], firstf[:, 1:2], dstf[:, 0:1], ALU.is_equal))
                    link(v.tensor_tensor(joins[:, 1:2], firstf[:, 0:1], dstf[:, GC - 1:GC], ALU.is_equal))
                    link(v.tensor_tensor(joins[:, 2:3], dstf[:, 0:1], dstf[:, GC - 1:GC], ALU.is_equal))
                    link(v.tensor_scalar(starts[:, :], keep[:, :], -1.0, 1.0, ALU.mult, ALU.add))
                    link(v.tensor_scalar(starts[:, 0:1], joins[:, 0:1], -1.0, 1.0, ALU.mult, ALU.add))
                    with v.Fori(0, GC - 2 * RG + 1, 2 * RG) as t0:
                        link = linker(v, dve, (t0 // RG) + 15)
                        for i in range(2):
                            v.wait_ge(got[i], (t0 // (2 * RG)) * (16 * RG) + 16 * RG)
                            link(v.tensor_copy(vals[:, :, bass.ds(t0 + i * RG, RG)].rearrange("p c t -> p t c"),
                                               ring[:, i, :, :]))
                            v.sem_inc(free, 1)
                    link = linker(v, dve, GC // RG + 15)
                    link(v.tensor_tensor(vals[:, CH + NH:C24, :], vals[:, CH + NH:C24, :],
                                         starts[:, :].unsqueeze(1).to_broadcast([P, NH, GC]), ALU.mult))
        pay = c.sb("pay", [P, C20, GC])
        best = c.sb("best", [P, NH, GC])
        node = c.sb("node", [P, NT, C20])
        segment_scan(nc, "sa", S, work[:, :, :], vals[:, CH + NH:C24, :], keep[:, :], joins, GC, ALU.add)
        logits = vals[:, CH:CH + NH, :]
        with ExitStack() as s2:
            c2 = Scope(nc, s2, "a3")
            dve = c2.sem("dve")
            with nc.Block() as block:
                @block.vector
                def _(v):
                    link = linker(v, dve)
                    link(v.tensor_tensor(logits, logits, work[:, :, :], ALU.add))
                    link(v.scalar_tensor_tensor(work[:, :, :], logits, 0.2, logits, ALU.mult, ALU.max))
        segment_scan(nc, "sb", S, best[:, :, :], work[:, :, :], keep[:, :], joins, GC, ALU.max)
        segment_scan(nc, "sc", S, logits, best[:, :, :], keep[:, :], joins, GC, ALU.max, reverse=True)
        with ExitStack() as s2:
            c2 = Scope(nc, s2, "a4")
            dve, raised = c2.sem("dve"), c2.sem("raised")
            with nc.Block() as block:
                @block.scalar
                def _(a):
                    a.wait_ge(dve, 1)
                    a.activation(pay[:, CH:C20, :], work[:, :, :], ACT.Exp).then_inc(raised, 1)

                @block.vector
                def _(v):
                    v.tensor_tensor(work[:, :, :], work[:, :, :], logits, ALU.subtract).then_inc(dve, 1)
                    v.wait_ge(raised, 1)
                    for hd in range(NH):
                        v.tensor_tensor(pay[:, hd * NX1:(hd + 1) * NX1, :], vals[:, hd * NX1:(hd + 1) * NX1, :],
                                        pay[:, CH + hd:CH + hd + 1, :].to_broadcast([P, NX1, GC]), ALU.mult)
        total = vals[:, 0:C20, :]
        segment_scan(nc, "sd", S, total, pay[:, :, :], keep[:, :], joins, GC, ALU.add)
        with ExitStack() as s2:
            c2 = Scope(nc, s2, "a5")
            flat = pay[:, :, :].rearrange("p c t -> p (c t)").rearrange("p (t c) -> p t c", c=C20)
            small = c2.sb("small", [P, 3, CH])
            z = c2.sb("z", [P, NT, CH])
            sq = c2.sb("sq", [P, NT, CH])
            mean, var, std, top, low = [c2.sb(x, [P, NT]) for x in ("mean", "var", "std", "top", "low")]
            score, hot1, hot2 = [c2.sb(x, [P, NT, NX1]) for x in ("score", "hot1", "hot2")]
            rec = c2.sb("rec", [P, NT, NH])
            order = c2.sb("order", [P, NX1])
            names = ("loaded", "dve", "sent", "made", "rooted", "raised")
            fetched = S.gathers["a1_fetched"]
            loaded, dve, sent, made, rooted, raised = [c2.sem(x) for x in names]
            with nc.Block() as block:

                @block.sync
                def _(sp):
                    for i, n in enumerate(("b_gat", "ln_gamma", "ln_beta")):
                        sp.dma_start(small[:, i, :], io[f"L1_ffn_{n}"].rearrange("(a n) -> a n", a=1)
                                     .to_broadcast([P, CH])).then_inc(loaded, 16)
                    sp.wait_ge(dve, 1)
                    sp.dma_start(io["gsum"].rearrange("(p t) c -> p t c", p=P), flat).then_inc(sent, 16)
                    sp.wait_ge(sent, 16)

                @block.gpsimd
                def _(pool):
                    pool.iota(order[:, :], [[-1, NX1]], base=NX1, channel_multiplier=0,
                              allow_small_or_imprecise_dtypes=True).then_inc(made, 1)
                    pool.wait_ge(sent, 16)
                    for t in range(NT):
                        pool.indirect_dma_start(
                            out=node[:, t, :], out_offset=None, in_=io["gsum"],
                            in_offset=bass.IndirectOffsetOnAxis(ap=last[:, t:t + 1], axis=0)).then_inc(fetched, 16)

                @block.scalar
                def _(a):
                    a.wait_ge(dve, 12)
                    a.activation(std[:, :], var[:, :], ACT.Sqrt).then_inc(rooted, 1)
                    a.wait_ge(dve, 30)
                    a.activation(top[:, :], low[:, :], ACT.Exp).then_inc(raised, 1)

                @block.vector
                def _(v):
                    link = linker(v, dve)
                    link(v.tensor_copy(flat.rearrange("p t c -> p c t"), total))
                    v.wait_ge(fetched, 16 * NT)
                    v.wait_ge(loaded, 48)
                    v.wait_ge(made, 1)

                    def wide(x, n=CH):
                        return x.unsqueeze(2).to_broadcast([P, NT, n])

                    def rows(i):
                        return small[:, i, :].unsqueeze(1).to_broadcast([P, NT, CH])

                    link(v.tensor_scalar(rec[:, :, :], node[:, :, CH:C20], 1e-16, None, ALU.add))
                    link(v.reciprocal(rec[:, :, :], rec[:, :, :]))
                    for hd in range(NH):
                        ins = v.tensor_tensor(z[:, :, hd * NX1:(hd + 1) * NX1], node[:, :, hd * NX1:(hd + 1) * NX1],
                                              wide(rec[:, :, hd], NX1), ALU.mult)
                    link(ins)
                    link(v.tensor_tensor(z[:, :, :], z[:, :, :], rows(0), ALU.add))
                    link(v.tensor_reduce(mean[:, :], z[:, :, :], AX.X, ALU.add))
                    link(v.tensor_scalar(mean[:, :], mean[:, :], 1.0 / CH, None, ALU.mult))
                    link(v.tensor_tensor(z[:, :, :], z[:, :, :], wide(mean[:, :]), ALU.subtract))
                    link(v.tensor_tensor(sq[:, :, :], z[:, :, :], z[:, :, :], ALU.mult))
                    link(v.tensor_reduce(var[:, :], sq[:, :, :], AX.X, ALU.add))
                    link(v.tensor_scalar(var[:, :], var[:, :], 1.0 / CH, None, ALU.mult))
                    link(v.tensor_scalar(var[:, :], var[:, :], EPS, None, ALU.add))
                    v.wait_ge(rooted, 1)
                    link(v.reciprocal(std[:, :], std[:, :]))
                    link(v.tensor_tensor(z[:, :, :], z[:, :, :], wide(std[:, :]), ALU.mult))
                    link(v.tensor_tensor(z[:, :, :], z[:, :, :], rows(1), ALU.mult))
                    link(v.tensor_tensor(z[:, :, :], z[:, :, :], rows(2), ALU.add))
                    link(v.tensor_reduce(score[:, :, :], z[:, :, :].rearrange("p t (h e) -> p t e h", e=NX1),
                                         AX.X, ALU.add))
                    link(v.tensor_scalar(score[:, :, :], score[:, :, :], 1.0 / NH, None, ALU.mult))
                    ranked = order[:, :].unsqueeze(1).to_broadcast([P, NT, NX1])

                    def first_best(hot, best):
                        link(v.tensor_reduce(best, score[:, :, :], AX.X, ALU.max))
                        link(v.tensor_tensor(hot, score[:, :, :], wide(best, NX1), ALU.is_equal))
                        link(v.tensor_tensor(hot, hot, ranked, ALU.mult))
                        link(v.tensor_reduce(mean[:, :], hot, AX.X, ALU.max))
                        link(v.tensor_tensor(hot, ranked, wide(mean[:, :], NX1), ALU.is_equal))

                    first_best(hot1[:, :, :], top[:, :])        
                    link(v.scalar_tensor_tensor(score[:, :, :], hot1[:, :, :], -BIG, score[:, :, :],
                                                ALU.mult, ALU.add))
                    first_best(hot2[:, :, :], low[:, :])        
                    link(v.tensor_tensor(low[:, :], low[:, :], top[:, :], ALU.subtract))
                    v.wait_ge(raised, 1)
                    link(v.tensor_scalar(var[:, :], top[:, :], 1.0, None, ALU.add))
                    link(v.reciprocal(var[:, :], var[:, :]))
                    link(v.tensor_tensor(top[:, :], top[:, :], var[:, :], ALU.mult))
                    link(v.tensor_tensor(hot1[:, :, :], hot1[:, :, :], wide(var[:, :], NX1), ALU.mult))
                    link(v.tensor_tensor(hot2[:, :, :], hot2[:, :, :], wide(top[:, :], NX1), ALU.mult))
                    v.tensor_tensor(gates[:, :, :], hot1[:, :, :], hot2[:, :, :], ALU.add)


class Experts1:

    def __init__(self, c, io, S, lo, hi):
        self.S, self.io, self.lo, self.hi = S, io, lo, hi
        self.experts = hi - lo
        self.chunks = self.experts * NCH1
        self.w1 = c.sb("w1", [128, KC, self.experts * HX1])
        self.w2 = c.sb("w2", [128, self.chunks, D])
        self.b1 = c.sb("b1", [128, self.chunks])
        self.b2 = c.sb("b2", [1, self.experts, 2, D])
        self.hid = c.sb("hid", [128, 2, U * P])
        self.p_hidden = [c.ps(f"hidden{i}", (128, 1024)) for i in range(2)]
        self.p_out = c.ps("out", (128, 1536))
        names = ("x_loaded", "x_hidden", "x_active", "x_done", "x_emptied")
        self.loaded, self.hidden, self.active, self.done, self.emptied = [c.sem(x) for x in names]

    CUT = ((0, 3 * P, 0), (3 * P, U * P, 512))

    def load(self, sp):
        io, lo, hi = self.io, self.lo, self.hi
        sp.dma_start(self.w1[:, :, :], io["L1_ffn_W1"][:, lo * HX1:hi * HX1]
                     .rearrange("(k p) n -> p k n", p=128)).then_inc(self.loaded, 16)
        sp.dma_start(self.w2[:, :, :], io["L1_ffn_W2"][lo * HX1:hi * HX1, :]
                     .rearrange("(c p) n -> p c n", p=128)).then_inc(self.loaded, 16)
        sp.dma_start(self.b1[:, :], io["L1_ffn_b1"][:, lo * NCH1:hi * NCH1]).then_inc(self.loaded, 16)
        for i in range(2):
            sp.dma_start(self.b2[:, :, i, :], io["L1_ffn_b2"][lo:hi, :]
                         .rearrange("(a e) n -> a e n", a=1)).then_inc(self.loaded, 16)

    def multiply(self, pe):
        S, w1, w2, b2, hid, p_hidden, p_out = self.S, self.w1, self.w2, self.b2, self.hid, self.p_hidden, self.p_out
        ALLC = self.chunks
        pe.wait_ge(self.loaded, 5 * 16)
        with pe.Fori(0, NT - U + 1, U) as t0:

            def make_hidden(ch):
                pe.wait_ge(self.active, (t0 // U) * ALLC + ch + 1)
                for lo, hi, at in self.CUT:
                    for k in range(KC):
                        mm = pe.matmul(p_hidden[ch % 2][:, at:at + hi - lo], w1[:, k, ch * 128:(ch + 1) * 128],
                                       S.xnT[:, k, bass.ds(t0 * P + lo, hi - lo)],
                                       start=(k == 0), stop=(k == KC - 1))
                mm.then_inc(self.hidden, 1)

            def add_output(ch):
                e = ch // NCH1
                if ch % NCH1 == 0:
                    pe.wait_ge(self.emptied, (t0 // U) * self.experts + e + 1)
                    for lo, hi in ((0, 512), (512, 1024), (1024, U * D)):
                        pe.matmul(p_out[0:P, lo:hi], S.ones[0:1, 0:P],
                                  b2[0:1, e, :, :].rearrange("a i n -> a (i n)")[:, 0:hi - lo],
                                  start=True, stop=False, skip_group_check=True)
                pe.wait_ge(self.active, (t0 // U) * ALLC + ch + 3)
                for u in range(U):
                    mm = pe.matmul(p_out[0:P, u * D:(u + 1) * D], hid[:, ch % 2, u * P:(u + 1) * P],
                                   w2[:, ch, :], start=False, stop=(ch % NCH1 == NCH1 - 1), skip_group_check=True)
                mm.then_inc(self.done, 1)

            make_hidden(0)
            for ch in range(ALLC):
                if ch + 1 < ALLC:
                    make_hidden(ch + 1)
                add_output(ch)

    def activate(self, a, outs=None):
        ALLC = self.chunks
        a.wait_ge(self.loaded, 5 * 16)
        a.sem_inc(self.active, 2)
        a.sem_inc(self.done, 2)
        if outs is not None:
            a.sem_inc(self.emptied, 1)
        with a.Fori(0, NT - U + 1, U) as t0:

            def empty(e):
                a.wait_ge(self.done, (t0 // U) * ALLC + (e + 1) * NCH1 + 2)
                a.activation(outs[:, e, bass.ds(t0, U), :].rearrange("p u d -> p (u d)"), self.p_out[0:P, 0:U * D],
                             ACT.Copy).then_inc(self.emptied, 1)

            for ch in range(ALLC):
                a.wait_ge(self.hidden, (t0 // U) * ALLC + ch + 1)
                a.wait_ge(self.done, (t0 // U) * ALLC + ch + 1)
                for lo, hi, at in self.CUT:
                    ins = a.activation(self.hid[:, ch % 2, lo:hi], self.p_hidden[ch % 2][:, at:at + hi - lo],
                                       ACT.Gelu, bias=self.b1[:, ch:ch + 1])
                ins.then_inc(self.active, 1)
                if outs is not None and ch % NCH1 == 0 and ch > 0:
                    empty(ch // NCH1 - 1)
            if outs is not None:
                empty(self.experts - 1)


def combine1(nc, io, S, gates, outs):
    with ExitStack() as stack:
        c = Scope(nc, stack, "h1")
        experts = Experts1(c, io, S, EARLY, NX1)
        dve = c.sem("dve")
        with nc.Block() as block:

            @block.sync
            def _(sp):
                experts.load(sp)

            @block.tensor
            def _(pe):
                experts.multiply(pe)

            @block.scalar
            def _(a):
                experts.activate(a)

            @block.vector
            def _(v):
                v.sem_inc(experts.emptied, 1)
                with v.Fori(0, NT - U + 1, U) as t0:
                    link = linker(v, dve, (t0 // U) * NX1)
                    for e in range(NX1):
                        if e == EARLY:
                            v.wait_ge(experts.done, (t0 // U + 1) * NCH1 + 2)
                        for u in range(U):
                            xt = S.x[:, bass.ds(t0 + u, 1), :].rearrange("p a b -> p (a b)")
                            made = (experts.p_out[0:P, u * D:(u + 1) * D] if e == EARLY else
                                    outs[:, e, bass.ds(t0 + u, 1), :].rearrange("p a b -> p (a b)"))
                            ins = v.scalar_tensor_tensor(xt, made, gates[:, bass.ds(t0 + u, 1), e], xt,
                                                         ALU.mult, ALU.add)
                        link(ins)
                    v.sem_inc(experts.emptied, 1)


class State:
    pass


_TRANSPOSED = {"L0_gnn_W", "L0_ffn_router_w"}


def build(nc, io, out):
    with ExitStack() as stack:
        stack.enter_context(nc.allow_non_contiguous_dma(reason="single columns, small vectors"))
        c = Scope(nc, stack, "all")
        S = State()
        S.gathers = {name: c.sem(name) for name in GATHER_SEMAPHORES}
        S.first_semaphore = min(nc.free_semaphores)
        S.x = c.sb("x", [P, NT, D])
        S.ident = c.sb("ident", [128, 128])
        S.ones = c.sb("ones", [128, 128])
        S.row = c.sb("row", [128, 1])
        with ExitStack() as sg:
            cg = Scope(nc, sg, "graph")
            S.dst = cg.sb("dst", [P, T], I32)
            S.src = cg.sb("src", [P, T + STEP], I32)
            S.keep = cg.sb("keep", [P, T])
            S.joins = cg.sb("joins", [P, 4])
            S.goes_on = cg.sb("goes_on", [P, 1])
            S.last = cg.sb("last", [P, NT], I32)
            with ExitStack() as s0:
                c0 = Scope(nc, s0, "sort")
                S.xnT = c0.sb("xnT", [128, KC, N])
                S.w = c0.sb("w", [P, T])
                S.dstf = c0.sb("dstf", [P, T])
                S.iota_lo = c0.sb("iota_lo", [128, LO])
                S.tri = c0.sb("tri", [128, 128])
                S.below = c0.sb("below", [128, 128])
                S.dst_lo, S.dst_hi = c0.sb("dst_lo", [P, T], I32), c0.sb("dst_hi", [P, T], I32)
                S.rsrc, S.rdst, S.rdst_lo, S.rdst_hi = [
                    c0.sb(x, [128, GT], I32) for x in ("rsrc", "rdst", "rdst_lo", "rdst_hi")]
                S.rdstf = c0.sb("rdstf", [128, GT])
                S.count = c0.sb("counts", [128, GT + 1, HI])
                S.hot_hi = c0.sb("hot_hi", [128, GT, HI], BF16)
                S.loop_i, S.rlast_i = c0.sb("loop_i", [128, HI], I32), c0.sb("rlast_i", [128, HI], I32)
                load(nc, io, S)
                normalize(nc, "n0", S, None, S.xnT)
                layer0_graph(nc, io, S)
                normalize(nc, "n1", S, None, S.xnT)
                layer0_experts(nc, io, S)
            clear_semaphores(nc, io, S)
            layer1_graph(nc, io, S)
        clear_semaphores(nc, io, S)
        layer1_experts(nc, io, S)
        done = c.sem("done")
        with nc.Block() as block:
            @block.sync
            def _(sp):
                sp.dma_start(out.rearrange("(t p) d -> p t d", p=P), S.x[:, :, :]).then_inc(done, 16)
                sp.wait_ge(done, 16)


_SCRATCH = {
    "last": ((LO * HI,), I32),
    "table": ((N, D), F32),
    "sums": ((E, D), F32),
    "queries": ((N, D), F32),
    "keys_values": ((N, 2 * D), F32),
    "dens": ((E, 2 * NH), F32),
    "sorted": ((GP, 2), I32),
    "last2": ((LO * HI,), I32),
    "gat": ((N, 24), F32),
    "gsum": ((GP, 20), F32),
}


def kernel(**inputs):
    import numpy as _np
    import concourse.bacc as _bacc
    from concourse.bass_utils import run_bass_kernel_spmd as _run

    nc = _bacc.Bacc("TRN2", target_bir_lowering=False, num_devices=1)
    arrays, io = {}, {}
    inputs["L0_mix_W_v_T"] = _np.asarray(inputs["L0_mix_W_qkv"])[:, 2 * D:].T
    inputs["L1_mix_W_q_T"] = _np.asarray(inputs["L1_mix_W_qkv"])[:, 0:128].T
    inputs["type_row"] = _np.asarray(inputs["edge_type_64"]).reshape(P, T).T.reshape(1, E)
    edges = _np.asarray(inputs["L1_ffn_edge_index"])
    edges = _np.concatenate([edges, _np.full((2, GT * 128 - GE), PAD, edges.dtype)], axis=1)
    inputs["edge_columns"] = edges.reshape(2, GT, 128).transpose(0, 2, 1)
    inputs["edge_row"] = edges[1:2]
    inputs["L1_ffn_W1"] = _np.asarray(inputs["L1_ffn_W1"]).transpose(1, 0, 2).reshape(D, NX1 * HX1)
    inputs["L1_ffn_b1"] = _np.asarray(inputs["L1_ffn_b1"]).reshape(NX1 * HX1 // 128, 128).T
    inputs["L1_ffn_W2"] = _np.asarray(inputs["L1_ffn_W2"]).reshape(NX1 * HX1, D)
    w1 = _np.asarray(inputs["L0_ffn_W1"])
    inputs["L0_ffn_W1"] = w1.transpose(1, 0, 2).reshape(D, NX * HX)
    inputs["L0_ffn_b1"] = _np.asarray(inputs["L0_ffn_b1"]).reshape(NC0, 128).T
    inputs["L0_ffn_W2"] = _np.asarray(inputs["L0_ffn_W2"]).reshape(NX * HX, D)
    for name, a in inputs.items():
        a = _np.asarray(a)
        if name in _TRANSPOSED:
            a = a.T
        a = _np.ascontiguousarray(a)
        arrays[f"in_{name}"] = a
        io[name] = nc.dram_tensor(f"in_{name}", a.shape, mybir.dt.from_np(a.dtype), kind="ExternalInput").ap()
    for name, (shape, dt) in _SCRATCH.items():
        io[name] = nc.dram_tensor(f"s_{name}", list(shape), dt, kind="Internal").ap()
    out = nc.dram_tensor("out", (N, D), F32, kind="ExternalOutput").ap()
    build(nc, io, out)
    r = _run(nc, [arrays], core_ids=[0])
    return r.results[0]["out"]
```

```python
from contextlib import ExitStack

import concourse.bass as bass
from concourse import mybir

F32 = mybir.dt.float32
BF16 = mybir.dt.bfloat16
I32 = mybir.dt.int32
ALU = mybir.AluOpType
ACT = mybir.ActivationFunctionType
AX = mybir.AxisListType

D = 256
KC = D // 128
P = 125
N = 3125
NT = N // P
U = 5
E = 53125
T = E // P
G = 5
RING = 5
STEP = G * RING
ITERS = T // STEP
BIG = 1.0e30
EPS = 1e-5
NH = 4
HD = D // NH
NX = 32
HX = 64
NC0 = NX * HX // 128
LO = 128
HI = 25
GE = 32768
GB = 13
QB = 4
GT = GB * QB * (N // 125 // 5)
PAD = 25 * 128 - 1
GN = GE + N
GC = 288
GP = P * GC
NX1 = 4
HX1 = 512
NCH1 = HX1 // 128
EARLY = 3


def linker(eng, sem, base=0):
    count = [0]

    def link(ins):
        count[0] += 1
        ins.then_inc(sem, 1)
        eng.wait_ge(sem, base + count[0])

    return link


GATHER_SEMAPHORES = (
    [f"w0_got{g}" for g in range(RING)] + [f"q1_got{g}" for g in range(RING)] +
    [f"kv1_got{g}" for g in range(RING)] + ["g0_fetched", "g1_fetched", "g1_dens_in", "so_sent0", "so_sent1",
                                           "so_loops_sent", "a1_got0", "a1_got1", "a1_fetched"])


class Scope:

    def __init__(self, nc, stack, tag):
        self.nc, self.stack, self.tag = nc, stack, tag

    def sb(self, name, shape, dt=F32):
        return self.stack.enter_context(self.nc.sbuf_tensor(f"{self.tag}_{name}", shape, dt))

    def ps(self, name, shape=(128, 512), dt=F32):
        return self.stack.enter_context(self.nc.psum_tensor(f"{self.tag}_p_{name}", list(shape), dt))

    def sem(self, name):
        return self.stack.enter_context(self.nc.semaphore(f"{self.tag}_{name}"))


def clear_semaphores(nc, S):
    with nc.Block() as block:

        @block.sync
        def _(sp):
            sp.sem_clear(range(S.first_semaphore, 256))


def load(nc, io, S):
    with ExitStack() as stack:
        c = Scope(nc, stack, "load")
        first = c.sb("first", [P, 4], I32)
        firstf = c.sb("firstf", [P, 4])
        loaded, made, dve, filled = [c.sem(x) for x in ("loaded", "made", "dve", "filled")]
        with nc.Block() as block:

            @block.sync
            def _(sp):
                sp.dma_start(S.dst[:, :], io["dst"].rearrange("(p t) -> p t", p=P)).then_inc(loaded, 16)
                sp.dma_start(S.src[:, 0:T], io["src"].rearrange("(p t) -> p t", p=P)).then_inc(loaded, 16)
                sp.dma_start(S.w[:, :], io["edge_weight"].rearrange("(p t) -> p t", p=P)).then_inc(loaded, 16)
                sp.wait_ge(filled, 1)
                d2 = io["dst"].rearrange("(p t) -> p t", p=P)
                sp.dma_start(first[0:P - 1, 0:1], d2[1:P, 0:1]).then_inc(loaded, 16)
                sp.dma_start(first[1:P, 1:2], d2[0:P - 1, T - 1:T]).then_inc(loaded, 16)
                sp.dma_start(S.x[:, :, :], io["x"].rearrange("(t p) d -> p t d", p=P)).then_inc(loaded, 16)
                sp.dma_start(S.rsrc[:, :], io["edge_columns"][0]).then_inc(loaded, 16)
                sp.dma_start(S.rdst[:, :], io["edge_columns"][1]).then_inc(loaded, 16)

            @block.gpsimd
            def _(pool):
                pool.iota(S.iota_lo[:, :], [[1, LO]], base=0, channel_multiplier=0,
                          allow_small_or_imprecise_dtypes=True).then_inc(made, 1)
                pool.iota(S.row[:, :], [[0, 1]], base=0, channel_multiplier=1,
                          allow_small_or_imprecise_dtypes=True).then_inc(made, 1)
                pool.memset(S.ones[:, :], 1.0).then_inc(made, 1)
                pool.memset(S.ident[:, :], 0.0).then_inc(made, 1)
                pool.wait_ge(made, 4)
                pool.affine_select(out=S.ident[:, :], in_=S.ident[:, :], compare_op=ALU.not_equal, fill=1.0, base=0,
                                   pattern=[[-1, 128]], channel_multiplier=1).then_inc(made, 1)
                pool.affine_select(out=S.tri[:, :], in_=S.ones[:, :], compare_op=ALU.is_ge, fill=0.0, base=0,
                                   pattern=[[1, 128]], channel_multiplier=-1).then_inc(made, 1)
                pool.affine_select(out=S.below[:, :], in_=S.ones[:, :], compare_op=ALU.is_gt, fill=0.0, base=0,
                                   pattern=[[-1, 128]], channel_multiplier=1).then_inc(made, 1)

            @block.vector
            def _(v):
                link = linker(v, dve)
                link(v.memset(first[:, :], -1))
                v.memset(S.src[:, T:T + STEP], 0)
                v.memset(S.ones3[:, :], 1.0)
                v.sem_inc(filled, 1)
                v.wait_ge(loaded, 8 * 16)
                link(v.tensor_copy(S.dstf[:, :], S.dst[:, :]))
                link(v.tensor_copy(firstf[:, :], first[:, :]))
                v.wait_ge(made, 2)
                for i in range(2):
                    link(v.tensor_scalar(S.minus[:, i:i + 1], S.row[0:3, :], float(i), -1.0, ALU.is_gt, ALU.mult))
                link(v.memset(S.keep[:, :], 1.0))
                link(v.tensor_tensor(S.keep[:, 1:T], S.dstf[:, 1:T], S.dstf[:, 0:T - 1], ALU.is_equal))
                link(v.tensor_tensor(S.joins[:, 0:1], firstf[:, 1:2], S.dstf[:, 0:1], ALU.is_equal))
                link(v.tensor_tensor(S.joins[:, 1:2], firstf[:, 0:1], S.dstf[:, T - 1:T], ALU.is_equal))
                link(v.tensor_tensor(S.joins[:, 2:3], S.dstf[:, 0:1], S.dstf[:, T - 1:T], ALU.is_equal))
                link(v.scalar_tensor_tensor(S.goes_on[:, :], S.dstf[:, T - 1:T], 1.0, S.joins[:, 1:2],
                                            ALU.add, ALU.mult))
                link(v.tensor_scalar(S.goes_on[:, :], S.goes_on[:, :], 1.0, None, ALU.subtract))
                for lo, hi, dst in ((S.dst_lo, S.dst_hi, S.dst), (S.rdst_lo, S.rdst_hi, S.rdst)):
                    link(v.tensor_scalar(lo[:, :], dst[:, :], LO - 1, None, ALU.bitwise_and))
                    link(v.tensor_scalar(hi[:, :], dst[:, :], 7, None, ALU.logical_shift_right))


def exact_parts(link, v, S, full, parts):
    for i in range(2):
        link(v.tensor_copy(parts, full))
        link(v.scalar_tensor_tensor(full, parts, S.minus[:, i:i + 1], full, ALU.mult, ALU.add))
    link(v.tensor_copy(parts, full))


MV_STEPS = 8


def mean_and_var(link, stats, v, mean, var, diff, scale=1.0, eps=EPS):
    me, qe, mo, qo = [stats[:, :, i] for i in (1, 2, 4, 5)]
    link(v.tensor_tensor(mean, me, mo, ALU.add))
    link(v.tensor_scalar(mean, mean, 0.5, None, ALU.mult))
    link(v.tensor_tensor(diff, me, mo, ALU.subtract))
    link(v.scalar_tensor_tensor(diff, diff, 0.25, diff, ALU.mult, ALU.mult))
    link(v.tensor_tensor(var, qe, qo, ALU.add))
    link(v.tensor_scalar(var, var, 1.0 / D, None, ALU.mult))
    link(v.tensor_tensor(var, var, diff, ALU.add))
    link(v.tensor_scalar(var, var, scale, eps, ALU.mult, ALU.add))


def normalize(nc, tag, S, xn, xnT):
    with ExitStack() as stack:
        c = Scope(nc, stack, tag)
        stats = c.sb("stats", [P, NT, 6])
        mean = c.sb("mean", [P, NT])
        diff = c.sb("diff", [P, NT])
        var = c.sb("var", [P, NT])
        std = c.sb("std", [P, NT])
        rstd = c.sb("rstd", [P, NT])
        tile = c.sb("tile", [P, U, D])
        p_t = [c.ps(f"t{u}") for u in range(U)]
        counted, spread, rooted, normed, turned, copied = [
            c.sem(x) for x in ("counted", "spread", "rooted", "normed", "turned", "copied")]
        with nc.Block() as block:

            @block.vector
            def _(v):
                with v.Fori(0, NT) as t:
                    v.bn_stats(stats[:, bass.ds(t, 1), :].rearrange("p a b -> p (a b)"),
                               S.x[:, bass.ds(t, 1), :].rearrange("p a b -> p (a b)")).then_inc(counted, 1)
                v.wait_ge(counted, NT)
                mean_and_var(linker(v, spread), stats, v, mean[:, :], var[:, :], diff[:, :])
                v.wait_ge(rooted, 1)
                v.reciprocal(rstd[:, :], std[:, :]).then_inc(spread, 1)
                v.wait_ge(spread, MV_STEPS + 1)
                with v.Fori(0, NT - U + 1, U) as t0:
                    for u in range(U):
                        t = t0 + u
                        v.wait_ge(turned, t + 1)
                        v.tensor_scalar(tile[:, u, :], S.x[:, bass.ds(t, 1), :].rearrange("p a b -> p (a b)"),
                                        mean[:, bass.ds(t, 1)], rstd[:, bass.ds(t, 1)],
                                        ALU.subtract, ALU.mult).then_inc(normed, 1)
                        if xn is not None:
                            v.tensor_scalar(xn[:, bass.ds(t, 1), :].rearrange("p a b -> p (a b)"),
                                            S.x[:, bass.ds(t, 1), :].rearrange("p a b -> p (a b)"),
                                            mean[:, bass.ds(t, 1)], rstd[:, bass.ds(t, 1)],
                                            ALU.subtract, ALU.mult)

            @block.tensor
            def _(pe):
                pe.sem_inc(turned, U)
                with pe.Fori(0, NT - U + 1, U) as t0:
                    for u in range(U):
                        pe.wait_ge(normed, t0 + u + 1)
                        pe.wait_ge(copied, t0 + u + 1)
                        for k in range(KC):
                            mm = pe.transpose(p_t[u][:, k * P:(k + 1) * P], tile[:, u, k * 128:(k + 1) * 128],
                                              S.ident[0:P, 0:P])
                        mm.then_inc(turned, 1)

            @block.scalar
            def _(a):
                a.wait_ge(spread, MV_STEPS)
                a.activation(std[:, :], var[:, :], ACT.Sqrt).then_inc(rooted, 1)
                a.sem_inc(copied, U)
                with a.Fori(0, NT - U + 1, U) as t0:
                    for u in range(U):
                        a.wait_ge(turned, t0 + u + 1 + U)
                        a.activation(xnT[:, :, bass.ds((t0 + u) * P, P)],
                                     p_t[u][:, 0:KC * P].rearrange("q (k p) -> q k p", k=KC),
                                     ACT.Copy).then_inc(copied, 1)


class Walk:

    def __init__(self, c, S, tag):
        self.idx = c.sb("w_idx", [P, RING, G], I32)
        self.all_rows = c.sb("w_rows", [128, RING, G, D])
        self.rows = self.all_rows[0:P, :, :, :]
        self.sums = c.sb("w_sums", [P, RING, G, D])
        self.end = self.sums[:, RING - 1, G - 1, :]
        self.asked, self.weighed, self.walked, self.free = [
            c.sem(x) for x in ("w_asked", "w_weighed", "w_walked", "w_free")]
        self.got = [S.gathers[f"{tag}_got{g}"] for g in range(RING)]
        self.sent = [c.sem(f"w_sent{g}") for g in range(RING)]

    def gather(self, pool, table):
        with pool.Fori(0, ITERS) as i:
            for g in range(RING):
                pool.wait_ge(self.free, i * RING + g + 1)
                pool.sem_inc(self.asked, 1)
                for j in range(G):
                    pool.indirect_dma_start(
                        out=self.rows[:, g, j, :], out_offset=None, in_=table,
                        in_offset=bass.IndirectOffsetOnAxis(ap=self.idx[:, g, j:j + 1], axis=0),
                    ).then_inc(self.got[g], 16)

    def begin(self, v, src):
        v.memset(self.end, 0.0).then_inc(self.walked, 1)
        v.tensor_copy(self.idx[:, :, :], src[:, 0:STEP].rearrange("p (g t) -> p g t", g=RING)).then_inc(self.free, RING)

    def weigh(self, a, weights, i, g):
        a.wait_ge(self.got[g], i * (16 * G) + 16 * G)
        for j in range(G):
            row = self.rows[:, g, j, :]
            ins = a.activation(row, row, ACT.Copy, scale=weights[:, bass.ds(i * STEP + (g * G + j), 1)])
        ins.then_inc(self.weighed, 1)

    def walk(self, v, src, keep, begin, end, beside):
        with v.Fori(begin * STEP, (end - 1) * STEP + 1, STEP) as t0:
            link = linker(v, self.walked, t0 + 1)
            for g in range(RING):
                beside(g, t0 + g * G, t0 // G + g, t0 // STEP)
                v.wait_ge(self.weighed, t0 // G + g + 1)
                v.wait_ge(self.sent[g], (t0 // STEP) * 16 + 16)
                before = self.sums[:, (g - 1) % RING, G - 1, :]
                for j in range(G):
                    link(v.scalar_tensor_tensor(self.sums[:, g, j, :], before, keep[:, bass.ds(t0 + g * G + j, 1)],
                                                self.rows[:, g, j, :], ALU.mult, ALU.add))
                    before = self.sums[:, g, j, :]
                v.tensor_copy(self.idx[:, g, :], src[:, bass.ds(t0 + STEP + g * G, G)]).then_inc(self.free, 1)

    def send(self, sp, sums):
        for g in range(RING):
            sp.sem_inc(self.sent[g], 16)
        view = sums.rearrange("(p t) d -> p t d", p=P)
        with sp.Fori(0, T - STEP + 1, STEP) as t0:
            for g in range(RING):
                sp.wait_ge(self.free, t0 // G + g + 1 + RING)
                sp.dma_start(view[:, bass.ds(t0 + g * G, G), :], self.sums[:, g, :, :]).then_inc(self.sent[g], 16)
        for g in range(RING):
            sp.wait_ge(self.sent[g], 16 * (ITERS + 1))


def collect(nc, c, io, S, walk, agg, fetched, before_fetch, p_count=None):
    carry = c.sb("carry", [P, N])
    p_c = [c.ps(f"carry{i}") for i in range(4)]
    ready, carried, added, made = [c.sem(x) for x in ("c_ready", "c_carried", "c_added", "c_made")]
    if p_count is not None:
        ends = Ends(c)
    with nc.Block() as block:

        @block.sync
        def _(sp):
            if p_count is not None:
                ends.store(sp, io, S)

        @block.gpsimd
        def _(pool):
            pool.iota(carry[:, :], [[1, N]], base=0, channel_multiplier=0,
                      allow_small_or_imprecise_dtypes=True).then_inc(made, 1)
            before_fetch(pool)
            if p_count is not None:
                pool.wait_ge(ends.fetched, 32)
            for t in range(NT):
                pool.indirect_dma_start(
                    out=agg[:, t, :], out_offset=None, in_=io["sums"],
                    in_offset=bass.IndirectOffsetOnAxis(ap=S.last[:, t:t + 1], axis=0),
                    bounds_check=E - 1, oob_is_err=False).then_inc(fetched, 16)

        @block.vector
        def _(v):
            if p_count is not None:
                ends.find(v, p_count)
            v.wait_ge(made, 1)
            v.tensor_scalar(carry[:, :], carry[:, :], S.goes_on[:, 0:1], None, ALU.is_equal).then_inc(ready, 1)
            if p_count is not None:
                place_nodes(v, ends, S)
            v.wait_ge(fetched, 16 * NT)
            for t in range(NT):
                v.wait_ge(carried, t + 1)
                v.tensor_tensor(agg[:, t, :], agg[:, t, :], p_c[t % 4][0:P, 0:D], ALU.add).then_inc(added, 1)
            v.wait_ge(added, NT)

        @block.tensor
        def _(pe):
            if p_count is not None:
                ends.sum(pe, S, ends.degree, 0)
            pe.wait_ge(ready, 1)
            for t in range(4):
                pe.matmul(p_c[t][0:P, 0:D], carry[:, t * P:(t + 1) * P], walk.end,
                          start=True, stop=True).then_inc(carried, 1)
            if p_count is not None:
                ends.sum(pe, S, ends.degree2, 1)
            for t in range(4, NT):
                if t >= 4:
                    pe.wait_ge(added, t - 3)
                pe.matmul(p_c[t % 4][0:P, 0:D], carry[:, t * P:(t + 1) * P], walk.end,
                          start=True, stop=True).then_inc(carried, 1)


class Ends:

    def __init__(self, c):
        self.degree, self.degree2, self.total, self.upto, self.last, self.start = [
            c.sb(x, [128, HI]) for x in ("degree", "degree2", "total", "upto", "last", "start")]
        self.last_i = c.sb("last_i", [128, HI], I32)
        self.p_s = c.ps("ends")
        self.dve, self.asked, self.summed, self.stored, self.fetched = [
            c.sem(x) for x in ("e_dve", "e_asked", "e_summed", "e_stored", "e_fetched")]
        self.rlast_out = c.sem("e_rlast_out")
        self.placed, self.step = c.sem("e_placed"), c.sem("e_step")

    def sum(self, pe, S, degree, i):
        at = 128 * i
        pe.wait_ge(self.asked, i + 1)
        pe.matmul(self.p_s[:, at:at + HI], S.ones[:, :], degree[:, :], start=True, stop=True)
        pe.matmul(self.p_s[:, at + 64:at + 64 + HI], S.tri[:, :], degree[:, :], start=True,
                  stop=True).then_inc(self.summed, 1)

    def cumulate(self, v, link, i):
        at = 128 * i
        v.wait_ge(self.summed, i + 1)
        link(v.tensor_copy(self.total[:, :], self.p_s[:, at:at + HI]))
        link(v.memset(self.start[:, :], 1.0))
        link(v.tensor_tensor_scan(self.upto[:, :], self.start[:, :], self.total[:, :], 0.0, ALU.mult, ALU.add))
        link(v.tensor_tensor(self.upto[:, :], self.upto[:, :], self.total[:, :], ALU.subtract))
        link(v.tensor_tensor(self.upto[:, :], self.upto[:, :], self.p_s[:, at + 64:at + 64 + HI], ALU.add))

    def find(self, v, p_count):
        link = linker(v, self.dve)
        link(v.tensor_copy(self.degree[:, :], p_count))
        v.sem_inc(self.asked, 1)
        self.cumulate(v, link, 0)
        link(v.tensor_scalar(self.last[:, :], self.degree[:, :], 0.0, None, ALU.is_equal))
        link(v.scalar_tensor_tensor(self.last[:, :], self.last[:, :], 3.0e7, self.upto[:, :], ALU.mult, ALU.add))
        link(v.tensor_scalar(self.last[:, :], self.last[:, :], 1.0, None, ALU.subtract))
        link(v.tensor_copy(self.last_i[:, :], self.last[:, :]))
        v.sem_inc(self.stored, 1)

    def store(self, sp, io, S):
        sp.wait_ge(self.stored, 1)
        sp.dma_start(io["last"].rearrange("(h l) -> l h", l=LO), self.last_i[:, :]).then_inc(self.fetched, 16)
        sp.wait_ge(self.fetched, 16)
        sp.dma_start(S.last[:, :], io["last"][0:N].rearrange("(t p) -> p t", p=P)).then_inc(self.fetched, 16)
        sp.wait_ge(self.placed, 1)
        sp.dma_start(io["last2"].rearrange("(h l) -> l h", l=LO), S.rlast_i[:, :]).then_inc(self.rlast_out, 16)
        sp.wait_ge(self.rlast_out, 16)


def place_nodes(v, ends, S):
    step = linker(v, ends.step)
    for h in range(HI):
        ins = v.tensor_tensor_scan(S.count[:, :, h], S.ones[:, 0:1].to_broadcast([128, GT + 1]), S.count[:, :, h],
                                   0.0, ALU.mult, ALU.add)
    step(ins)
    step(v.tensor_scalar(ends.degree2[:, :], S.count[:, GT, :], 1.0, None, ALU.add))
    v.sem_inc(ends.asked, 1)
    ends.cumulate(v, step, 1)
    step(v.tensor_scalar(ends.last[:, :], ends.upto[:, :], 1.0, None, ALU.subtract))
    step(v.tensor_copy(S.rlast_i[:, :], ends.last[:, :]))
    step(v.tensor_tensor(ends.upto[:, :], ends.upto[:, :], ends.degree2[:, :], ALU.subtract))
    step(v.tensor_copy(S.loop_i[:, :], ends.upto[:, :]))
    step(v.tensor_scalar(ends.upto[:, :], ends.upto[:, :], 1.0, None, ALU.add))
    step(v.tensor_tensor(S.count[:, 0:GT, :], S.count[:, 0:GT, :],
                         ends.upto[:, :].unsqueeze(1).to_broadcast([128, GT, HI]), ALU.add))
    v.tensor_copy(S.rdstf[:, :], S.rdst[:, :]).then_inc(ends.placed, 1)


def layer0_graph(nc, io, S):
    with ExitStack() as stack:
        c = Scope(nc, stack, "g0")
        kvT = c.sb("kvT", [128, KC, D])
        knorm = c.sb("knorm", [128, KC])
        walk = Walk(c, S, "w0")
        with ExitStack() as s2:
            q2T = Scope(nc, s2, "m0").sb("q2T", [128, KC, N])
            project0(nc, io, S, kvT, knorm, q2T, walk)
            p_count = c.ps("count")
            mix0(nc, io, S, kvT, knorm, q2T, walk, p_count)
        agg = c.sb("agg", [P, NT, D])

        def clear(pool):
            pool.memset(agg[:, :, :], 0.0).then_inc(cleared, 1)
            pool.wait_ge(cleared, 1)

        cleared = c.sem("cleared")
        with ExitStack() as s3:
            collect(nc, Scope(nc, s3, "g0c"), io, S, walk, agg, S.gathers["g0_fetched"], clear, p_count[:, 0:HI])
        with nc.Block() as block:
            @block.vector
            def _(v):
                v.tensor_tensor(S.x[:, :, :], S.x[:, :, :], agg[:, :, :], ALU.add)


def project0(nc, io, S, kvT, knorm, q2T, walk):
    W4 = 4 * D
    GROUPS = NT // U
    with ExitStack() as stack:
        c = Scope(nc, stack, "p0")
        w = c.sb("w", [128, KC, W4])
        bias = c.sb("bias", [3, W4])
        bias3 = c.sb("bias3", [3, W4], BF16)
        qk, vy0, sq, vy1 = [x.rearrange("p g j d -> p (g j d)").rearrange("p (u n) -> p u n", u=U)
                            for x in (walk.rows[:, 0:2, :, :], walk.rows[:, 2:4, :, :], walk.sums[:, 0:2, :, :],
                                      walk.sums[:, 3:5, :, :])]
        vy = (vy0, vy1)
        ksq = walk.sums[:, 2, :, :]
        junk = c.sb("junk", [P, D])
        stats = c.sb("stats", [P, 2 * U, 6])
        mean, diff, var, r, root, f = [c.sb(x, [P, 2 * U]) for x in ("mean", "diff", "var", "r", "root", "f")]
        ss = c.sb("ss", [P, U])
        p_qk = [c.ps(f"qk{i}") for i in range(2)]
        p_vy = [c.ps(f"vy{i}") for i in range(2)]
        p_t = c.ps("t")
        p_kv = c.ps("kv")
        p_ss = c.ps("ss")
        p_n = c.ps("n")
        hot_lo = c.sb("hot_lo", [128, 2, GB, LO], BF16)
        names = ("hot_made", "counted", "count_out", "loaded", "cleared", "multiplied", "evacuated", "dve",
                 "bias_in", "biased", "centred", "squared", "sum_ready", "rooted", "scaled", "turned", "copied", "group")
        (hot_made, counted, count_out, loaded, cleared, multiplied, evacuated, dve, bias_in, biased, centred, squared,
         sum_ready, rooted, scaled, turned, copied, group) = [c.sem(x) for x in names]
        table_out = [c.sem(f"table_out{i}") for i in range(2)]
        PAIRS = [(u, min(2, U - u)) for u in range(0, U, 2)]
        with nc.Block() as block:

            @block.sync
            def _(sp):
                sp.wait_ge(cleared, 1)
                sp.dma_start(bias[:, 0:3 * D], io["L0_mix_b_qkv"].rearrange("(a n) -> a n", a=1)
                             .to_broadcast([3, 3 * D])).then_inc(bias_in, 16)
                sp.dma_start(w[:, :, 0:3 * D], io["L0_mix_W_qkv"].rearrange("(k p) n -> p k n", p=128)).then_inc(loaded, 16)
                sp.dma_start(w[:, :, 3 * D:W4], io["L0_gnn_W"].rearrange("(k p) n -> p k n", p=128)).then_inc(loaded, 16)
                table = io["table"].rearrange("(t p) d -> p t d", p=P)
                for i in range(GROUPS):
                    sp.wait_ge(evacuated, (i + 1) * U)
                    sp.dma_start(table[:, i * U:(i + 1) * U, :], vy[i % 2][:, :, D:2 * D]).then_inc(table_out[i % 2], 16)
                sp.wait_ge(table_out[0], 16 * ((GROUPS + 1) // 2))
                sp.wait_ge(table_out[1], 16 * (GROUPS // 2))

            @block.gpsimd
            def _(pool):
                pool.memset(bias[:, :], 0.0).then_inc(cleared, 1)

            @block.tensor
            def _(pe):

                def project(i):
                    for t in range(i * U, (i + 1) * U):
                        if t >= 2:
                            pe.wait_ge(evacuated, t - 1)
                        for p_o, lo in ((p_qk, 0), (p_vy, 2 * D)):
                            for k in range(KC):
                                pe.matmul(p_o[t % 2][0:P, :], S.xnT[:, k, t * P:(t + 1) * P], w[:, k, lo:lo + 2 * D],
                                          start=(k == 0), stop=False)
                            mm = pe.matmul(p_o[t % 2][0:P, :], S.ones3[:, 0:P], bias3[:, lo:lo + 2 * D],
                                           start=False, stop=True)
                        mm.then_inc(multiplied, 1)

                def count(i):
                    for n in range(i * QB, (i + 1) * QB):
                        pe.wait_ge(hot_made, n + 1)
                        if n >= 1:
                            pe.wait_ge(count_out, n)
                        for j in range(GB):
                            mm = pe.matmul(p_n[:, j * HI:(j + 1) * HI], hot_lo[:, n % 2, j, :],
                                           S.hot_hi[:, n * GB + j, :], start=True, stop=True)
                        mm.then_inc(counted, 1)

                def context(i):
                    pe.wait_ge(scaled, i + 1)
                    for m, (u0, many) in enumerate(PAIRS):
                        if i * len(PAIRS) + m >= 1:
                            pe.wait_ge(copied, i * len(PAIRS) + m)
                        for u in range(u0, u0 + many):
                            for k in range(KC):
                                mm = pe.transpose(p_t[:, ((u - u0) * KC + k) * P:((u - u0) * KC + k + 1) * P],
                                                  sq[:, u, k * 128:(k + 1) * 128], S.ident[0:P, 0:P])
                        mm.then_inc(turned, 1)
                        for u in range(u0, u0 + many):
                            for k in range(KC):
                                pe.matmul(p_kv[:, k * D:(k + 1) * D], vy[i % 2][:, u, k * 128:(k + 1) * 128],
                                          sq[:, u, D:2 * D], start=False, stop=True, skip_group_check=True)
                                mm = pe.matmul(p_ss[:, k:k + 1], ksq[:, u, k * 128:(k + 1) * 128], S.ones[0:P, 0:1],
                                               start=False, stop=True, skip_group_check=True)
                    mm.then_inc(group, 1)

                pe.wait_ge(loaded, 2 * 16)
                pe.wait_ge(biased, 5)
                pe.wait_ge(dve, 2)
                project(0)
                count(0)
                for i in range(GROUPS):
                    if i + 1 < GROUPS:
                        project(i + 1)
                    context(i)
                    if i + 1 < GROUPS:
                        count(i + 1)

            @block.scalar
            def _(a):

                def evacuate(i, us):
                    for u in us:
                        t = i * U + u
                        if u == 0 and i >= 1:
                            a.wait_ge(squared, i * 2 * U)
                        if u == 0 and i >= 2:
                            a.wait_ge(group, i - 1)
                            a.wait_ge(table_out[i % 2], 16 * (i // 2))
                        a.wait_ge(multiplied, t + 1)
                        a.activation(qk[:, u, :], p_qk[t % 2][0:P, :], ACT.Copy)
                        a.activation(vy[i % 2][:, u, :], p_vy[t % 2][0:P, :], ACT.Copy).then_inc(evacuated, 1)

                def take_counts(i):
                    for n in range(i * QB, (i + 1) * QB):
                        a.wait_ge(counted, n + 1)
                        a.activation(S.count[:, n * GB + 1:(n + 1) * GB + 1, :].rearrange("p a b -> p (a b)"),
                                     p_n[:, 0:GB * HI], ACT.Copy).then_inc(count_out, 1)

                def square(i):
                    a.wait_ge(centred, i + 1)
                    if i >= 1:
                        a.wait_ge(group, i)
                    for j in range(2 * U):
                        half = slice((j % 2) * D, (j % 2 + 1) * D)
                        a.activation(sq[:, j // 2, half], qk[:, j // 2, half], ACT.Square,
                                     bias=mean[:, j:j + 1]).then_inc(squared, 1)

                evacuate(0, range(U))
                take_counts(0)
                square(0)
                for i in range(GROUPS):
                    if i + 1 < GROUPS:
                        evacuate(i + 1, range(2))
                    a.wait_ge(sum_ready, i + 1)
                    a.activation(root[:, 0:U], ss[:, :], ACT.Sqrt).then_inc(rooted, 1)
                    if i + 1 < GROUPS:
                        evacuate(i + 1, range(2, U))
                    for m, (u0, many) in enumerate(PAIRS):
                        a.wait_ge(turned, i * len(PAIRS) + m + 1)
                        n0 = (i * U + u0) * P
                        a.activation(q2T[:, :, n0:n0 + many * P].rearrange("q k (u p) -> q u k p", p=P),
                                     p_t[:, 0:many * KC * P].rearrange("q (u k p) -> q u k p", k=KC, p=P),
                                     ACT.Copy).then_inc(copied, 1)
                    if i + 1 < GROUPS:
                        take_counts(i + 1)
                        square(i + 1)

            @block.vector
            def _(v):
                v.wait_ge(bias_in, 16)
                exact_parts(linker(v, biased), v, S, bias[:, :], bias3[:, :])
                link = linker(v, dve)
                link(v.memset(p_kv[:, :], 0.0))
                link(v.memset(p_ss[:, :], 0.0))
                v.memset(S.count[:, 0, :], 0.0)

                def one_hot(i):
                    for n in range(i * QB, (i + 1) * QB):
                        if n >= 2:
                            v.wait_ge(counted, n - 1)
                        v.tensor_tensor(hot_lo[:, n % 2, :, :],
                                        S.rdst_lo[:, n * GB:(n + 1) * GB].unsqueeze(2).to_broadcast([128, GB, LO]),
                                        S.iota_lo[:, :].unsqueeze(1).to_broadcast([128, GB, LO]), ALU.is_equal)
                        v.tensor_tensor(S.hot_hi[:, n * GB:(n + 1) * GB, :],
                                        S.rdst_hi[:, n * GB:(n + 1) * GB].unsqueeze(2).to_broadcast([128, GB, HI]),
                                        S.iota_lo[:, 0:HI].unsqueeze(1).to_broadcast([128, GB, HI]),
                                        ALU.is_equal).then_inc(hot_made, 1)

                for i in range(GROUPS):
                    one_hot(i)
                    for j in range(2 * U):
                        if j % 2 == 0:
                            v.wait_ge(evacuated, i * U + j // 2 + 1)
                        ins = v.bn_stats(stats[:, j, :], qk[:, j // 2, (j % 2) * D:(j % 2 + 1) * D])
                    link(ins)
                    if i >= 1:
                        v.wait_ge(squared, i * 2 * U)
                    mean_and_var(link, stats, v, mean[:, :], var[:, :], diff[:, :], float(D), 1e-7)
                    link(v.tensor_scalar(mean[:, :], mean[:, :], -1.0, None, ALU.mult))
                    link(v.reciprocal(r[:, :], var[:, :]))
                    v.sem_inc(centred, 1)
                    for u in range(U):
                        v.wait_ge(squared, i * 2 * U + 2 * u + 2)
                        link(v.tensor_tensor_reduce(junk[:, :], sq[:, u, 0:D], sq[:, u, 0:D], 1.0, 0.0,
                                                    ALU.mult, ALU.add, ss[:, u:u + 1]))
                    v.sem_inc(sum_ready, 1)
                    v.wait_ge(rooted, i + 1)
                    rq = r[:, 0:2 * U:2]
                    link(v.tensor_tensor(f[:, 0:U], root[:, 0:U], rq, ALU.mult))
                    link(v.tensor_scalar(f[:, 0:U], f[:, 0:U], 1e-12, None, ALU.max))
                    link(v.reciprocal(f[:, 0:U], f[:, 0:U]))
                    link(v.tensor_tensor(f[:, 0:U], f[:, 0:U], rq, ALU.mult))
                    for u in range(U):
                        v.tensor_scalar(sq[:, u, 0:D], sq[:, u, 0:D], f[:, u:u + 1], None, ALU.mult)
                        ins = v.tensor_scalar(sq[:, u, D:2 * D], sq[:, u, D:2 * D], r[:, 2 * u + 1:2 * u + 2], None,
                                              ALU.mult)
                    link(ins)
                    link(v.tensor_tensor(ksq[:, :, :], sq[:, :, D:2 * D], sq[:, :, D:2 * D], ALU.mult))
                    v.sem_inc(scaled, 1)
                v.wait_ge(group, GROUPS)
                v.tensor_copy(kvT[:, :, :], p_kv[:, :].rearrange("p (k n) -> p k n", k=KC))
                v.tensor_copy(knorm[:, :], p_ss[:, 0:KC])


def mix0(nc, io, S, kvT, knorm, q2T, walk, p_count):
    TWICE = NT - ITERS
    SPANS = ((0, TWICE, {0: lambda i: i * 2, 2: lambda i: i * 2 + 1}), (TWICE, ITERS, {2: lambda i: i + TWICE}))
    SLOT = {0: 0, 2: 1}
    with ExitStack() as stack:
        c = Scope(nc, stack, "x0")
        wout = c.sb("wout", [128, KC, D])
        wvT = c.sb("wvT", [128, KC, D])
        bv = c.sb("bv", [128, KC])
        rows = c.sb("rows", [1, 3, D])
        root = c.sb("root", [128, KC])
        kvw = c.sb("kvw", [128, KC, D])
        wvw = c.sb("wvw", [128, KC, D])
        xq = c.sb("xq", [128, 2, 2 * KC, P])
        p_a, p_b, p_r = c.ps("a"), c.ps("b"), c.ps("r")
        p_o = [c.ps(f"o{i}") for i in range(2)]
        hot_lo = c.sb("hot_lo", [P, 2, G, LO], BF16)
        hot_hi = c.sb("hot_hi", [P, 2, G, HI], BF16)
        names = ("loaded", "small", "rooted", "dve", "staged", "multiplied", "added", "hot_made", "counted", "zeroed")
        loaded, small, rooted, dve, staged, multiplied, added, hot_made, counted, zeroed = [c.sem(x) for x in names]
        with nc.Block() as block:

            @block.sync
            def _(sp):
                sp.dma_start(wout[:, :, :], io["L0_mix_W_out"].rearrange("(k p) n -> p k n", p=128)).then_inc(loaded, 16)
                sp.dma_start(wvT[:, :, :], io["L0_mix_W_v_T"].rearrange("(k p) n -> p k n", p=128)).then_inc(loaded, 16)
                sp.dma_start(bv[:, :], io["L0_mix_b_qkv"][2 * D:3 * D].rearrange("(k p) -> p k", p=128)).then_inc(loaded, 16)
                sp.dma_start(rows[0:1, 0, :], io["L0_mix_b_out"].rearrange("(a n) -> a n", a=1)).then_inc(loaded, 16)
                sp.dma_start(rows[0:1, 1, :], io["L0_gnn_b"].rearrange("(a n) -> a n", a=1)).then_inc(loaded, 16)
                walk.send(sp, io["sums"])

            @block.gpsimd
            def _(pool):
                walk.gather(pool, io["table"])

            @block.tensor
            def _(pe):
                pe.wait_ge(loaded, 5 * 16)
                for m in range(KC):
                    for k in range(KC):
                        pe.matmul(p_a[:, m * D:(m + 1) * D], kvT[:, k, m * 128:(m + 1) * 128], wout[:, k, :],
                                  start=(k == 0), stop=(k == KC - 1))
                    for k in range(KC):
                        pe.matmul(p_b[:, m * D:(m + 1) * D], wvT[:, k, m * 128:(m + 1) * 128], wout[:, k, :],
                                  start=(k == 0), stop=(k == KC - 1))
                for k in range(KC):
                    mm = pe.matmul(p_r[0:1, 0:D], bv[:, k:k + 1], wout[:, k, :], start=(k == 0), stop=(k == KC - 1))
                mm.then_inc(small, 1)
                pe.wait_ge(dve, 8)
                pe.sem_inc(multiplied, 2)
                pe.sem_inc(counted, 2)
                pe.wait_ge(zeroed, 1)
                for begin, end, tile in SPANS:
                    with pe.Fori(begin * STEP, (end - 1) * STEP + 1, STEP) as t0:
                        for g in range(RING):
                            pe.wait_ge(hot_made, t0 // G + g + 1)
                            for j in range(G):
                                mm = pe.matmul(p_count[:, 0:HI], hot_lo[:, g % 2, j, :], hot_hi[:, g % 2, j, :],
                                               start=False, stop=True, skip_group_check=True)
                            mm.then_inc(counted, 1)
                            if g not in tile:
                                continue
                            t, slot = tile[g](t0 // STEP), SLOT[g]
                            pe.wait_ge(staged, t + 1)
                            pe.wait_ge(added, t + 1)
                            o = p_o[slot][0:P, 0:D]
                            for k in range(KC):
                                pe.matmul(o, xq[:, slot, k, :], wvw[:, k, :], start=(k == 0), stop=False)
                                pe.matmul(o, xq[:, slot, KC + k, :], kvw[:, k, :], start=False, stop=False)
                            pe.matmul(o, S.ones[0:1, 0:P], rows[0:1, 2, :], start=False,
                                      stop=True).then_inc(multiplied, 1)

            @block.scalar
            def _(a):
                a.activation(root[:, :], knorm[:, :], ACT.Sqrt).then_inc(rooted, 1)
                for begin, end, tile in SPANS:
                    with a.Fori(begin, end) as i:
                        for g in range(RING):
                            walk.weigh(a, S.w, i, g)
                            if g not in tile:
                                continue
                            t, slot = tile[g](i), SLOT[g]
                            a.wait_ge(multiplied, t + 2)
                            a.activation(xq[:, slot, 0:KC, :], S.xnT[:, :, bass.ds(t * P, P)], ACT.Copy)
                            a.activation(xq[:, slot, KC:2 * KC, :], q2T[:, :, bass.ds(t * P, P)],
                                         ACT.Copy).then_inc(staged, 1)

            @block.vector
            def _(v):
                link = linker(v, dve)
                walk.begin(v, S.src)
                v.wait_ge(rooted, 1)
                link(v.tensor_scalar(root[:, :], root[:, :], 1e-12, None, ALU.max))
                link(v.reciprocal(root[:, :], root[:, :]))
                link(v.tensor_scalar(root[:, :], root[:, :], float(N) ** -0.5, None, ALU.mult))
                v.wait_ge(small, 1)
                for k in range(KC):
                    link(v.tensor_scalar(kvw[:, k, :], p_a[:, k * D:(k + 1) * D], root[:, k:k + 1], None, ALU.mult))
                link(v.tensor_copy(wvw[:, :, :], p_b[:, :].rearrange("p (k n) -> p k n", k=KC)))
                link(v.tensor_tensor(rows[0:1, 2, :], rows[0:1, 0, :], rows[0:1, 1, :], ALU.add))
                link(v.tensor_tensor(rows[0:1, 2, :], rows[0:1, 2, :], p_r[0:1, 0:D], ALU.add))
                v.memset(p_count[:, 0:HI], 0.0).then_inc(zeroed, 1)
                v.sem_inc(added, 1)

                def one_hot(g, t, n):
                    v.wait_ge(counted, n + (2 if g == 0 else 1))
                    v.tensor_tensor(hot_lo[:, g % 2, :, :],
                                    S.dst_lo[:, bass.ds(t, G)].unsqueeze(2).to_broadcast([P, G, LO]),
                                    S.iota_lo[0:P, :].unsqueeze(1).to_broadcast([P, G, LO]), ALU.is_equal)
                    v.tensor_tensor(hot_hi[:, g % 2, :, :],
                                    S.dst_hi[:, bass.ds(t, G)].unsqueeze(2).to_broadcast([P, G, HI]),
                                    S.iota_lo[0:P, 0:HI].unsqueeze(1).to_broadcast([P, G, HI]),
                                    ALU.is_equal).then_inc(hot_made, 1)

                for begin, end, tile in SPANS:

                    def beside(g, t, n, i):
                        one_hot(g, t, n)
                        if g - 1 in tile:
                            m = tile[g - 1](i)
                            xt = S.x[:, bass.ds(m, 1), :].rearrange("p a b -> p (a b)")
                            v.wait_ge(multiplied, m + 1 + 2)
                            v.tensor_tensor(xt, xt, p_o[SLOT[g - 1]][0:P, 0:D], ALU.add).then_inc(added, 1)

                    walk.walk(v, S.src, S.keep, begin, end, beside)
                v.wait_ge(counted, T // G + 2)


def layer0_experts(nc, io, S):
    with ExitStack() as stack:
        c = Scope(nc, stack, "e0")
        hot = c.sb("hot", [P, NT, NX])
        hotT = c.sb("hotT", [NX, N])
        off = c.sb("off", [NX, N], BF16)
        weights = (c.sb("w1", [128, KC, NX * HX]), c.sb("w2", [128, NC0, D]), c.sb("b1", [128, NC0]), c.sb("b2", [NX, D]))
        weights_in = c.sem("weights_in")
        route0(nc, io, S, hot, hotT, off, weights, weights_in)
        experts0(nc, io, S, hotT, off, weights, weights_in)


def route0(nc, io, S, hot, hotT, off, weights, weights_in):
    with ExitStack() as stack:
        c = Scope(nc, stack, "r0")
        rw = c.sb("rw", [128, KC, NX])
        rb = c.sb("rb", [1, NX])
        logits = c.sb("logits", [P, NT, NX])
        order = c.sb("order", [P, NX])
        top = c.sb("top", [P, NT])
        half = 512 // NX
        p_l = [c.ps(f"l{i}") for i in range(2)]
        p_t = [c.ps(f"t{i}") for i in range(2)]
        loaded, made, routed, dve, turned, copied = [
            c.sem(x) for x in ("loaded", "made", "routed", "dve", "turned", "copied")]
        with nc.Block() as block:

            @block.sync
            def _(sp):
                sp.dma_start(rw[:, :, :], io["L0_ffn_router_w"].rearrange("(k p) n -> p k n", p=128)).then_inc(loaded, 16)
                sp.dma_start(rb[:, :], io["L0_ffn_router_b"].rearrange("(a n) -> a n", a=1)).then_inc(loaded, 16)
                w1, w2, b1, b2 = weights
                sp.dma_start(w1[:, :, :], io["L0_ffn_W1"].rearrange("(k p) n -> p k n", p=128)).then_inc(weights_in, 16)
                sp.dma_start(w2[:, :, :], io["L0_ffn_W2"].rearrange("(c p) n -> p c n", p=128)).then_inc(weights_in, 16)
                sp.dma_start(b1[:, :], io["L0_ffn_b1"]).then_inc(weights_in, 16)
                sp.dma_start(b2[:, :], io["L0_ffn_b2"]).then_inc(weights_in, 16)

            @block.gpsimd
            def _(pool):
                pool.iota(order[:, :], [[-1, NX]], base=NX, channel_multiplier=0,
                          allow_small_or_imprecise_dtypes=True).then_inc(made, 1)

            @block.tensor
            def _(pe):
                pe.wait_ge(loaded, 32)
                for t in range(NT):
                    o = p_l[t // half][0:P, (t % half) * NX:(t % half + 1) * NX]
                    for k in range(KC):
                        pe.matmul(o, S.xnT[:, k, t * P:(t + 1) * P], rw[:, k, :], start=(k == 0), stop=False)
                    mm = pe.matmul(o, S.ones[0:1, 0:P], rb[0:1, :], start=False, stop=True)
                mm.then_inc(routed, 1)
                pe.wait_ge(dve, 7)
                for t in range(NT):
                    if t >= 2:
                        pe.wait_ge(copied, t - 1)
                    pe.transpose(p_t[t % 2][0:NX, 0:P], hot[:, t, :], S.ident[0:P, 0:P]).then_inc(turned, 1)

            @block.scalar
            def _(a):
                for t in range(NT):
                    a.wait_ge(turned, t + 1)
                    a.activation(hotT[:, t * P:(t + 1) * P], p_t[t % 2][0:NX, 0:P], ACT.Copy).then_inc(copied, 1)

            @block.vector
            def _(v):
                link = linker(v, dve)
                v.wait_ge(routed, 1)
                v.wait_ge(made, 1)
                link(v.tensor_copy(logits[:, 0:half, :], p_l[0][0:P, 0:half * NX].rearrange("p (t e) -> p t e", e=NX)))
                link(v.tensor_copy(logits[:, half:NT, :],
                                   p_l[1][0:P, 0:(NT - half) * NX].rearrange("p (t e) -> p t e", e=NX)))
                ranked = order[:, :].unsqueeze(1).to_broadcast([P, NT, NX])
                link(v.tensor_reduce(top[:, :], logits[:, :, :], AX.X, ALU.max))
                link(v.tensor_tensor(hot[:, :, :], logits[:, :, :], top[:, :].unsqueeze(2).to_broadcast([P, NT, NX]),
                                     ALU.is_equal))
                link(v.tensor_tensor(hot[:, :, :], hot[:, :, :], ranked, ALU.mult))
                link(v.tensor_reduce(top[:, :], hot[:, :, :], AX.X, ALU.max))
                link(v.tensor_tensor(hot[:, :, :], ranked, top[:, :].unsqueeze(2).to_broadcast([P, NT, NX]),
                                     ALU.is_equal))
                v.wait_ge(copied, NT)
                link(v.tensor_scalar(off[:, :], hotT[:, :], 1.0, BIG, ALU.subtract, ALU.mult))


def experts0(nc, io, S, hotT, off, weights, weights_in):
    B = U * P
    CUT = ((0, 3 * P, 0), (3 * P, B, 512))
    with ExitStack() as stack:
        c = Scope(nc, stack, "f0")
        w1, w2, b1, b2 = weights
        sel = c.sb("sel", [NX, NC0, 2, HX], BF16)
        hot = c.sb("hot", [NX, B])
        hid = c.sb("hid", [128, 2, B])
        p_h = [c.ps(f"h{i}", (128, 1024)) for i in range(2)]
        p_o = c.ps("o", (128, 1536))
        sort = Places(c, S)
        names = ("made", "hidden", "active", "staged", "done", "added")
        made, hidden, active, staged, done, added = [c.sem(x) for x in names]
        with nc.Block() as block:

            @block.sync
            def _(sp):
                sort.load_rows(sp, io)

            @block.gpsimd
            def _(pool):
                pool.memset(sel[:, :, :, :], 0.0).then_inc(made, 1)
                pool.wait_ge(made, 1)
                pool.affine_select(out=sel[:, :, :, :], in_=sel[:, :, :, :], compare_op=ALU.not_equal, fill=1.0,
                                   base=0, pattern=[[-2, NC0], [-1, 2], [0, HX]], channel_multiplier=1).then_inc(made, 1)
                sort.scatter(pool, io, S)

            @block.tensor
            def _(pe):
                pe.wait_ge(weights_in, 4 * 16)
                pe.wait_ge(made, 2)
                with pe.Fori(0, NT - U + 1, U) as t0:
                    n0 = t0 * P

                    def make_hidden(ch):
                        pe.wait_ge(active, (t0 // U) * NC0 + ch + 1)
                        for lo, hi, at in CUT:
                            o = p_h[ch % 2][:, at:at + hi - lo]
                            for k in range(KC):
                                pe.matmul(o, w1[:, k, ch * 128:(ch + 1) * 128], S.xnT[:, k, bass.ds(n0 + lo, hi - lo)],
                                          start=(k == 0), stop=False)
                            mm = pe.matmul(o, sel[:, ch, :, :].rearrange("e a h -> e (a h)"),
                                           off[:, bass.ds(n0 + lo, hi - lo)], start=False, stop=True)
                        mm.then_inc(hidden, 1)

                    def add_output(ch):
                        pe.wait_ge(active, (t0 // U) * NC0 + ch + 3)
                        for u in range(U):
                            mm = pe.matmul(p_o[0:P, u * D:(u + 1) * D], hid[:, ch % 2, u * P:(u + 1) * P],
                                           w2[:, ch, :], start=False, stop=(ch == NC0 - 1), skip_group_check=True)
                        mm.then_inc(done, 1)

                    make_hidden(0)
                    pe.wait_ge(staged, t0 // U + 1)
                    for u in range(U):
                        pe.matmul(p_o[0:P, u * D:(u + 1) * D], hot[:, u * P:(u + 1) * P], b2[:, :],
                                  start=False, stop=False, skip_group_check=True)
                    for ch in range(NC0):
                        if ch + 1 < NC0:
                            make_hidden(ch + 1)
                        add_output(ch)
                        if ch % (NC0 // QB) == 1:
                            sort.fetch(pe, t0 // U, ch // (NC0 // QB))

            @block.scalar
            def _(a):
                a.wait_ge(weights_in, 4 * 16)
                a.sem_inc(active, 2)
                a.sem_inc(done, 2)
                with a.Fori(0, NT - U + 1, U) as t0:
                    for ch in range(NC0):
                        a.wait_ge(hidden, (t0 // U) * NC0 + ch + 1)
                        a.wait_ge(done, (t0 // U) * NC0 + ch + 1)
                        for lo, hi, at in CUT:
                            ins = a.activation(hid[:, ch % 2, lo:hi], p_h[ch % 2][:, at:at + hi - lo], ACT.Relu,
                                               bias=b1[:, ch:ch + 1])
                        ins.then_inc(active, 1)

            @block.vector
            def _(v):
                v.sem_inc(added, 1)
                sort.begin(v)
                with v.Fori(0, NT - U + 1, U) as t0:
                    v.wait_ge(added, t0 + 1)
                    v.memset(p_o[0:P, 0:U * D], 0.0)
                    v.tensor_copy(hot[:, :], hotT[:, bass.ds(t0 * P, B)]).then_inc(staged, 1)
                    for b in range(QB):
                        sort.rank_and_place(v, S, t0 // U, b)
                    v.wait_ge(done, (t0 // U) * NC0 + NC0 + 2)
                    for u in range(U):
                        xt = S.x[:, bass.ds(t0 + u, 1), :].rearrange("p a b -> p (a b)")
                        v.scalar_tensor_tensor(xt, p_o[0:P, u * D:(u + 1) * D], 0.0, xt,
                                               ALU.max, ALU.add).then_inc(added, 1)


class Places:

    def __init__(self, c, S):
        self.row = c.sb("z_row", [128, 2, GB * 128], I32)
        self.row_lo = c.sb("z_row_lo", [128, GB * 128], I32)
        self.hotT = c.sb("z_hotT", [128, GB * 128], BF16)
        self.parts = c.sb("z_parts", [128, 2, GB, HI], BF16)
        self.junk = c.sb("z_junk", [128, GB, 128], BF16)
        self.picked = c.sb("z_picked", [128, GB, HI])
        self.place = c.sb("z_place", [128, GB])
        self.rank = c.sb("z_rank", [128, GB])
        self.place_i = c.sb("z_place_i", [128, 2, GB], I32)
        self.record = c.sb("z_record", [128, 2, GB, 2], I32)
        self.loop_rec = c.sb("z_loop_rec", [128, HI, 2], I32)
        self.pad = c.sb("z_pad", [1, GP - GN, 2], I32)
        self.p_g = c.ps("z_g")
        self.hot_made, self.fetched, self.step, self.ready, self.used, self.made, self.pads, self.asked = [
            c.sem("z_" + x) for x in ("hot_made", "fetched", "step", "ready", "used", "made", "pads", "asked")]
        self.rows_in = [c.sem(f"z_rows_in{i}") for i in range(2)]
        self.sent = [S.gathers[f"so_sent{i}"] for i in range(2)]
        self.loops_sent = S.gathers["so_loops_sent"]

    def load_rows(self, sp, io):
        sp.wait_ge(self.made, 3)
        sp.dma_start(io["sorted"][GN:GP, :].rearrange("(a n) c -> a n c", a=1), self.pad[:, :, :]).then_inc(self.pads, 16)
        with sp.Fori(0, GT // GB - 1, 2) as n0:
            for i in range(2):
                sp.wait_ge(self.used, n0 + i + 1)
                sp.dma_start(self.row[:, i, :], io["edge_row"][:, bass.ds((n0 + i) * GB * 128, GB * 128)]
                             .to_broadcast([128, GB * 128])).then_inc(self.rows_in[i], 16)
        sp.wait_ge(self.pads, 16)

    def fetch(self, pe, i, b):
        n = i * QB + b
        pe.wait_ge(self.hot_made, n + 1)
        pe.wait_ge(self.used, n + 2)
        for j in range(GB):
            for i in range(2):
                mm = pe.matmul(self.p_g[:, j * HI:(j + 1) * HI], self.hotT[:, j * 128:(j + 1) * 128],
                               self.parts[:, i, j, :], start=(i == 0), stop=(i == 1))
        mm.then_inc(self.fetched, 1)

    def begin(self, v):
        v.sem_inc(self.used, 2)

    def rank_and_place(self, v, S, i, b):
        n = i * QB + b
        link = linker(v, self.step, n * 7)
        v.wait_ge(self.rows_in[b % 2], (i * (QB // 2) + b // 2) * 16 + 16)
        link(v.tensor_scalar(self.row_lo[:, :], self.row[:, b % 2, :], LO - 1, None, ALU.bitwise_and))
        base = S.count[:, bass.ds(n * GB, GB), :]
        link(v.tensor_copy(self.parts[:, 0, :, :], base))
        v.tensor_tensor(self.parts[:, 1, :, :], base, self.parts[:, 0, :, :], ALU.subtract)
        v.tensor_scalar(self.hotT[:, :], self.row_lo[:, :], S.row[:, 0:1], None, ALU.is_equal).then_inc(self.hot_made, 1)
        for j in range(GB):
            ins = v.scalar_tensor_tensor(self.junk[:, j, :], self.row[:, b % 2, j * 128:(j + 1) * 128],
                                         S.rdstf[:, bass.ds(n * GB + j, 1)], S.below[:, :], ALU.is_equal, ALU.mult,
                                         accum_out=self.rank[:, j:j + 1])
        link(ins)
        v.wait_ge(self.fetched, n + 1)
        link(v.tensor_tensor(self.picked[:, :, :], self.p_g[:, 0:GB * HI].rearrange("p (a b) -> p a b", b=HI),
                             S.hot_hi[:, bass.ds(n * GB, GB), :], ALU.mult))
        link(v.tensor_reduce(self.place[:, :], self.picked[:, :, :], AX.X, ALU.add))
        link(v.tensor_tensor(self.place[:, :], self.place[:, :], self.rank[:, :], ALU.add))
        v.wait_ge(self.asked, n + 1)
        v.tensor_copy(self.record[:, b % 2, :, 0], S.rsrc[:, bass.ds(n * GB, GB)])
        v.tensor_copy(self.record[:, b % 2, :, 1], S.rdst[:, bass.ds(n * GB, GB)])
        link(v.tensor_copy(self.place_i[:, b % 2, :], self.place[:, :]))
        v.sem_inc(self.ready, 1)
        v.sem_inc(self.used, 1)

    def scatter(self, pool, io, S):
        pool.iota(self.loop_rec[:, :, :], [[LO, HI], [0, 2]], base=0, channel_multiplier=1).then_inc(self.made, 1)
        pool.memset(self.pad[:, :, 0:1], 0).then_inc(self.made, 1)
        pool.memset(self.pad[:, :, 1:2], N).then_inc(self.made, 1)
        pool.wait_ge(self.made, 3)
        for h in range(HI):
            pool.indirect_dma_start(
                out=io["sorted"], out_offset=bass.IndirectOffsetOnAxis(ap=S.loop_i[:, h:h + 1], axis=0),
                in_=self.loop_rec[:, h, :], in_offset=None,
                bounds_check=GN - 1, oob_is_err=False).then_inc(self.loops_sent, 16)
        pool.sem_inc(self.asked, 2)
        with pool.Fori(0, GT // GB - 1, 2) as n0:
            for i in range(2):
                pool.wait_ge(self.ready, n0 + i + 1)
                pool.sem_inc(self.made, 1)
                for j in range(GB):
                    pool.indirect_dma_start(
                        out=io["sorted"], out_offset=bass.IndirectOffsetOnAxis(ap=self.place_i[:, i, j:j + 1], axis=0),
                        in_=self.record[:, i, j, :], in_offset=None,
                        bounds_check=GN - 1, oob_is_err=False).then_inc(self.sent[i], 16)
                pool.wait_ge(self.sent[i], (n0 // 2) * (16 * GB) + 16 * GB)
                pool.sem_inc(self.asked, 1)
        pool.wait_ge(self.loops_sent, 16 * HI)


def segment_scan(nc, tag, S, out, src, keep, joins, cols, op, reverse=False):
    C = src.shape[1]
    add = op == ALU.add
    combine = ALU.mult if add else ALU.add
    zero = 0.0 if add else -BIG
    with ExitStack() as stack:
        c = Scope(nc, stack, tag)
        gate = c.sb("gate", [P, cols + 1])
        ends = c.sb("ends", [P, C])
        through = c.sb("through", [P, C])
        enters = c.sb("enters", [P, 1])
        endsT = c.sb("endsT", [C, P])
        throughT = c.sb("throughT", [C, P])
        chain = c.sb("chain", [C, P])
        shifted = c.sb("shifted", [C, P])
        begin = c.sb("begin", [P, C])
        p_a, p_b, p_c = c.ps("a"), c.ps("b"), c.ps("c")
        dve, pe_done = c.sem("dve"), c.sem("turned")

        def turned(ap):
            return ap[:, ::-1] if reverse else ap

        with nc.Block() as block:

            @block.vector
            def _(v):
                link = linker(v, dve)
                link(v.memset(gate[:, cols:cols + 1], 1.0))
                link(v.tensor_copy(gate[:, 0:cols], keep))
                join = joins[:, 1:2] if reverse else joins[:, 0:1]
                link(v.tensor_tensor(through[:, 0:1], join, joins[:, 2:3], ALU.mult))
                link(v.tensor_copy(enters[:, :], join))
                if not add:
                    for flag in (gate[:, :], through[:, 0:1], enters[:, :]):
                        link(v.tensor_scalar(flag, flag, 1.0, BIG, ALU.subtract, ALU.mult))
                if C > 1:
                    link(v.tensor_copy(through[:, 1:C], through[:, 0:1].to_broadcast([P, C - 1])))
                gates = turned(gate[:, 1:cols + 1] if reverse else gate[:, 0:cols])

                def scan(begins):
                    for ch in range(C):
                        ins = v.tensor_tensor_scan(turned(out[:, ch, :]), gates, turned(src[:, ch, :]), begins(ch),
                                                   combine, op)
                    link(ins)

                scan(lambda ch: zero)
                at = 0 if reverse else cols - 1
                link(v.tensor_copy(ends[:, :], out[:, :, at]))
                v.wait_ge(pe_done, 1)
                link(v.tensor_copy(endsT[:, :], p_a[0:C, 0:P]))
                link(v.tensor_copy(throughT[:, :], p_b[0:C, 0:P]))
                link(v.tensor_tensor_scan(turned(chain[:, :]), turned(throughT[:, :]), turned(endsT[:, :]), zero,
                                          combine, op))
                link(v.memset(shifted[:, :], zero))
                if reverse:
                    link(v.tensor_copy(shifted[:, 0:P - 1], chain[:, 1:P]))
                else:
                    link(v.tensor_copy(shifted[:, 1:P], chain[:, 0:P - 1]))
                v.sem_inc(pe_done, 1)
                v.wait_ge(pe_done, 3)
                link(v.tensor_scalar(begin[:, :], p_c[0:P, 0:C], enters[:, 0:1], None, combine))
                scan(lambda ch: begin[:, ch:ch + 1])

            @block.tensor
            def _(pe):
                pe.wait_ge(dve, 5 + (0 if add else 3) + (1 if C > 1 else 0) + 1)
                pe.transpose(p_a[0:C, 0:P], ends[:, :], S.ident[0:P, 0:P])
                pe.transpose(p_b[0:C, 0:P], through[:, :], S.ident[0:P, 0:P]).then_inc(pe_done, 1)
                pe.wait_ge(pe_done, 2)
                pe.transpose(p_c[0:P, 0:C], shifted[:, :], S.ident[0:C, 0:C]).then_inc(pe_done, 1)


def layer1_graph(nc, io, S):
    with ExitStack() as stack:
        c = Scope(nc, stack, "g1")
        agg = c.sb("agg", [P, NT, D])
        xn = c.sb("xn", [P, NT, D])
        with ExitStack() as s2:
            S.xnT = Scope(nc, s2, "n2").sb("xnT", [128, KC, N])
            normalize(nc, "n2", S, xn, S.xnT)
            project1(nc, io, S, agg)
            mix1(nc, io, S)
        ends = c.sb("ends", [P, D + NH])
        with ExitStack() as s2:
            c2 = Scope(nc, s2, "t1")
            top = c2.sb("top", [P, NH, T + 1])
            den = c2.sb("den", [P, NH, T + 1])
            attend_edges(nc, io, S, top, den, ends)
            settle_edges(nc, io, S, top, den, ends, agg)
        den = c.sb("dens", [P, NT, 2 * NH])
        collect1(nc, io, S, agg, den, ends)
        finish1(nc, io, S, agg, den[:, :, NH:2 * NH], xn)


def project1(nc, io, S, agg):
    with ExitStack() as stack:
        c = Scope(nc, stack, "p1")
        w = c.sb("w", [128, KC, 3 * D])
        query = c.sb("query", [128, KC, 3])
        bias = c.sb("bias", [3, 3 * D])
        bias3 = c.sb("bias3", [3, 3 * D], BF16)
        qk = c.sb("qk", [P, U, 2 * D])
        p_qk = [c.ps(f"qk{i}") for i in range(3)]
        p_v = [c.ps(f"v{i}") for i in range(3)]
        names = ("loaded", "biased", "multiplied", "evacuated", "v_out", "out", "v_sent", "dve")
        loaded, biased, multiplied, evacuated, v_out, out, v_sent, dve = [c.sem(x) for x in names]
        with nc.Block() as block:

            @block.sync
            def _(sp):
                for i, n in enumerate("qkv"):
                    sp.dma_start(w[:, :, i * D:(i + 1) * D],
                                 io[f"L1_gnn_W{n}"].rearrange("(k p) n -> p k n", p=128)).then_inc(loaded, 16)
                    sp.dma_start(bias[:, i * D:(i + 1) * D], io[f"L1_gnn_b{n}"].rearrange("(a n) -> a n", a=1)
                                 .to_broadcast([3, D])).then_inc(loaded, 16)
                for i in range(3):
                    sp.dma_start(query[:, :, i],
                                 io["L1_gnn_query_emb"].rearrange("(k p) -> p k", p=128)).then_inc(loaded, 16)
                for g in range(NT // U):
                    sp.wait_ge(evacuated, U * (g + 1))
                    for i, table in enumerate((io["queries"], io["keys_values"][:, 0:D])):
                        sp.dma_start(table.rearrange("(t p) d -> p t d", p=P)[:, g * U:(g + 1) * U, :],
                                     qk[:, :, i * D:(i + 1) * D]).then_inc(out, 16)
                    sp.wait_ge(v_out, U * (g + 1))
                    sp.dma_start(io["keys_values"][:, D:2 * D].rearrange("(t p) d -> p t d", p=P)[:, g * U:(g + 1) * U, :],
                                 agg[:, g * U:(g + 1) * U, :]).then_inc(v_sent, 16)
                sp.wait_ge(out, 32 * (NT // U))
                sp.wait_ge(v_sent, 16 * (NT // U))

            @block.tensor
            def _(pe):
                pe.wait_ge(loaded, 9 * 16)
                for lo, hi, o in ((0, 2 * D, p_qk[0]), (2 * D, 3 * D, p_v[0])):
                    for k in range(KC):
                        mm = pe.matmul(o[0:3, 0:hi - lo], query[:, k, :], w[:, k, lo:hi],
                                       start=(k == 0), stop=(k == KC - 1))
                mm.then_inc(biased, 1)
                pe.wait_ge(dve, 7)
                for t in range(NT):
                    if t >= 3:
                        pe.wait_ge(evacuated, t - 2)
                        pe.wait_ge(v_out, t - 2)
                    for lo, hi, o in ((0, 2 * D, p_qk[t % 3]), (2 * D, 3 * D, p_v[t % 3])):
                        for k in range(KC):
                            pe.matmul(o[0:P, 0:hi - lo], S.xnT[:, k, t * P:(t + 1) * P], w[:, k, lo:hi],
                                      start=(k == 0), stop=False)
                        mm = pe.matmul(o[0:P, 0:hi - lo], S.ones3[:, 0:P], bias3[:, lo:hi], start=False, stop=True)
                    mm.then_inc(multiplied, 1)

            @block.scalar
            def _(a):
                for t in range(NT):
                    a.wait_ge(multiplied, t + 1)
                    if t >= U and t % U == 0:
                        a.wait_ge(out, 32 * (t // U))
                    a.activation(qk[:, t % U, :], p_qk[t % 3][0:P, :], ACT.Copy).then_inc(evacuated, 1)

            @block.vector
            def _(v):
                v.wait_ge(biased, 1)
                link = linker(v, dve)
                link(v.scalar_tensor_tensor(bias[:, 0:2 * D], p_qk[0][0:3, :], 0.1, bias[:, 0:2 * D],
                                            ALU.mult, ALU.add))
                link(v.scalar_tensor_tensor(bias[:, 2 * D:3 * D], p_v[0][0:3, 0:D], 0.1, bias[:, 2 * D:3 * D],
                                            ALU.mult, ALU.add))
                exact_parts(link, v, S, bias[:, :], bias3[:, :])
                for t in range(NT):
                    v.wait_ge(multiplied, t + 1)
                    v.tensor_copy(agg[:, t, :], p_v[t % 3][0:P, 0:D]).then_inc(v_out, 1)


def mix1(nc, io, S):
    W = 128
    HW = 32
    PIECES = [(n, min(512, N - n)) for n in range(0, N, 512)]
    with ExitStack() as stack:
        c = Scope(nc, stack, "x1")
        w = c.sb("w", [128, KC, 3 * W])
        wqT = c.sb("wqT", [W, D])
        wout = c.sb("wout", [W, D])
        bout = c.sb("bout", [1, D])
        kT = c.sb("kT", [W, N])
        top = c.sb("top", [W, 8])
        total = c.sb("total", [W, 8])
        norm = c.sb("norm", [W, 2])
        kv = c.sb("kv", [P, 2, 2 * W])
        ctx = c.sb("ctx", [W, W])
        cw = c.sb("cw", [W, D])
        fold = c.sb("fold", [128, KC, D])
        names = ("loaded", "keys", "topped", "raised", "turned", "copied", "context", "dve", "small", "mult", "added")
        loaded, keys, topped, raised, turned, copied, context, dve, small, mult, added = [c.sem(x) for x in names]
        with nc.Block() as block, ExitStack() as ps:
            p_k = [ps.enter_context(nc.psum_tensor(f"x1_p_k{i}", [128, 512], F32)) for i in range(len(PIECES))]
            p_c = ps.enter_context(nc.psum_tensor("x1_p_c", [128, 512], F32))
            p_kv = p_k[0:2]
            p_w, p_f = p_k[2], p_k[3]
            p_o = p_k[4:7]

            @block.sync
            def _(sp):
                sp.dma_start(w[:, :, :], io["L1_mix_W_qkv"].rearrange("(k p) n -> p k n", p=128)).then_inc(loaded, 16)
                sp.dma_start(wqT[:, :], io["L1_mix_W_q_T"]).then_inc(loaded, 16)
                sp.dma_start(wout[:, :], io["L1_mix_W_out"]).then_inc(loaded, 16)
                sp.dma_start(bout[:, :], io["L1_mix_b_out"].rearrange("(a n) -> a n", a=1)).then_inc(loaded, 16)

            @block.tensor
            def _(pe):
                pe.wait_ge(loaded, 4 * 16)
                for i, (n, m) in enumerate(PIECES):
                    for k in range(KC):
                        mm = pe.matmul(p_k[i][:, 0:m], w[:, k, W:2 * W], S.xnT[:, k, n:n + m],
                                       start=(k == 0), stop=(k == KC - 1))
                    mm.then_inc(keys, 1)
                pe.wait_ge(raised, len(PIECES))
                for t in range(NT):
                    if t >= 2:
                        pe.wait_ge(copied, t - 1)
                    pe.transpose(p_kv[t % 2][0:P, 0:W], kT[:, t * P:(t + 1) * P], S.ident[:, :])
                    for k in range(KC):
                        mm = pe.matmul(p_kv[t % 2][0:P, W:2 * W], S.xnT[:, k, t * P:(t + 1) * P], w[:, k, 2 * W:3 * W],
                                       start=(k == 0), stop=(k == KC - 1))
                    mm.then_inc(turned, 1)
                    if t >= 1:
                        pe.wait_ge(copied, t)
                        pe.matmul(p_c[:, 0:W], kv[:, (t - 1) % 2, W:2 * W], kv[:, (t - 1) % 2, 0:W],
                                  start=(t == 1), stop=False).then_inc(context, 1)
                pe.wait_ge(copied, NT)
                pe.matmul(p_c[:, 0:W], kv[:, (NT - 1) % 2, W:2 * W], kv[:, (NT - 1) % 2, 0:W],
                          start=False, stop=True).then_inc(context, 1)
                pe.wait_ge(dve, 8)
                pe.matmul(p_w[:, 0:D], ctx[:, :], wout[:, :], start=True, stop=True).then_inc(small, 1)
                pe.wait_ge(dve, 9)
                for k in range(KC):
                    mm = pe.matmul(p_f[:, k * D:(k + 1) * D], wqT[:, k * 128:(k + 1) * 128], cw[:, :],
                                   start=True, stop=True)
                mm.then_inc(small, 1)
                pe.wait_ge(dve, 10)
                for t in range(NT):
                    if t >= 3:
                        pe.wait_ge(added, t - 2)
                    o = p_o[t % 3][0:P, 0:D]
                    for k in range(KC):
                        pe.matmul(o, S.xnT[:, k, t * P:(t + 1) * P], fold[:, k, :], start=(k == 0), stop=False)
                    pe.matmul(o, S.ones[0:1, 0:P], bout[0:1, :], start=False, stop=True).then_inc(mult, 1)

            @block.scalar
            def _(a):
                a.wait_ge(topped, 1)
                for i, (n, m) in enumerate(PIECES):
                    a.activation(kT[:, n:n + m], p_k[i][:, 0:m], ACT.Exp, bias=norm[:, 0:1],
                                 accum_out=total[:, i:i + 1]).then_inc(raised, 1)
                for t in range(NT):
                    a.wait_ge(turned, t + 1)
                    if t >= 2:
                        a.wait_ge(context, t - 1)
                    a.activation(kv[:, t % 2, :], p_kv[t % 2][0:P, 0:2 * W], ACT.Copy).then_inc(copied, 1)

            @block.vector
            def _(v):
                link = linker(v, dve)
                for i, (n, m) in enumerate(PIECES):
                    v.wait_ge(keys, i + 1)
                    ins = v.tensor_reduce(top[:, i:i + 1], p_k[i][:, 0:m], AX.X, ALU.max)
                link(ins)
                link(v.tensor_reduce(norm[:, 1:2], top[:, 0:len(PIECES)], AX.X, ALU.max))
                link(v.tensor_scalar(norm[:, 0:1], norm[:, 1:2], -1.0, None, ALU.mult))
                v.sem_inc(topped, 1)
                v.wait_ge(raised, len(PIECES))
                link(v.tensor_reduce(norm[:, 1:2], total[:, 0:len(PIECES)], AX.X, ALU.add))
                link(v.reciprocal(norm[:, 1:2], norm[:, 1:2]))
                link(v.tensor_scalar(norm[:, 1:2], norm[:, 1:2], float(HW) ** -0.5, None, ALU.mult))
                link(v.memset(ctx[:, :], 0.0))
                v.wait_ge(context, NT)
                for h in range(W // HW):
                    blk = slice(h * HW, (h + 1) * HW)
                    ins = v.tensor_copy(ctx[blk, blk], p_c[blk, blk])
                link(ins)
                v.wait_ge(small, 1)
                link(v.tensor_scalar(cw[:, :], p_w[:, 0:D], norm[:, 1:2], None, ALU.mult))
                v.wait_ge(small, 2)
                link(v.tensor_copy(fold[:, :, :], p_f[:, :].rearrange("p (k n) -> p k n", k=KC)))
                for t in range(NT):
                    v.wait_ge(mult, t + 1)
                    v.tensor_tensor(S.x[:, t, :], S.x[:, t, :], p_o[t % 3][0:P, 0:D], ALU.add).then_inc(added, 1)


def attend_edges(nc, io, S, top, den, ends):
    NR = 64
    LAST = T - STEP
    with ExitStack() as stack:
        c = Scope(nc, stack, "ae")
        rel = c.sb("rel", [NR, HD])
        rel4 = c.sb("rel4", [NR, NH, HD])
        minus_row = c.sb("minus_row", [NR, 1])
        types = c.sb("types", [NR, G * P], I32)
        hotT = c.sb("hotT", [NR, 2, G * P])
        idx = c.sb("idx", [P, RING, 2, G], I32)
        kv = c.sb("kv", [P, RING, G, 2 * D])
        queries = c.sb("queries", [P, RING, G, D])
        sums = c.sb("sums", [P, RING, G, D])
        gate = c.sb("gate", [P, T])
        score = c.sb("score", [P, RING, NH, G])
        arg = fade_p = c.sb("fade_p", [P, RING, 2, NH, G])
        p_k = [c.ps(f"k{i}", (128, 1536)) for i in range(2)]
        names = ("loaded", "begun", "asked", "hot_made", "related", "scored", "raised", "weighted",
                 "scores", "free", "differed", "signed", "walked")
        loaded, begun, asked, hot_made, related, scored, raised, weighted, scores, free, differed, signed, walked = [
            c.sem(x) for x in names]
        types_in = c.sem("types_in")
        got = [S.gathers[f"kv1_got{g}"] for g in range(RING)]
        got_q = [S.gathers[f"q1_got{g}"] for g in range(RING)]
        sent = [c.sem(f"sent{g}") for g in range(RING)]

        def passes(eng):
            with eng.Fori(0, LAST - STEP + 1, STEP) as t0:
                for g in range(RING):
                    yield t0 + g * G, t0 // G + g, t0 // STEP, g, False
            for g in range(RING):
                yield LAST + g * G, LAST // G + g, LAST // STEP, g, True

        def before(g):
            return 1 if g == 0 else 2

        with nc.Block() as block:

            @block.sync
            def _(sp):
                sp.dma_start(rel[:, :], io["L1_gnn_rel_w"]).then_inc(loaded, 16)
                for g in range(RING):
                    sp.sem_inc(sent[g], 16)
                view = io["sums"].rearrange("(p t) d -> p t d", p=P)

                def load_types(t, n):
                    sp.wait_ge(hot_made, n + 2)
                    sp.dma_start(types[:, :], io["type_row"][:, bass.ds(t * P, G * P)]
                                 .to_broadcast([NR, G * P])).then_inc(types_in, 16)

                for n in range(3):
                    load_types(n * G, n)
                for t, n, q, g, last in passes(sp):
                    if not (last and g + 3 >= RING):
                        load_types(t + 3 * G, n + 3)
                    sp.wait_ge(walked, (n + 1) * G + 1)
                    sp.dma_start(view[:, bass.ds(t, G), :], sums[:, g, :, :]).then_inc(sent[g], 16)
                for g in range(RING):
                    sp.wait_ge(sent[g], 16 * (ITERS + 1))

            @block.gpsimd
            def _(pool):
                with pool.Fori(0, ITERS) as i:
                    for g in range(RING):
                        pool.wait_ge(free, i * RING + g + 1)
                        pool.sem_inc(asked, 1)
                        for which, (rows, table, sem) in enumerate(((kv, "keys_values", got), (queries, "queries", got_q))):
                            for j in range(G):
                                pool.indirect_dma_start(
                                    out=rows[:, g, j, :], out_offset=None, in_=io[table],
                                    in_offset=bass.IndirectOffsetOnAxis(ap=idx[:, g, which, j:j + 1], axis=0),
                                ).then_inc(sem[g], 16)

            @block.tensor
            def _(pe):
                pe.wait_ge(begun, 1)
                for t, n, q, g, last in passes(pe):
                    pe.wait_ge(hot_made, n + 1 + 2)
                    pe.wait_ge(scored, n + 2 - before(g) + 1)
                    for j in range(G):
                        pe.matmul(p_k[g % 2][0:P, j * D:(j + 1) * D], hotT[:, g % 2, j * P:(j + 1) * P],
                                  rel4[:, :, :].rearrange("r h d -> r (h d)"), start=True, stop=False,
                                  skip_group_check=True)
                        if j == 0:
                            pe.wait_ge(got[g], q * (16 * G) + 16 * G)
                        mm = pe.matmul(p_k[g % 2][0:P, j * D:(j + 1) * D], S.ident[0:P, 0:P], kv[:, g, j, 0:D],
                                       start=False, stop=True, skip_group_check=True)
                    mm.then_inc(related, 1)

            @block.scalar
            def _(a):
                a.sem_inc(hot_made, 2)

                def one_hot(n, g, first=False):
                    a.wait_ge(types_in, n * 16 + 16)
                    if not first:
                        a.wait_ge(related, n - before(g) + 1)
                    a.activation(hotT[:, g % 2, :], types[:, :], ACT.Abs, bias=minus_row[:, :]).then_inc(differed, 1)
                    a.wait_ge(differed, n + 1)
                    a.activation(hotT[:, g % 2, :], hotT[:, g % 2, :], ACT.Relu, bias=S.ones[0:NR, 0:1],
                                 scale=-1.0).then_inc(hot_made, 1)

                a.wait_ge(signed, 1)
                one_hot(0, 0, first=True)
                one_hot(1, 1, first=True)
                for t, n, q, g, last in passes(a):
                    a.wait_ge(scored, n + 1 + 2)
                    a.activation(fade_p[:, g, :, :, :], arg[:, g, :, :, :], ACT.Exp,
                                 scale=float(HD) ** -0.5).then_inc(raised, 1)
                    a.wait_ge(raised, n + 1)
                    for j in range(G):
                        for h in range(NH):
                            part = kv[:, g, j, D + h * HD:D + (h + 1) * HD]
                            ins = a.activation(part, part, ACT.Copy, scale=fade_p[:, g, 1, h, j:j + 1])
                    ins.then_inc(weighted, 1)
                    if not (last and g + 2 >= RING):
                        one_hot(n + 2, (g + 2) % RING)

            @block.vector
            def _(v):
                link = linker(v, begun)
                v.tensor_scalar(minus_row[:, :], S.row[0:NR, :], -1.0, None, ALU.mult).then_inc(signed, 1)
                v.wait_ge(loaded, 16)
                v.tensor_scalar(gate[:, :], S.keep[:, :], 1.0, BIG, ALU.subtract, ALU.mult)
                v.memset(top[:, :, 0:1], -BIG)
                v.memset(den[:, :, 0:1], 0.0)
                v.memset(sums[:, RING - 1, G - 1, :], 0.0)
                link(v.tensor_scalar(rel4[:, :, :], rel[:, :].unsqueeze(1).to_broadcast([NR, NH, HD]), 0.2, None,
                                     ALU.mult))
                v.tensor_copy(idx[:, :, 0, :], S.src[:, 0:STEP].rearrange("p (g t) -> p g t", g=RING))
                v.tensor_copy(idx[:, :, 1, :],
                              S.dst[:, 0:STEP].rearrange("p (g t) -> p g t", g=RING)).then_inc(free, RING)
                v.sem_inc(scored, 2)
                v.sem_inc(walked, 1)

                def score_group(t, n, q, g):
                    link = linker(v, scores, n * 4)
                    v.wait_ge(related, n + 1)
                    v.wait_ge(got_q[g], q * (16 * G) + 16 * G)
                    qs = queries[:, g, :, :]
                    link(v.tensor_tensor(qs, qs, p_k[g % 2][0:P, 0:G * D].rearrange("p (t d) -> p t d", d=D), ALU.mult))
                    link(v.tensor_reduce(score[:, g, :, :].rearrange("p h t -> p t h"),
                                         qs.rearrange("p t (h d) -> p t h d", h=NH), AX.X, ALU.add))
                    for h in range(NH):
                        ins = v.tensor_tensor_scan(top[:, h, bass.ds(t + 1, G)], gate[:, bass.ds(t, G)],
                                                   score[:, g, h, :], top[:, h, bass.ds(t, 1)], ALU.add, ALU.max)
                    link(ins)
                    was, now = top[:, :, bass.ds(t, G)], top[:, :, bass.ds(t + 1, G)]
                    v.tensor_tensor(arg[:, g, 0, :, :], was,
                                    gate[:, bass.ds(t, G)].unsqueeze(1).to_broadcast([P, NH, G]),
                                    ALU.add).then_inc(scores, 1)
                    v.tensor_tensor(arg[:, g, 1, :, :], score[:, g, :, :], now, ALU.subtract)
                    v.wait_ge(scores, n * 4 + 4)
                    v.tensor_tensor(arg[:, g, 0, :, :], arg[:, g, 0, :, :], now, ALU.subtract).then_inc(scored, 1)

                def add_group(t, n, q, g, last):
                    v.wait_ge(weighted, n + 1)
                    v.wait_ge(walked, n * G + 1)
                    v.wait_ge(sent[g], q * 16 + 16)
                    f = fade_p[:, g, :, :, :]
                    was = sums[:, (g - 1) % RING, G - 1, :]
                    for j in range(G):
                        for h in range(NH):
                            hs = slice(h * HD, (h + 1) * HD)
                            ins = v.scalar_tensor_tensor(sums[:, g, j, hs], was[:, hs], f[:, 0, h, j:j + 1],
                                                         kv[:, g, j, D + h * HD:D + (h + 1) * HD], ALU.mult, ALU.add)
                        ins.then_inc(walked, 1)
                        if j < NH:
                            v.tensor_tensor_scan(den[:, j, bass.ds(t + 1, G)], f[:, 0, j, :], f[:, 1, j, :],
                                                 den[:, j, bass.ds(t, 1)], ALU.mult, ALU.add)
                        if j + 1 < G:
                            v.wait_ge(walked, n * G + j + 2)
                        was = sums[:, g, j, :]
                    if not last:
                        v.tensor_copy(idx[:, g, 0, :], S.src[:, bass.ds(t + STEP, G)])
                        v.tensor_copy(idx[:, g, 1, :], S.dst[:, bass.ds(t + STEP, G)]).then_inc(free, 1)

                score_group(0, 0, 0, 0)
                for t, n, q, g, last in passes(v):
                    if not (last and g + 1 >= RING):
                        score_group(t + G, n + 1, q + (g + 1) // RING, (g + 1) % RING)
                    add_group(t, n, q, g, last)
                v.wait_ge(walked, T + 1)
                v.tensor_copy(ends[:, 0:D], sums[:, RING - 1, G - 1, :])


def settle_edges(nc, io, S, top, den, ends, agg):
    with ExitStack() as stack:
        c = Scope(nc, stack, "m1")
        whole = c.sb("whole", [P, NH, T])
        best = c.sb("best", [P, NH, T])
        pair = c.sb("pair", [P, T, 2 * NH])
        dve, raised, out = c.sem("dve"), c.sem("raised"), c.sem("out")
        own = top[:, :, 1:T + 1]
        segment_scan(nc, "m1a", S, best[:, :, :], own, S.keep[:, :], S.joins, T, ALU.max)
        segment_scan(nc, "m1b", S, whole[:, :, :], best[:, :, :], S.keep[:, :], S.joins, T, ALU.max, reverse=True)
        fetched = S.gathers["g1_fetched"]
        with nc.Block() as block:

            @block.gpsimd
            def _(pool):
                for t in range(NT):
                    pool.indirect_dma_start(
                        out=agg[:, t, :], out_offset=None, in_=io["sums"],
                        in_offset=bass.IndirectOffsetOnAxis(ap=S.last[:, t:t + 1], axis=0),
                        bounds_check=E - 1, oob_is_err=False).then_inc(fetched, 16)

            @block.scalar
            def _(a):
                a.wait_ge(dve, 1)
                a.activation(best[:, :, :], whole[:, :, :], ACT.Exp, scale=float(HD) ** -0.5).then_inc(raised, 1)

            @block.vector
            def _(v):
                link = linker(v, dve)
                link(v.tensor_tensor(whole[:, :, :], own, whole[:, :, :], ALU.subtract))
                v.wait_ge(raised, 1)
                v.tensor_copy(pair[:, :, 0:NH].rearrange("p t h -> p h t"), best[:, :, :])
                link(v.tensor_tensor(pair[:, :, NH:2 * NH].rearrange("p t h -> p h t"), den[:, :, 1:T + 1],
                                     best[:, :, :], ALU.mult))
                v.tensor_copy(ends[:, D:D + NH], pair[:, T - 1, NH:2 * NH])
                for h in range(NH):
                    hs = slice(h * HD, (h + 1) * HD)
                    v.tensor_scalar(ends[:, hs], ends[:, hs], best[:, h, T - 1:T], None, ALU.mult)

            @block.sync
            def _(sp):
                sp.wait_ge(dve, 2)
                sp.dma_start(io["dens"].rearrange("(p t) h -> p t h", p=P), pair[:, :, :]).then_inc(out, 16)
                sp.wait_ge(out, 16)


def collect1(nc, io, S, agg, den, ends):
    with ExitStack() as stack:
        c = Scope(nc, stack, "c1")
        carry = c.sb("carry", [P, N])
        p_c = [c.ps(f"carry{i}") for i in range(4)]
        ready, carried, added, made, scaled = [c.sem(x) for x in ("ready", "carried", "added", "made", "scaled")]
        fetched, dens_in = S.gathers["g1_fetched"], S.gathers["g1_dens_in"]
        with nc.Block() as block:

            @block.gpsimd
            def _(pool):
                pool.iota(carry[:, :], [[1, N]], base=0, channel_multiplier=0,
                          allow_small_or_imprecise_dtypes=True).then_inc(made, 1)
                pool.wait_ge(made, 2)
                for t in range(NT):
                    pool.indirect_dma_start(
                        out=den[:, t, :], out_offset=None, in_=io["dens"],
                        in_offset=bass.IndirectOffsetOnAxis(ap=S.last[:, t:t + 1], axis=0),
                        bounds_check=E - 1, oob_is_err=False).then_inc(dens_in, 16)

            @block.vector
            def _(v):
                v.wait_ge(made, 1)
                v.memset(den[:, :, :], 1.0).then_inc(made, 1)
                v.tensor_scalar(carry[:, :], carry[:, :], S.goes_on[:, 0:1], None, ALU.is_equal).then_inc(ready, 1)
                v.wait_ge(fetched, 16 * NT)
                v.wait_ge(dens_in, 16 * NT)
                for h in range(NH):
                    v.tensor_tensor(agg[:, :, h * HD:(h + 1) * HD], agg[:, :, h * HD:(h + 1) * HD],
                                    den[:, :, h:h + 1].to_broadcast([P, NT, HD]), ALU.mult).then_inc(scaled, 1)
                v.wait_ge(scaled, NH)
                for t in range(NT):
                    v.wait_ge(carried, t + 1)
                    v.tensor_tensor(den[:, t, NH:2 * NH], den[:, t, NH:2 * NH], p_c[t % 4][0:P, D:D + NH], ALU.add)
                    v.tensor_tensor(agg[:, t, :], agg[:, t, :], p_c[t % 4][0:P, 0:D], ALU.add).then_inc(added, 1)

            @block.tensor
            def _(pe):
                pe.wait_ge(ready, 1)
                for t in range(NT):
                    if t >= 4:
                        pe.wait_ge(added, t - 3)
                    pe.matmul(p_c[t % 4][0:P, 0:D + NH], carry[:, t * P:(t + 1) * P], ends[:, :],
                              start=True, stop=True).then_inc(carried, 1)


def finish1(nc, io, S, agg, den, xn):
    with ExitStack() as stack:
        c = Scope(nc, stack, "o1")
        w = c.sb("w", [128, KC, D])
        bo = c.sb("bo", [1, D])
        gamma = c.sb("gamma", [P, D])
        beta = c.sb("beta", [P, D])
        aT = c.sb("aT", [128, 2, KC, P])
        stats = c.sb("stats", [P, NT, 6])
        mean, diff, var, std = [c.sb(x, [P, NT]) for x in ("mean", "diff", "var", "std")]
        p_t = [c.ps(f"t{i}") for i in range(2)]
        p_o = [c.ps(f"o{i}") for i in range(3)]
        names = ("loaded", "dve", "turned", "copied", "mult", "added", "rooted", "ready", "counted")
        loaded, dve, turned, copied, mult, added, rooted, ready, counted = [c.sem(x) for x in names]
        with nc.Block() as block:

            @block.sync
            def _(sp):
                sp.dma_start(w[:, :, :], io["L1_gnn_Wo"].rearrange("(k p) n -> p k n", p=128)).then_inc(loaded, 16)
                sp.dma_start(bo[:, :], io["L1_gnn_bo"].rearrange("(a n) -> a n", a=1)).then_inc(loaded, 16)
                for name, tile in (("L1_gnn_gamma", gamma), ("L1_gnn_beta", beta)):
                    sp.dma_start(tile[:, :], io[name].rearrange("(a n) -> a n", a=1)
                                 .to_broadcast([P, D])).then_inc(loaded, 16)

            @block.tensor
            def _(pe):
                pe.wait_ge(loaded, 4 * 16)
                pe.wait_ge(ready, 1)
                for t in range(NT + 1):
                    if t < NT:
                        if t >= 2:
                            pe.wait_ge(copied, t - 1)
                        for k in range(KC):
                            mm = pe.transpose(p_t[t % 2][:, k * P:(k + 1) * P], agg[:, t, k * 128:(k + 1) * 128],
                                              S.ident[0:P, 0:P])
                        mm.then_inc(turned, 1)
                    if t >= 1:
                        s = t - 1
                        pe.wait_ge(copied, s + 1)
                        if s >= 3:
                            pe.wait_ge(added, s - 2)
                        o = p_o[s % 3][0:P, 0:D]
                        for k in range(KC):
                            pe.matmul(o, aT[:, s % 2, k, :], w[:, k, :], start=(k == 0), stop=False)
                        pe.matmul(o, S.ones[0:1, 0:P], bo[0:1, :], start=False, stop=True).then_inc(mult, 1)

            @block.scalar
            def _(a):
                for t in range(NT):
                    a.wait_ge(turned, t + 1)
                    if t >= 2:
                        a.wait_ge(mult, t - 1)
                    a.activation(aT[:, t % 2, :, :], p_t[t % 2][:, 0:KC * P].rearrange("q (k p) -> q k p", k=KC),
                                 ACT.Copy).then_inc(copied, 1)
                a.wait_ge(counted, MV_STEPS)
                a.activation(std[:, :], var[:, :], ACT.Sqrt).then_inc(rooted, 1)

            @block.vector
            def _(v):
                link = linker(v, dve)
                link(v.reciprocal(den, den))
                for h in range(NH):
                    ins = v.tensor_tensor(agg[:, :, h * HD:(h + 1) * HD], agg[:, :, h * HD:(h + 1) * HD],
                                          den[:, :, h:h + 1].to_broadcast([P, NT, HD]), ALU.mult)
                link(ins)
                v.sem_inc(ready, 1)
                for t in range(NT):
                    v.wait_ge(mult, t + 1)
                    v.tensor_tensor(xn[:, t, :], xn[:, t, :], p_o[t % 3][0:P, 0:D], ALU.add).then_inc(added, 1)
                    v.wait_ge(added, t + 1)
                    link(v.bn_stats(stats[:, t, :], xn[:, t, :]))
                mean_and_var(linker(v, counted), stats, v, mean[:, :], var[:, :], diff[:, :])
                v.wait_ge(rooted, 1)
                link(v.reciprocal(std[:, :], std[:, :]))
                for t in range(NT):
                    link(v.tensor_scalar(xn[:, t, :], xn[:, t, :], mean[:, t:t + 1], std[:, t:t + 1],
                                         ALU.subtract, ALU.mult))
                v.wait_ge(loaded, 4 * 16)
                link(v.tensor_tensor(xn[:, :, :], xn[:, :, :], gamma[:, :].unsqueeze(1).to_broadcast([P, NT, D]), ALU.mult))
                link(v.tensor_tensor(xn[:, :, :], xn[:, :, :], beta[:, :].unsqueeze(1).to_broadcast([P, NT, D]), ALU.add))
                v.tensor_tensor(S.x[:, :, :], S.x[:, :, :], xn[:, :, :], ALU.add)


def layer1_experts(nc, io, S, out):
    with ExitStack() as stack:
        c = Scope(nc, stack, "f1")
        gates = c.sb("gates", [P, NT, NX1])
        S.xnT = c.sb("xnT", [128, KC, N])
        outs = c.sb("outs", [P, EARLY, NT, D])
        normalize(nc, "n3", S, None, S.xnT)
        values = c.sb("values", [P, (NH * NX1 + 2 * NH) * GC])
        late = values[:, 0:NT * D].rearrange("p (t d) -> p t d", d=D)
        attend1(nc, io, S, gates, outs, values, late)
        combine1(nc, S, gates, outs, late, out)


def attend1(nc, io, S, gates, outs, values, late):
    CH = NH * NX1
    C20 = CH + NH
    C24 = CH + 2 * NH
    RG = 16
    with ExitStack() as stack:
        c = Scope(nc, stack, "a1")
        joins = c.sb("joins", [P, 4])
        keep = c.sb("keep", [P, GC])
        starts = c.sb("starts", [P, GC])
        edges = c.sb("edges", [P, GC, 2], I32)
        vals = values[:, :].rearrange("p (c t) -> p c t", c=C24)
        work = c.sb("work", [P, NH, GC])
        last = c.sb("last", [P, NT], I32)
        with ExitStack() as s2:
            c2 = Scope(nc, s2, "a2")
            w = c2.sb("w", [128, KC, CH])
            att = c2.sb("att", [P, 2, CH])
            h = c2.sb("h", [P, NT, C24])
            prod = c2.sb("prod", [P, NT, CH])
            first = c2.sb("first", [P, 4], I32)
            firstf = c2.sb("firstf", [P, 4])
            dstf = c2.sb("dstf", [P, GC])
            ring_i = c2.sb("ring_i", [P, 2, RG], I32)
            ring = c2.sb("ring", [P, 2, RG, C24])
            p_h = c2.ps("h")
            experts = Experts1(c2, io, S, 0, EARLY)
            names = ("loaded", "cleared", "mult", "dve", "tabled", "sent", "staged", "asked", "free")
            loaded, cleared, mult, dve, tabled, sent, staged, asked, free = [c2.sem(x) for x in names]
            got = [S.gathers[f"a1_got{i}"] for i in range(2)]
            with nc.Block() as block:

                @block.sync
                def _(sp):
                    sp.dma_start(w[:, :, :], io["L1_ffn_W_gat"].rearrange("(k p) n -> p k n", p=128)).then_inc(loaded, 16)
                    for i, n in enumerate(("src", "dst")):
                        sp.dma_start(att[:, i, :], io[f"L1_ffn_att_{n}"].rearrange("(a h) e -> a (h e)", a=1)
                                     .to_broadcast([P, CH])).then_inc(loaded, 16)
                    sp.dma_start(edges[:, :, :], io["sorted"].rearrange("(p t) c -> p t c", p=P)).then_inc(loaded, 16)
                    sp.dma_start(last[:, :], io["last2"][0:N].rearrange("(t p) -> p t", p=P)).then_inc(loaded, 16)
                    d2 = io["sorted"].rearrange("(p t) c -> p t c", p=P)
                    sp.wait_ge(cleared, 1)
                    sp.dma_start(first[0:P - 1, 0:1], d2[1:P, 0, 1:2]).then_inc(loaded, 16)
                    sp.dma_start(first[1:P, 1:2], d2[0:P - 1, GC - 1, 1:2]).then_inc(loaded, 16)
                    experts.load(sp)
                    sp.wait_ge(tabled, 1)
                    sp.dma_start(io["gat"].rearrange("(t p) c -> p t c", p=P), h[:, :, :]).then_inc(sent, 16)

                @block.tensor
                def _(pe):
                    pe.wait_ge(loaded, 7 * 16)
                    for t in range(NT):
                        for k in range(KC):
                            mm = pe.matmul(p_h[0:P, t * CH:(t + 1) * CH], S.xnT[:, k, t * P:(t + 1) * P], w[:, k, :],
                                           start=(k == 0), stop=(k == KC - 1))
                    mm.then_inc(mult, 1)
                    experts.multiply(pe)

                @block.scalar
                def _(a):
                    experts.begin(a)
                    experts.activate(a, 0, NT, lambda e, t0: outs[:, e, bass.ds(t0, U), :])

                @block.gpsimd
                def _(pool):
                    pool.wait_ge(sent, 16)
                    with pool.Fori(0, GC - 2 * RG + 1, 2 * RG) as t0:
                        for i in range(2):
                            pool.wait_ge(free, t0 // RG + i + 1)
                            pool.tensor_copy(ring_i[:, i, :], edges[:, bass.ds(t0 + i * RG, RG), 0]).then_inc(staged, 1)
                            pool.wait_ge(staged, t0 // RG + i + 1)
                            pool.sem_inc(asked, 1)
                            for j in range(RG):
                                pool.indirect_dma_start(
                                    out=ring[:, i, j, :], out_offset=None, in_=io["gat"],
                                    in_offset=bass.IndirectOffsetOnAxis(ap=ring_i[:, i, j:j + 1], axis=0),
                                ).then_inc(got[i], 16)

                @block.vector
                def _(v):
                    link = linker(v, dve)
                    link(v.memset(first[:, :], -1))
                    v.sem_inc(cleared, 1)
                    experts.split_bias(v)
                    v.sem_inc(free, 2)
                    v.wait_ge(mult, 1)
                    link(v.tensor_copy(h[:, :, 0:CH], p_h[0:P, 0:NT * CH].rearrange("p (t c) -> p t c", c=CH)))
                    for i in range(2):
                        link(v.tensor_tensor(prod[:, :, :], h[:, :, 0:CH],
                                             att[:, i, :].unsqueeze(1).to_broadcast([P, NT, CH]), ALU.mult))
                        link(v.tensor_reduce(h[:, :, CH + i * NH:CH + (i + 1) * NH],
                                             prod[:, :, :].rearrange("p t (h e) -> p t h e", e=NX1), AX.X, ALU.add))
                    v.sem_inc(tabled, 1)
                    link(v.tensor_copy(dstf[:, :], edges[:, :, 1]))
                    link(v.tensor_copy(firstf[:, :], first[:, :]))
                    link(v.memset(keep[:, :], 1.0))
                    link(v.tensor_tensor(keep[:, 1:GC], dstf[:, 1:GC], dstf[:, 0:GC - 1], ALU.is_equal))
                    link(v.tensor_tensor(joins[:, 0:1], firstf[:, 1:2], dstf[:, 0:1], ALU.is_equal))
                    link(v.tensor_tensor(joins[:, 1:2], firstf[:, 0:1], dstf[:, GC - 1:GC], ALU.is_equal))
                    link(v.tensor_tensor(joins[:, 2:3], dstf[:, 0:1], dstf[:, GC - 1:GC], ALU.is_equal))
                    link(v.tensor_scalar(starts[:, :], keep[:, :], -1.0, 1.0, ALU.mult, ALU.add))
                    link(v.tensor_scalar(starts[:, 0:1], joins[:, 0:1], -1.0, 1.0, ALU.mult, ALU.add))
                    with v.Fori(0, GC - 2 * RG + 1, 2 * RG) as t0:
                        link = linker(v, dve, (t0 // RG) + 15)
                        for i in range(2):
                            v.wait_ge(got[i], (t0 // (2 * RG)) * (16 * RG) + 16 * RG)
                            link(v.tensor_copy(vals[:, :, bass.ds(t0 + i * RG, RG)].rearrange("p c t -> p t c"),
                                               ring[:, i, :, :]))
                            v.sem_inc(free, 1)
                    link = linker(v, dve, GC // RG + 15)
                    link(v.tensor_tensor(vals[:, CH + NH:C24, :], vals[:, CH + NH:C24, :],
                                         starts[:, :].unsqueeze(1).to_broadcast([P, NH, GC]), ALU.mult))
        pay = c.sb("pay", [P, C20, GC])
        node = c.sb("node", [P, NT, C20])
        logits = vals[:, CH:CH + NH, :]
        with ExitStack() as s3:
            best = Scope(nc, s3, "ab").sb("best", [P, NH, GC])
            segment_scan(nc, "sa", S, work[:, :, :], vals[:, CH + NH:C24, :], keep[:, :], joins, GC, ALU.add)
            with ExitStack() as s2:
                c2 = Scope(nc, s2, "a3")
                dve = c2.sem("dve")
                with nc.Block() as block:
                    @block.vector
                    def _(v):
                        link = linker(v, dve)
                        link(v.tensor_tensor(logits, logits, work[:, :, :], ALU.add))
                        link(v.scalar_tensor_tensor(work[:, :, :], logits, 0.2, logits, ALU.mult, ALU.max))
            segment_scan(nc, "sb", S, best[:, :, :], work[:, :, :], keep[:, :], joins, GC, ALU.max)
            segment_scan(nc, "sc", S, logits, best[:, :, :], keep[:, :], joins, GC, ALU.max, reverse=True)
            with ExitStack() as s2:
                c2 = Scope(nc, s2, "a4")
                dve, raised = c2.sem("dve"), c2.sem("raised")
                with nc.Block() as block:
                    @block.scalar
                    def _(a):
                        a.wait_ge(dve, 1)
                        a.activation(pay[:, CH:C20, :], work[:, :, :], ACT.Exp).then_inc(raised, 1)

                    @block.vector
                    def _(v):
                        v.tensor_tensor(work[:, :, :], work[:, :, :], logits, ALU.subtract).then_inc(dve, 1)
                        v.wait_ge(raised, 1)
                        for hd in range(NH):
                            v.tensor_tensor(pay[:, hd * NX1:(hd + 1) * NX1, :], vals[:, hd * NX1:(hd + 1) * NX1, :],
                                            pay[:, CH + hd:CH + hd + 1, :].to_broadcast([P, NX1, GC]), ALU.mult)
        total = vals[:, 0:C20, :]
        segment_scan(nc, "sd", S, total, pay[:, :, :], keep[:, :], joins, GC, ALU.add)
        with ExitStack() as s2:
            c2 = Scope(nc, s2, "a5")
            flat = pay[:, :, :].rearrange("p c t -> p (c t)").rearrange("p (t c) -> p t c", c=C20)
            small = c2.sb("small", [P, 3, CH])
            z = c2.sb("z", [P, NT, CH])
            sq = c2.sb("sq", [P, NT, CH])
            mean, var, std, top, low = [c2.sb(x, [P, NT]) for x in ("mean", "var", "std", "top", "low")]
            score, hot1, hot2 = [c2.sb(x, [P, NT, NX1]) for x in ("score", "hot1", "hot2")]
            rec = c2.sb("rec", [P, NT, NH])
            order = c2.sb("order", [P, NX1])
            experts = Experts1(c2, io, S, EARLY, NX1)
            names = ("loaded", "dve", "sent", "made", "rooted", "raised")
            fetched = S.gathers["a1_fetched"]
            loaded, dve, sent, made, rooted, raised = [c2.sem(x) for x in names]
            with nc.Block() as block:

                @block.sync
                def _(sp):
                    for i, n in enumerate(("b_gat", "ln_gamma", "ln_beta")):
                        sp.dma_start(small[:, i, :], io[f"L1_ffn_{n}"].rearrange("(a n) -> a n", a=1)
                                     .to_broadcast([P, CH])).then_inc(loaded, 16)
                    experts.load(sp)
                    sp.wait_ge(dve, 1)
                    sp.dma_start(io["gsum"].rearrange("(p t) c -> p t c", p=P), flat).then_inc(sent, 16)
                    sp.wait_ge(sent, 16)

                @block.gpsimd
                def _(pool):
                    pool.iota(order[:, :], [[-1, NX1]], base=NX1, channel_multiplier=0,
                              allow_small_or_imprecise_dtypes=True).then_inc(made, 1)
                    pool.wait_ge(sent, 16)
                    for t in range(NT):
                        pool.indirect_dma_start(
                            out=node[:, t, :], out_offset=None, in_=io["gsum"],
                            in_offset=bass.IndirectOffsetOnAxis(ap=last[:, t:t + 1], axis=0)).then_inc(fetched, 16)

                @block.tensor
                def _(pe):
                    experts.multiply(pe)

                @block.scalar
                def _(a):
                    def place(e, t0):
                        return late[:, bass.ds(t0, U), :]

                    experts.begin(a)
                    a.wait_ge(dve, 1)
                    experts.activate(a, 0, 3 * U, place)
                    a.wait_ge(dve, 12)
                    a.activation(std[:, :], var[:, :], ACT.Sqrt).then_inc(rooted, 1)
                    experts.activate(a, 3 * U, NT, place)
                    a.wait_ge(dve, 30)
                    a.activation(top[:, :], low[:, :], ACT.Exp).then_inc(raised, 1)

                @block.vector
                def _(v):
                    link = linker(v, dve)
                    link(v.tensor_copy(flat.rearrange("p t c -> p c t"), total))
                    experts.split_bias(v)
                    v.wait_ge(fetched, 16 * NT)
                    v.wait_ge(loaded, 48)
                    v.wait_ge(made, 1)

                    def wide(x, n=CH):
                        return x.unsqueeze(2).to_broadcast([P, NT, n])

                    def rows(i):
                        return small[:, i, :].unsqueeze(1).to_broadcast([P, NT, CH])

                    link(v.tensor_scalar(rec[:, :, :], node[:, :, CH:C20], 1e-16, None, ALU.add))
                    link(v.reciprocal(rec[:, :, :], rec[:, :, :]))
                    for hd in range(NH):
                        ins = v.tensor_tensor(z[:, :, hd * NX1:(hd + 1) * NX1], node[:, :, hd * NX1:(hd + 1) * NX1],
                                              wide(rec[:, :, hd], NX1), ALU.mult)
                    link(ins)
                    link(v.tensor_tensor(z[:, :, :], z[:, :, :], rows(0), ALU.add))
                    link(v.tensor_reduce(mean[:, :], z[:, :, :], AX.X, ALU.add))
                    link(v.tensor_scalar(mean[:, :], mean[:, :], 1.0 / CH, None, ALU.mult))
                    link(v.tensor_tensor(z[:, :, :], z[:, :, :], wide(mean[:, :]), ALU.subtract))
                    link(v.tensor_tensor(sq[:, :, :], z[:, :, :], z[:, :, :], ALU.mult))
                    link(v.tensor_reduce(var[:, :], sq[:, :, :], AX.X, ALU.add))
                    link(v.tensor_scalar(var[:, :], var[:, :], 1.0 / CH, None, ALU.mult))
                    link(v.tensor_scalar(var[:, :], var[:, :], EPS, None, ALU.add))
                    v.wait_ge(rooted, 1)
                    link(v.reciprocal(std[:, :], std[:, :]))
                    link(v.tensor_tensor(z[:, :, :], z[:, :, :], wide(std[:, :]), ALU.mult))
                    link(v.tensor_tensor(z[:, :, :], z[:, :, :], rows(1), ALU.mult))
                    link(v.tensor_tensor(z[:, :, :], z[:, :, :], rows(2), ALU.add))
                    link(v.tensor_reduce(score[:, :, :], z[:, :, :].rearrange("p t (h e) -> p t e h", e=NX1),
                                         AX.X, ALU.add))
                    link(v.tensor_scalar(score[:, :, :], score[:, :, :], 1.0 / NH, None, ALU.mult))
                    ranked = order[:, :].unsqueeze(1).to_broadcast([P, NT, NX1])

                    def first_best(hot, best):
                        link(v.tensor_reduce(best, score[:, :, :], AX.X, ALU.max))
                        link(v.tensor_tensor(hot, score[:, :, :], wide(best, NX1), ALU.is_equal))
                        link(v.tensor_tensor(hot, hot, ranked, ALU.mult))
                        link(v.tensor_reduce(mean[:, :], hot, AX.X, ALU.max))
                        link(v.tensor_tensor(hot, ranked, wide(mean[:, :], NX1), ALU.is_equal))

                    first_best(hot1[:, :, :], top[:, :])
                    link(v.scalar_tensor_tensor(score[:, :, :], hot1[:, :, :], -BIG, score[:, :, :],
                                                ALU.mult, ALU.add))
                    first_best(hot2[:, :, :], low[:, :])
                    link(v.tensor_tensor(low[:, :], low[:, :], top[:, :], ALU.subtract))
                    v.wait_ge(raised, 1)
                    link(v.tensor_scalar(var[:, :], top[:, :], 1.0, None, ALU.add))
                    link(v.reciprocal(var[:, :], var[:, :]))
                    link(v.tensor_tensor(top[:, :], top[:, :], var[:, :], ALU.mult))
                    link(v.tensor_tensor(hot1[:, :, :], hot1[:, :, :], wide(var[:, :], NX1), ALU.mult))
                    link(v.tensor_tensor(hot2[:, :, :], hot2[:, :, :], wide(top[:, :], NX1), ALU.mult))
                    v.tensor_tensor(gates[:, :, :], hot1[:, :, :], hot2[:, :, :], ALU.add)


class Experts1:

    def __init__(self, c, io, S, lo, hi):
        self.S, self.io, self.lo, self.hi = S, io, lo, hi
        self.experts = hi - lo
        self.chunks = self.experts * NCH1
        self.w1 = c.sb("w1", [128, KC, self.experts * HX1])
        self.w2 = c.sb("w2", [128, self.chunks, D])
        self.b1 = c.sb("b1", [128, self.chunks])
        self.b2 = c.sb("b2", [3, self.experts * D])
        self.parts = c.sb("b2_parts", [3, self.experts * D], BF16)
        self.hid = c.sb("hid", [128, 2, U * P])
        self.p_hidden = [c.ps(f"hidden{i}", (128, 1024)) for i in range(2)]
        self.p_out = c.ps("out", (128, 1536))
        self.bias_in, self.biased = c.sem("x_bias_in"), c.sem("x_biased")
        names = ("x_loaded", "x_hidden", "x_active", "x_done", "x_emptied")
        self.loaded, self.hidden, self.active, self.done, self.emptied = [c.sem(x) for x in names]

    CUT = ((0, 3 * P, 0), (3 * P, U * P, 512))

    def load(self, sp):
        io, lo, hi = self.io, self.lo, self.hi
        sp.dma_start(self.w1[:, :, :], io["L1_ffn_W1"][:, lo * HX1:hi * HX1]
                     .rearrange("(k p) n -> p k n", p=128)).then_inc(self.loaded, 16)
        sp.dma_start(self.w2[:, :, :], io["L1_ffn_W2"][lo * HX1:hi * HX1, :]
                     .rearrange("(c p) n -> p c n", p=128)).then_inc(self.loaded, 16)
        sp.dma_start(self.b1[:, :], io["L1_ffn_b1"][:, lo * NCH1:hi * NCH1]).then_inc(self.loaded, 16)
        sp.dma_start(self.b2[:, :], io["L1_ffn_b2"][lo:hi, :].rearrange("(a e) n -> a (e n)", a=1)
                     .to_broadcast([3, self.experts * D])).then_inc(self.bias_in, 16)

    def split_bias(self, v):
        v.wait_ge(self.bias_in, 16)
        exact_parts(linker(v, self.biased), v, self.S, self.b2[:, :], self.parts[:, :])

    def multiply(self, pe):
        S, w1, w2, hid, p_hidden, p_out = self.S, self.w1, self.w2, self.hid, self.p_hidden, self.p_out
        ALLC = self.chunks
        pe.wait_ge(self.loaded, 3 * 16)
        pe.wait_ge(self.biased, 5)
        with pe.Fori(0, NT - U + 1, U) as t0:

            def make_hidden(ch):
                pe.wait_ge(self.active, (t0 // U) * ALLC + ch + 1)
                for lo, hi, at in self.CUT:
                    for k in range(KC):
                        mm = pe.matmul(p_hidden[ch % 2][:, at:at + hi - lo], w1[:, k, ch * 128:(ch + 1) * 128],
                                       S.xnT[:, k, bass.ds(t0 * P + lo, hi - lo)],
                                       start=(k == 0), stop=(k == KC - 1))
                mm.then_inc(self.hidden, 1)

            def add_output(ch):
                e = ch // NCH1
                if ch % NCH1 == 0:
                    pe.wait_ge(self.emptied, (t0 // U) * self.experts + e + 1)
                    for u in range(U):
                        pe.matmul(p_out[0:P, u * D:(u + 1) * D], S.ones3[:, 0:P], self.parts[:, e * D:(e + 1) * D],
                                  start=(u % 2 == 0), stop=False, skip_group_check=True)
                pe.wait_ge(self.active, (t0 // U) * ALLC + ch + 3)
                for u in range(U):
                    mm = pe.matmul(p_out[0:P, u * D:(u + 1) * D], hid[:, ch % 2, u * P:(u + 1) * P],
                                   w2[:, ch, :], start=False, stop=(ch % NCH1 == NCH1 - 1), skip_group_check=True)
                mm.then_inc(self.done, 1)

            make_hidden(0)
            for ch in range(ALLC):
                if ch + 1 < ALLC:
                    make_hidden(ch + 1)
                add_output(ch)

    def begin(self, a):
        a.wait_ge(self.loaded, 3 * 16)
        a.sem_inc(self.active, 2)
        a.sem_inc(self.done, 2)
        a.sem_inc(self.emptied, 1)

    def activate(self, a, begin, end, place):
        ALLC = self.chunks
        with a.Fori(begin, end - U + 1, U) as t0:

            def empty(e):
                a.wait_ge(self.done, (t0 // U) * ALLC + (e + 1) * NCH1 + 2)
                a.activation(place(e, t0).rearrange("p u d -> p (u d)"), self.p_out[0:P, 0:U * D],
                             ACT.Copy).then_inc(self.emptied, 1)

            for ch in range(ALLC):
                a.wait_ge(self.hidden, (t0 // U) * ALLC + ch + 1)
                a.wait_ge(self.done, (t0 // U) * ALLC + ch + 1)
                for lo, hi, at in self.CUT:
                    ins = a.activation(self.hid[:, ch % 2, lo:hi], self.p_hidden[ch % 2][:, at:at + hi - lo],
                                       ACT.Gelu, bias=self.b1[:, ch:ch + 1])
                ins.then_inc(self.active, 1)
                if ch % NCH1 == 0 and ch > 0:
                    empty(ch // NCH1 - 1)
            empty(self.experts - 1)


def combine1(nc, S, gates, outs, late, out):
    with ExitStack() as stack:
        c = Scope(nc, stack, "h1")
        dve, stored = c.sem("dve"), c.sem("stored")
        with nc.Block() as block:

            @block.vector
            def _(v):
                with v.Fori(0, NT - U + 1, U) as t0:
                    link = linker(v, dve, (t0 // U) * NX1)
                    for e in range(NX1):
                        for u in range(U):
                            made = (late[:, bass.ds(t0 + u, 1), :] if e == EARLY else
                                    outs[:, e, bass.ds(t0 + u, 1), :]).rearrange("p a b -> p (a b)")
                            xt = S.x[:, bass.ds(t0 + u, 1), :].rearrange("p a b -> p (a b)")
                            ins = v.scalar_tensor_tensor(xt, made, gates[:, bass.ds(t0 + u, 1), e], xt,
                                                         ALU.mult, ALU.add)
                        link(ins)

            @block.sync
            def _(sp):
                rows = out.rearrange("(t p) d -> p t d", p=P)
                for i in range(NT // U):
                    sp.wait_ge(dve, (i + 1) * NX1)
                    sp.dma_start(rows[:, i * U:(i + 1) * U, :], S.x[:, i * U:(i + 1) * U, :]).then_inc(stored, 16)
                sp.wait_ge(stored, 16 * (NT // U))


class State:
    pass


_TRANSPOSED = {"L0_gnn_W", "L0_ffn_router_w"}


def build(nc, io, out):
    with ExitStack() as stack:
        stack.enter_context(nc.allow_non_contiguous_dma(reason="single columns, small vectors"))
        c = Scope(nc, stack, "all")
        S = State()
        S.gathers = {name: c.sem(name) for name in GATHER_SEMAPHORES}
        S.first_semaphore = min(nc.free_semaphores)
        S.x = c.sb("x", [P, NT, D])
        S.ident = c.sb("ident", [128, 128])
        S.ones = c.sb("ones", [128, 128])
        S.row = c.sb("row", [128, 1])
        S.minus = c.sb("minus", [3, 2])
        S.ones3 = c.sb("ones3", [3, 128], BF16)
        with ExitStack() as sg:
            cg = Scope(nc, sg, "graph")
            S.dst = cg.sb("dst", [P, T], I32)
            S.src = cg.sb("src", [P, T + STEP], I32)
            S.keep = cg.sb("keep", [P, T])
            S.joins = cg.sb("joins", [P, 4])
            S.goes_on = cg.sb("goes_on", [P, 1])
            S.last = cg.sb("last", [P, NT], I32)
            with ExitStack() as s0:
                c0 = Scope(nc, s0, "sort")
                S.xnT = c0.sb("xnT", [128, KC, N])
                S.w = c0.sb("w", [P, T])
                S.dstf = c0.sb("dstf", [P, T])
                S.iota_lo = c0.sb("iota_lo", [128, LO])
                S.tri = c0.sb("tri", [128, 128])
                S.below = c0.sb("below", [128, 128])
                S.dst_lo, S.dst_hi = c0.sb("dst_lo", [P, T], I32), c0.sb("dst_hi", [P, T], I32)
                S.rsrc, S.rdst, S.rdst_lo, S.rdst_hi = [
                    c0.sb(x, [128, GT], I32) for x in ("rsrc", "rdst", "rdst_lo", "rdst_hi")]
                S.rdstf = c0.sb("rdstf", [128, GT])
                S.count = c0.sb("counts", [128, GT + 1, HI])
                S.hot_hi = c0.sb("hot_hi", [128, GT, HI], BF16)
                S.loop_i, S.rlast_i = c0.sb("loop_i", [128, HI], I32), c0.sb("rlast_i", [128, HI], I32)
                load(nc, io, S)
                normalize(nc, "n0", S, None, S.xnT)
                layer0_graph(nc, io, S)
                normalize(nc, "n1", S, None, S.xnT)
                layer0_experts(nc, io, S)
            clear_semaphores(nc, S)
            layer1_graph(nc, io, S)
        clear_semaphores(nc, S)
        layer1_experts(nc, io, S, out)


_SCRATCH = {
    "last": ((LO * HI,), I32),
    "table": ((N, D), F32),
    "sums": ((E, D), F32),
    "queries": ((N, D), F32),
    "keys_values": ((N, 2 * D), F32),
    "dens": ((E, 2 * NH), F32),
    "sorted": ((GP, 2), I32),
    "last2": ((LO * HI,), I32),
    "gat": ((N, 24), F32),
    "gsum": ((GP, 20), F32),
}


def kernel(**inputs):
    import numpy as _np
    import concourse.bacc as _bacc
    from concourse.bass_utils import run_bass_kernel_spmd as _run

    nc = _bacc.Bacc("TRN2", target_bir_lowering=False, num_devices=1)
    arrays, io = {}, {}
    inputs["L0_mix_W_v_T"] = _np.asarray(inputs["L0_mix_W_qkv"])[:, 2 * D:].T
    inputs["L1_mix_W_q_T"] = _np.asarray(inputs["L1_mix_W_qkv"])[:, 0:128].T
    inputs["type_row"] = _np.asarray(inputs["edge_type_64"]).reshape(P, T).T.reshape(1, E)
    edges = _np.asarray(inputs["L1_ffn_edge_index"])
    edges = _np.concatenate([edges, _np.full((2, GT * 128 - GE), PAD, edges.dtype)], axis=1)
    inputs["edge_columns"] = edges.reshape(2, GT, 128).transpose(0, 2, 1)
    inputs["edge_row"] = edges[1:2]
    inputs["L1_ffn_W1"] = _np.asarray(inputs["L1_ffn_W1"]).transpose(1, 0, 2).reshape(D, NX1 * HX1)
    inputs["L1_ffn_b1"] = _np.asarray(inputs["L1_ffn_b1"]).reshape(NX1 * HX1 // 128, 128).T
    inputs["L1_ffn_W2"] = _np.asarray(inputs["L1_ffn_W2"]).reshape(NX1 * HX1, D)
    w1 = _np.asarray(inputs["L0_ffn_W1"])
    inputs["L0_ffn_W1"] = w1.transpose(1, 0, 2).reshape(D, NX * HX)
    inputs["L0_ffn_b1"] = _np.asarray(inputs["L0_ffn_b1"]).reshape(NC0, 128).T
    inputs["L0_ffn_W2"] = _np.asarray(inputs["L0_ffn_W2"]).reshape(NX * HX, D)
    for name, a in inputs.items():
        a = _np.asarray(a)
        if name in _TRANSPOSED:
            a = a.T
        a = _np.ascontiguousarray(a)
        arrays[f"in_{name}"] = a
        io[name] = nc.dram_tensor(f"in_{name}", a.shape, mybir.dt.from_np(a.dtype), kind="ExternalInput").ap()
    for name, (shape, dt) in _SCRATCH.items():
        io[name] = nc.dram_tensor(f"s_{name}", list(shape), dt, kind="Internal").ap()
    out = nc.dram_tensor("out", (N, D), F32, kind="ExternalOutput").ap()
    build(nc, io, out)
    r = _run(nc, [arrays], core_ids=[0])
    return r.results[0]["out"]
```
